# Optimizing a Trainium2 kernel written in Bass

```python
import numpy as np
import jax
import jax.numpy as jnp

def _softmax(x, axis=-1):
    return jax.nn.softmax(x, axis=axis)

def _gelu(x):
    return jax.nn.gelu(x, approximate=True)

def _silu(x):
    return jax.nn.silu(x)

def _sigmoid(x):
    return jax.nn.sigmoid(x)

def _layernorm(x, axis=-1, eps=1e-05):
    m = jnp.mean(x, axis=axis, keepdims=True)
    v = jnp.var(x, axis=axis, keepdims=True)
    return (x - m) / jnp.sqrt(v + eps)

def _scatter_add(tgt, idx, src, axis=0):
    return tgt.at[idx].add(src)

def _segment_sum(src, seg, n):
    return jax.ops.segment_sum(src, seg, n)
kernel_name = 'mk_adaln_d1_jaxref_r8_6d157e'

def setup_inputs(seed: int=0):
    np.random.seed(seed)
    _w = jnp.asarray

    def _L0_attn_setup():
        import jax, jax.numpy as jnp
        import numpy as np
        import math
        HEADS = 16
        LN_EPS = 1e-05

        def _layernorm(x, w, b):
            mu = jnp.mean(x, axis=-1, keepdims=True)
            var = jnp.mean((x - mu) ** 2, axis=-1, keepdims=True)
            return (x - mu) * jax.lax.rsqrt(var + LN_EPS) * w + b
        key = jax.random.key(seed)
        ks = jax.random.split(key, 8)
        b, t, e = (2, 256, 128)
        s = e // HEADS
        sc = 1.0 / math.sqrt(e)
        inp = {'x': jax.random.normal(ks[0], (b, t, e), dtype=jnp.float32), 'Wk': jax.random.normal(ks[1], (e, e), dtype=jnp.float32) * sc, 'Wq': jax.random.normal(ks[2], (e, e), dtype=jnp.float32) * sc, 'Wv': jax.random.normal(ks[3], (e, e), dtype=jnp.float32) * sc, 'Wo': jax.random.normal(ks[4], (e, e), dtype=jnp.float32) * sc, 'bo': jnp.zeros((e,), dtype=jnp.float32), 'kln_w': jnp.ones((s,), dtype=jnp.float32), 'kln_b': jnp.zeros((s,), dtype=jnp.float32), 'qln_w': jnp.ones((s,), dtype=jnp.float32), 'qln_b': jnp.zeros((s,), dtype=jnp.float32)}
        return inp
    _L0_attn_in = _L0_attn_setup()

    def _L0_ffn_setup():
        import jax, jax.numpy as jnp
        import numpy as np
        MIN_EXPERT_CAPACITY = 4
        CAPACITY_FACTOR = 1.0

        def _moe_forward(x, router_w, w1, b1, w2, b2):
            B, S, D = x.shape
            E = router_w.shape[1]
            G = 1
            T = B * S
            C = max(int(round(CAPACITY_FACTOR * T / E)), MIN_EXPERT_CAPACITY)
            xt = x.reshape(G, T, D)
            logits = jnp.einsum('gtd,de->gte', xt, router_w)
            probs = jax.nn.softmax(logits, axis=-1)
            gate = jnp.max(probs, axis=-1)
            idx = jnp.argmax(probs, axis=-1)
            emask = jax.nn.one_hot(idx, E, dtype=x.dtype)
            pos = jnp.cumsum(emask, axis=1) * emask - 1.0
            pos = pos.astype(jnp.int32)
            slot = jax.nn.one_hot(pos, C, dtype=x.dtype)
            dispatch = emask[..., None] * slot
            combine = dispatch * gate[..., None, None]
            expert_inputs = jnp.einsum('gtd,gtec->gecd', xt, dispatch)
            h = jax.nn.relu(jnp.einsum('gecd,edf->gecf', expert_inputs, w1) + b1[None, :, None, :])
            expert_outputs = jnp.einsum('gecf,efd->gecd', h, w2) + b2[None, :, None, :]
            out = jnp.einsum('gecd,gtec->gtd', expert_outputs, combine)
            return out.reshape(B, S, D)
        key = jax.random.key(seed)
        k0, k1, k2, k3 = jax.random.split(key, 4)
        B, S, D, E, F = (4, 256, 128, 8, 512)
        x = jax.random.normal(k0, (B, S, D), dtype=jnp.float32)
        router_w = jax.random.normal(k1, (D, E), dtype=jnp.float32) * D ** (-0.5)
        w1 = jax.random.normal(k2, (E, D, F), dtype=jnp.float32) * D ** (-0.5)
        b1 = jnp.zeros((E, F), dtype=jnp.float32)
        w2 = jax.random.normal(k3, (E, F, D), dtype=jnp.float32) * F ** (-0.5)
        b2 = jnp.zeros((E, D), dtype=jnp.float32)
        return {'x': x, 'router_w': router_w, 'w1': w1, 'b1': b1, 'w2': w2, 'b2': b2}
    _L0_ffn_in = _L0_ffn_setup()
    _L0_c = _w((lambda *s: np.random.randn(*s).astype(np.float32) * 0.05)(2, 128))
    _L0_wmod = _w((lambda *s: np.random.randn(*s).astype(np.float32) * 0.05)(128, 6 * 128) * 128 ** (-0.5))
    _d = {'L0_attn_x': _L0_attn_in['x'], 'L0_attn_Wk': _L0_attn_in['Wk'], 'L0_attn_Wq': _L0_attn_in['Wq'], 'L0_attn_Wv': _L0_attn_in['Wv'], 'L0_attn_Wo': _L0_attn_in['Wo'], 'L0_attn_bo': _L0_attn_in['bo'], 'L0_attn_kln_w': _L0_attn_in['kln_w'], 'L0_attn_kln_b': _L0_attn_in['kln_b'], 'L0_attn_qln_w': _L0_attn_in['qln_w'], 'L0_attn_qln_b': _L0_attn_in['qln_b'], 'L0_ffn_router_w': _L0_ffn_in['router_w'], 'L0_ffn_w1': _L0_ffn_in['w1'], 'L0_ffn_b1': _L0_ffn_in['b1'], 'L0_ffn_w2': _L0_ffn_in['w2'], 'L0_ffn_b2': _L0_ffn_in['b2'], 'L0_c': _L0_c, 'L0_wmod': _L0_wmod}
    _x0 = _d['L0_attn_x']
    _d['L0_attn_x'] = jax.random.normal(jax.random.fold_in(jax.random.key(seed), 1), (2, 1024, 128), dtype=_x0.dtype)
    del _x0
    return _d

def reference(L0_attn_x, L0_attn_Wk, L0_attn_Wq, L0_attn_Wv, L0_attn_Wo, L0_attn_bo, L0_attn_kln_w, L0_attn_kln_b, L0_attn_qln_w, L0_attn_qln_b, L0_ffn_router_w, L0_ffn_w1, L0_ffn_b1, L0_ffn_w2, L0_ffn_b2, L0_c, L0_wmod):

    def _L0_attn_ref(x, Wk, Wq, Wv, Wo, bo, kln_w, kln_b, qln_w, qln_b):
        import jax, jax.numpy as jnp
        import numpy as np
        import math
        HEADS = 16
        LN_EPS = 1e-05

        def _layernorm(x, w, b):
            mu = jnp.mean(x, axis=-1, keepdims=True)
            var = jnp.mean((x - mu) ** 2, axis=-1, keepdims=True)
            return (x - mu) * jax.lax.rsqrt(var + LN_EPS) * w + b
        b, t, e = x.shape
        h = HEADS
        s = e // h
        scale = 1.0 / math.sqrt(s)
        k = (x @ Wk).reshape(b, t, h, s)
        q = (x @ Wq).reshape(b, t, h, s)
        v = (x @ Wv).reshape(b, t, h, s)
        k = _layernorm(k, kln_w, kln_b)
        q = _layernorm(q, qln_w, qln_b)
        dot = jnp.einsum('bqhs,bkhs->bhqk', q, k) * scale
        causal = jnp.tril(jnp.ones((t, t), dtype=bool))
        dot = jnp.where(causal, dot, -jnp.inf)
        attn = jax.nn.softmax(dot, axis=-1)
        out = jnp.einsum('bhqk,bkhs->bqhs', attn, v).reshape(b, t, e)
        return out @ Wo + bo

    def _L0_ffn_ref(x, router_w, w1, b1, w2, b2):
        import jax, jax.numpy as jnp
        import numpy as np
        MIN_EXPERT_CAPACITY = 4
        CAPACITY_FACTOR = 1.0

        def _moe_forward(x, router_w, w1, b1, w2, b2):
            B, S, D = x.shape
            E = router_w.shape[1]
            G = 1
            T = B * S
            C = max(int(round(CAPACITY_FACTOR * T / E)), MIN_EXPERT_CAPACITY)
            xt = x.reshape(G, T, D)
            logits = jnp.einsum('gtd,de->gte', xt, router_w)
            probs = jax.nn.softmax(logits, axis=-1)
            gate = jnp.max(probs, axis=-1)
            idx = jnp.argmax(probs, axis=-1)
            emask = jax.nn.one_hot(idx, E, dtype=x.dtype)
            pos = jnp.cumsum(emask, axis=1) * emask - 1.0
            pos = pos.astype(jnp.int32)
            slot = jax.nn.one_hot(pos, C, dtype=x.dtype)
            dispatch = emask[..., None] * slot
            combine = dispatch * gate[..., None, None]
            expert_inputs = jnp.einsum('gtd,gtec->gecd', xt, dispatch)
            h = jax.nn.relu(jnp.einsum('gecd,edf->gecf', expert_inputs, w1) + b1[None, :, None, :])
            expert_outputs = jnp.einsum('gecf,efd->gecd', h, w2) + b2[None, :, None, :]
            out = jnp.einsum('gecd,gtec->gtd', expert_outputs, combine)
            return out.reshape(B, S, D)
        return _moe_forward(x, router_w, w1, b1, w2, b2)
    x = L0_attn_x
    mod = (_silu(L0_c) @ L0_wmod).reshape(L0_c.shape[0], 6, 1, -1)
    sa, ca, ga, sb, cb, gb = (mod[:, 0], mod[:, 1], mod[:, 2], mod[:, 3], mod[:, 4], mod[:, 5])
    ga = (2 * (ga >= 0) - 1) * jnp.maximum(jnp.abs(ga), 0.25)
    gb = (2 * (gb >= 0) - 1) * jnp.maximum(jnp.abs(gb), 0.25)
    h = _layernorm(x, axis=-1) * (1 + ca) + sa
    x = x + ga * _L0_attn_ref(h, L0_attn_Wk, L0_attn_Wq, L0_attn_Wv, L0_attn_Wo, L0_attn_bo, L0_attn_kln_w, L0_attn_kln_b, L0_attn_qln_w, L0_attn_qln_b)
    h = _layernorm(x, axis=-1) * (1 + cb) + sb
    x = x + gb * _L0_ffn_ref(h, L0_ffn_router_w, L0_ffn_w1, L0_ffn_b1, L0_ffn_w2, L0_ffn_b2)
    return x

_drawn_inputs = setup_inputs


def setup_inputs(seed=0):
    import zlib

    import numpy as np

    out = dict(_drawn_inputs(seed))
    spreads = {'L0_attn_bo': (0.0, 0.294),
     'L0_attn_kln_w': (1.0, 0.6),
     'L0_attn_kln_b': (0.0, 2.0),
     'L0_attn_qln_w': (1.0, 0.6),
     'L0_attn_qln_b': (0.0, 2.0),
     'L0_ffn_b1': (0.0, 0.8),
     'L0_ffn_b2': (0.0, 0.8)}
    factors = {}
    for name, (base, spread) in spreads.items():
        noise = np.random.default_rng([zlib.crc32(name.encode()), seed]).standard_normal(out[name].shape)
        drawn = base * np.exp(spread * noise) if base else spread * noise
        out[name] = jnp.asarray(drawn.astype(out[name].dtype))
    for name, factor in factors.items():
        out[name] = (out[name] * factor).astype(out[name].dtype)
    return out
```

```python
from contextlib import ExitStack

import concourse.bass as bass
from concourse import mybir

F32 = mybir.dt.float32
BF16 = mybir.dt.bfloat16
I32 = mybir.dt.int32
U32 = mybir.dt.uint32
ALU = mybir.AluOpType
ACT = mybir.ActivationFunctionType
AX = mybir.AxisListType

P = 128
EPS = 1e-5
NEG = -1e30
FAR = 1e6
Q_PART = [0, 0, 1, 0, 2, 1]
K_PART = [0, 1, 0, 2, 0, 1]
TERMS = len(Q_PART)


def adaln_block(nc, x, Wk, Wq, Wv, Wo, bo, kln_w, kln_b, qln_w, qln_b,
                router_w, w1, b1, w2, b2, c, wmod, out):
    B, T, D = x.shape
    HD = kln_w.shape[0]
    H = D // HD
    E = router_w.shape[1]
    F = w1.shape[2]
    FC = F // P
    NT = T // P
    TT = B * NT
    CAP = B * T // E
    NS = E * CAP
    SPE = CAP // P
    NP = H // 2
    SCALE = 1.0 / float(HD) ** 0.5
    XW = D + 4
    assert D == P and HD == 8 and E == 8 and NT == 8 and T * 4 == 8 * 512
    KM = TERMS * HD
    KS = KM + 3

    UNITS = [[(0, 0, 4)], [(0, 4, 4)], [(1, 1, 3), (3, 3, 1)], [(1, 4, 4)],
             [(2, 2, 2), (6, 6, 2)], [(2, 4, 4)], [(3, 4, 4)], [(4, 4, 4)], [(5, 5, 3), (7, 7, 1)]]
    NU = len(UNITS)
    DIAG = [[u for u in UNITS if u[0][0] == u[0][1]].index(u) if u[0][0] == u[0][1] else None for u in UNITS]
    ND = sum(d is not None for d in DIAG)

    def diag_columns(unit):
        at, cols = 0, []
        for j, i0, n in unit:
            if j == i0:
                cols.append(at)
            at += n * P
        return cols

    def unit_of(n):
        pair, u = divmod(n, NU)
        return pair // NP, pair % NP, u

    def masked_before(n):
        return (n // NU) * ND + sum(DIAG[u] is not None for u in range(n % NU))

    xs_dram = nc.dram_tensor("dispatched", [NS, XW], F32, kind="Internal").ap()
    yt_dram = nc.dram_tensor("expert_out", [B * T, D], F32, kind="Internal").ap()

    with ExitStack() as ctx:
        def sb(name, shape, dt=F32):
            return ctx.enter_context(nc.sbuf_tensor(name, shape, dt))

        def ps(name, shape):
            return ctx.enter_context(nc.psum_tensor(name, shape, F32))

        def sem(name):
            return ctx.enter_context(nc.semaphore(name))

        psS = [ps("psS0", [P, 2, 512]), ps("psS1", [P, 2, 512])]
        psO = [ps("psO0", [P, 512]), ps("psO1", [P, 512])]
        psN = ps("psN", [P, 512])
        psM = ps("psM", [P, 512])

        ident = sb("ident", [P, P])
        onesb = sb("onesb", [P, 1024], BF16)
        ones1 = sb("ones1", [1, P])
        upper = sb("upper", [P, P], BF16)
        sel = sb("sel", [P, 2, 32])
        e8 = sb("e8", [HD, P])
        mask = sb("mask", [P, T])
        desc8 = sb("desc8", [P, NT, E])
        tokid = sb("tokid", [P, TT])
        zeros = sb("zeros", [P, XW * SPE])
        epsc = sb("epsc", [P, 1])
        xt = sb("xt", [P, TT, D])
        wst = sb("wst", [P, 2, D])
        wmean = sb("wmean", [P, 2 * H])
        wcen = sb("wcen", [P, 2, D])
        wqk = sb("wqk", [P, 2, D])
        wv = sb("wv", [P, D])
        wo = sb("wo", [P, D])
        bor = sb("bor", [1, D])
        lnr = sb("lnr", [4, HD])
        crow = sb("crow", [B, D])
        wm = sb("wm", [P, 6 * D])
        rw = sb("rw", [P, E])
        b1r = sb("b1r", [E, F])
        b2r = sb("b2r", [1, E * D])
        cT = sb("cT", [P, B])
        silu = sb("silu", [P, 3, B])
        silub = sb("silub", [P, B, P])
        sT = sb("sT", [P, B])
        lnT = sb("lnT", [HD, 4])
        lncol = sb("lncol", [P, 4])
        b1c = sb("b1c", [P, FC, E])
        modc = sb("modc", [P, 2, B])
        modr = sb("modr", [P, B, 4, D])
        gsign = sb("gsign", [P, B, 2, D])
        wog = sb("wog", [P, B, D])
        bog = sb("bog", [1, B, D])
        bst = sb("bst", [P, NT, 6])
        mv = sb("mv", [P, NT, 2])
        nw = sb("nw", [P, 4, NT])
        xn = sb("xn", [P, NT, D])
        hT = sb("hT", [P, T])
        sq = sb("sq", [P, 2, 512])
        var = sb("var", [P, 4, 64])
        std = sb("std", [P, 256])
        rstd = sb("rstd", [P, 256])
        qkn = sb("qkn", [P, NT, 2, D])
        qkf = sb("qkf", [P, 2, 512])
        res = sb("res", [P, 2, 512])
        parts = sb("parts", [P, 2, 3, T], BF16)
        stack = [sb(f"stack{b}", [P, 2, NP, T], BF16) for b in range(B)]
        v9 = sb("v9", [P, TT, H, HD + 1])
        mx = sb("mx", [P, NT, H])
        NPB = 3
        pbuf = [sb(f"pbuf{i}", [P, 2, 512]) for i in range(NPB)]
        ots = sb("ots", [P, 2, 512])
        rl = sb("rl", [P, 2, NT, 2])
        attn = sb("attn", [P, NT, D])
        attnT = sb("attnT", [P, T])
        h2 = sb("h2", [P, NT, XW])
        mtmp = h2[:, :, :].rearrange("p t w -> p (t w)")[:, 0:T]
        negm = attn[:, :, :].rearrange("p t d -> p (t d)")[0:H, :]
        mres = attnT[0:H, :]
        mparts = qkn[:, :, :, :].rearrange("p t a d -> p (t a d)").bitcast(BF16)[0:H, 0:3 * T].rearrange(
            "p (n t) -> p n t", n=3)
        h2T = attnT
        rt = sb("rt", [P, 4, NT, E])
        ro = sb("ro", [P, 8, NT])
        oh = sb("oh", [P, B, NT, E], BF16)
        gate = sb("gate", [P, TT])
        slot = sb("slot", [P, TT], U32)
        w12 = stack[0][:, :, :, :].rearrange("p a h t -> p (a h t)").bitcast(F32)
        w1s = w12[:, 0:E * F].rearrange("p (e f) -> p e f", e=E)
        w2s = w12[:, E * F:2 * E * F].rearrange("p (e f) -> p e f", e=E)
        xe = sb("xe", [P, E, SPE, XW])
        back = sb("back", [P, E, SPE], U32)
        none = sb("none", [P, E, SPE])
        xeT = sb("xeT", [P, 2, CAP])
        hid = qkn[:, :, :, :].rearrange("p t a d -> p (t a d)").rearrange("p (b f c) -> p b f c", b=2, f=FC)
        ye = sb("ye", [P, 2, SPE, D])
        yall = stack[1][:, :, :, :].rearrange("p a h t -> p (a h t)").bitcast(F32)
        yt = yall[:, 0:TT * D].rearrange(
            "p (t d) -> p t d", t=TT)
        yo = yall[:, TT * D:2 * TT * D].rearrange(
            "p (t d) -> p t d", t=TT)

        l_small = sem("l_small")
        l_wm = sem("l_wm")
        l_x = [sem(f"l_x{b}") for b in range(B)]
        l_qkv = sem("l_qkv")
        l_late = sem("l_late")
        l_ffn = sem("l_ffn")
        k_pool = sem("k_pool")
        c_T = sem("c_T")
        c_cp = sem("c_cp")
        c_exp = sem("c_exp")
        c_silu = sem("c_silu")
        c_mod = sem("c_mod")
        c_modc = sem("c_modc")
        w_qk = sem("w_qk")
        v_ch = sem("v_ch")
        a_ch = sem("a_ch")
        g_ch = sem("g_ch")
        n_xn = sem("n_xn")
        n_T = sem("n_T")
        n_h = sem("n_h")
        q_mm = sem("q_mm")
        v_mm = sem("v_mm")
        v_cp = sem("v_cp")
        q_sq = sem("q_sq")
        q_var = sem("q_var")
        q_std = sem("q_std")
        q_n = sem("q_n")
        q_T = sem("q_T")
        q_f = sem("q_f")
        q_r = sem("q_r")
        q_2 = sem("q_2")
        q_3 = sem("q_3")
        st_d = [sem(f"st_d{b}") for b in range(B)]
        v_set = sem("v_set")
        m_mm = sem("m_mm")
        m_rd = sem("m_rd")
        m_T = sem("m_T")
        m_cp = sem("m_cp")
        m_p = sem("m_p")
        m_d = [sem(f"m_d{b}") for b in range(B)]
        s_mm = sem("s_mm")
        s_exp = sem("s_exp")
        s_mask = sem("s_mask")
        s_pv = sem("s_pv")
        o_cp = sem("o_cp")
        o_mm = sem("o_mm")
        o_n = sem("o_n")
        t_pe = [sem(f"t_pe{b}") for b in range(B)]
        t_v = [sem(f"t_v{b}") for b in range(B)]
        t_e = sem("t_e")
        z_d = sem("z_d")
        d_d = [sem(f"d_d{b}") for b in range(B)]
        x_d = [sem(f"x_d{i}") for i in range(E)]
        x_i = sem("x_i")
        x_T = sem("x_T")
        x_cp = sem("x_cp")
        h_mm = sem("h_mm")
        h_a = sem("h_a")
        h_v = sem("h_v")
        y_mm = sem("y_mm")
        y_cp = sem("y_cp")
        y_d = [sem(f"y_d{i}") for i in range(2)]
        f_l = [sem(f"f_l{b}") for b in range(B)]
        f_v = sem("f_v")
        f_o = sem("f_o")

        K_POOL = 5
        block = ctx.enter_context(nc.Block())

        @block.sync
        def _(sp):
            sp.dma_start(crow[:, :], c).then_inc(l_small, 16)
            for n, v in enumerate((qln_w, qln_b, kln_w, kln_b)):
                sp.dma_start(lnr[n:n + 1, :], v.rearrange("(a s) -> a s", a=1)).then_inc(l_small, 16)
            sp.dma_start(b1r[:, :], b1).then_inc(l_small, 16)
            sp.dma_start(xt[:, 0:NT, :], x[0].rearrange("(t p) d -> p t d", p=P)).then_inc(l_x[0], 16)
            sp.dma_start(wm[:, :], wmod).then_inc(l_wm, 16)
            for n, w in enumerate((Wq, Wk)):
                sp.dma_start(wst[:, n, :], w).then_inc(l_qkv, 16)
            sp.dma_start(wv[:, :], Wv).then_inc(l_qkv, 16)
            for b in range(1, B):
                sp.dma_start(xt[:, b * NT:(b + 1) * NT, :],
                             x[b].rearrange("(t p) d -> p t d", p=P)).then_inc(l_x[b], 16)
            sp.dma_start(wo[:, :], Wo).then_inc(l_late, 16)
            sp.dma_start(bor[:, :], bo.rearrange("(a d) -> a d", a=1)).then_inc(l_late, 16)
            sp.dma_start(rw[:, :], router_w).then_inc(l_late, 16)

            def stack_parts(b):
                sp.wait_ge(q_r, 4 * (b + 1))
                sp.wait_ge(q_2, 4 * (b + 1))
                sp.wait_ge(q_3, 4 * (b + 1))
                for a, order in enumerate((Q_PART, K_PART)):
                    for g in range(2):
                        for n, part in enumerate(order):
                            at = 64 * g + HD * n
                            sp.dma_start(stack[b][at:at + HD, a, :, :],
                                         parts[64 * g:64 * g + 64, a, part, :]).then_inc(st_d[b], 16)
                for g in range(2):
                    for n in range(3):
                        at = 64 * g + KM + n
                        sp.dma_start(stack[b][at:at + 1, 1, :, :], onesb[0:NP, :]).then_inc(st_d[b], 16)

            def stack_shift(b):
                sp.wait_ge(m_p, 3 * (b + 1))
                for g in range(2):
                    for n in range(3):
                        at = 64 * g + KM + n
                        sp.dma_start(stack[b][at:at + 1, 0, :, :],
                                     mparts[NP * g:NP * g + NP, n, :]).then_inc(m_d[b], 16)

            sp.wait_ge(k_pool, K_POOL)
            stack_parts(0)
            for e in range(E):
                sp.dma_start(xs_dram[e * CAP:(e + 1) * CAP, :].rearrange("(p t) w -> p (t w)", p=P),
                             zeros[:, :]).then_inc(z_d, 16)
                sp.dma_start(yt_dram[e * CAP:(e + 1) * CAP, :].rearrange("(p t) w -> p (t w)", p=P),
                             zeros[:, 0:SPE * D]).then_inc(z_d, 16)
            stack_shift(0)
            stack_parts(1)
            stack_shift(1)
            sp.wait_ge(s_mm, NP * NU)
            sp.dma_start(b2r[:, :], b2.rearrange("e (a d) -> a (e d)", a=1)).then_inc(l_ffn, 16)
            sp.dma_start(w1s[:, :, :], w1.rearrange("e d f -> d e f")).then_inc(l_ffn, 16)
            sp.dma_start(w2s[:, :, :], w2.rearrange("e (p c) d -> p e (c d)", c=FC)).then_inc(l_ffn, 16)
            for b in range(B):
                sp.wait_ge(d_d[b], 16 * NT)
            for e in range(E):
                sp.dma_start(xe[:, e, :, :], xs_dram[e * CAP:(e + 1) * CAP, :].rearrange(
                    "(t p) w -> p t w", p=P)).then_inc(x_d[e], 16)
            for i in range(2):
                sp.wait_ge(y_d[i], 16 * SPE * E // 2)
            for b in range(B):
                sp.dma_start(yt[:, b * NT:(b + 1) * NT, :], yt_dram[b * T:(b + 1) * T, :].rearrange(
                    "(t p) d -> p t d", p=P)).then_inc(f_l[b], 16)
            for b in range(B):
                sp.wait_ge(f_v, b + 1)
                sp.dma_start(out[b].rearrange("(t p) d -> p t d", p=P),
                             yo[:, b * NT:(b + 1) * NT, :]).then_inc(f_o, 16)
            sp.wait_ge(f_o, 16 * B)

        @block.gpsimd
        def _(pool):
            chain = [0]

            def link(ins):
                chain[0] += 1
                ins.then_inc(g_ch, 1)
                pool.wait_ge(g_ch, chain[0])

            link(nc.gpsimd.memset(ident[:, :], 0.0))
            nc.gpsimd.affine_select(out=ident[:, :], in_=ident[:, :], compare_op=ALU.not_equal, fill=1.0, base=0,
                                    pattern=[[-1, P]], channel_multiplier=1).then_inc(k_pool, 1)
            link(nc.gpsimd.memset(e8[:, :], 0.0))
            nc.gpsimd.affine_select(out=e8[:, :].rearrange("k (g s p) -> k g s p", g=2, s=HD),
                                    in_=e8[:, :].rearrange("k (g s p) -> k g s p", g=2, s=HD),
                                    compare_op=ALU.not_equal, fill=1.0, base=0,
                                    pattern=[[0, 2], [-1, HD], [0, NP]],
                                    channel_multiplier=1).then_inc(k_pool, 1)
            nc.gpsimd.memset(zeros[:, :], 0.0).then_inc(k_pool, 1)
            nc.gpsimd.memset(onesb[:, :], 1.0).then_inc(k_pool, 1)
            nc.gpsimd.memset(v9[:, :, :, HD:HD + 1], 1.0).then_inc(v_set, 1)
            link(nc.gpsimd.memset(sel[:, :, :], 0.0))
            for q in range(2):
                v = sel[:, q, :].rearrange("p (g r) -> p g r", g=2)[:, :, 0:HD + 1]
                link(nc.gpsimd.affine_select(out=v, in_=v, compare_op=ALU.not_equal, fill=1.0, base=-64 * q,
                                             pattern=[[-32, 2], [-1, HD + 1]], channel_multiplier=1))
            nc.gpsimd.affine_select(out=upper[:, :], in_=onesb[:, 0:P], compare_op=ALU.is_ge, fill=0.0, base=0,
                                    pattern=[[1, P]], channel_multiplier=-1).then_inc(v_set, 1)
            link(nc.gpsimd.memset(mask[:, :], 0.0))
            nc.gpsimd.affine_select(out=mask[:, T - P:T], in_=mask[:, T - P:T], compare_op=ALU.is_ge, fill=NEG,
                                    base=0, pattern=[[-1, P]], channel_multiplier=1).then_inc(v_set, 1)
            nc.gpsimd.iota(desc8[:, :, :], pattern=[[0, NT], [-1, E]], base=E, channel_multiplier=0,
                           allow_small_or_imprecise_dtypes=True).then_inc(v_set, 1)
            nc.gpsimd.iota(tokid[:, :], pattern=[[P, TT]], base=0, channel_multiplier=1,
                           allow_small_or_imprecise_dtypes=True).then_inc(v_set, 1)
            nc.gpsimd.memset(ones1[:, :], 1.0).then_inc(k_pool, 1)

            def third_parts(b):
                for n in range(4):
                    half, a = divmod(n, 2)
                    pool.wait_ge(q_2, 4 * b + n + 1)
                    nc.gpsimd.tensor_tensor(parts[:, a, 2, 512 * half:512 * half + 512], res[:, n % 2, :],
                                            parts[:, a, 1, 512 * half:512 * half + 512],
                                            ALU.subtract).then_inc(q_3, 1)

            def mask_units(b):
                for n in range(b * NP * NU, (b + 1) * NP * NU):
                    u = unit_of(n)[2]
                    if DIAG[u] is None:
                        continue
                    pool.wait_ge(s_exp, n + 1)
                    cols = diag_columns(UNITS[u])
                    step = cols[1] - cols[0] if len(cols) > 1 else P
                    for at in cols:
                        v = pbuf[n % NPB][:, :, at:at + P]
                        ins = nc.gpsimd.affine_select(out=v, in_=v, compare_op=ALU.is_ge, fill=0.0, base=0,
                                                      pattern=[[0, 2], [1, P]], channel_multiplier=-1)
                        if at == cols[-1]:
                            ins.then_inc(s_mask, 1)

            def dispatch(b):
                pool.wait_ge(t_v[b], 9)
                pool.wait_ge(z_d, 16 * 2 * E)
                for t in range(NT):
                    nc.gpsimd.indirect_dma_start(
                        out=xs_dram[:, :], out_offset=bass.IndirectOffsetOnAxis(
                            ap=slot[:, b * NT + t:b * NT + t + 1], axis=0),
                        in_=h2[:, t, :], in_offset=None, bounds_check=NS - 1,
                        oob_is_err=False).then_inc(d_d[b], 16)

            third_parts(0)
            third_parts(1)
            mask_units(0)
            dispatch(0)
            mask_units(1)
            dispatch(1)
            for e in range(E):
                pool.wait_ge(x_i, e + 1)
                pool.wait_ge(y_cp, e + 1)
                for t in range(SPE):
                    nc.gpsimd.indirect_dma_start(
                        out=yt_dram[:, :], out_offset=bass.IndirectOffsetOnAxis(
                            ap=back[:, e, t:t + 1], axis=0),
                        in_=ye[:, e % 2, t, :], in_offset=None, bounds_check=B * T - 1,
                        oob_is_err=False).then_inc(y_d[e % 2], 16)

        @block.scalar
        def _(act):
            act.wait_ge(c_cp, 1)
            nc.scalar.activation(silu[:, 0, :], cT[:, :], ACT.Exp, scale=-1.0).then_inc(c_exp, 1)
            act.wait_ge(c_modc, 1)

            def modulate(b):
                for half in range(2):
                    act.wait_ge(n_T, 2 * b + half + 1)
                    if b:
                        act.wait_ge(q_mm, 4 * b)
                        act.wait_ge(v_mm, 2 * b)
                    src = psN if half == 0 else psM
                    nc.scalar.activation(hT[:, 512 * half:512 * half + 512], src[:, :], ACT.Identity,
                                         bias=modc[:, 0, b:b + 1], scale=modc[:, 1, b:b + 1]).then_inc(n_h, 1)

            def squares(b):
                for n in range(4):
                    act.wait_ge(q_mm, 4 * b + n + 1)
                    if 4 * b + n >= 2:
                        act.wait_ge(q_var, 4 * b + n - 1)
                    nc.scalar.activation(sq[:, n % 2, :], psS[n // 2][:, n % 2, :],
                                         ACT.Square).then_inc(q_sq, 1)
                for n in range(2):
                    act.wait_ge(v_mm, 2 * b + n + 1)
                    t0 = b * NT + 4 * n
                    nc.scalar.activation(v9[:, t0:t0 + 4, :, 0:HD],
                                         psO[n][:, :].rearrange("p (t h s) -> p t h s", t=4, h=H),
                                         ACT.Copy).then_inc(v_cp, 1)

            def stds(b):
                act.wait_ge(q_var, 4 * (b + 1))
                if b:
                    act.wait_ge(q_n, 4 * b)
                act.wait_ge(k_pool, K_POOL)
                nc.scalar.activation(std[:, :], var[:, :, :].rearrange("p a c -> p (a c)"), ACT.Sqrt,
                                     bias=epsc[:, :], scale=1.0 / HD).then_inc(q_std, 1)

            def affine(b):
                def second(n):
                    half, a = divmod(n, 2)
                    act.wait_ge(q_r, 4 * b + n + 1)
                    nc.scalar.activation(parts[:, a, 1, 512 * half:512 * half + 512], res[:, n % 2, :],
                                         ACT.Copy).then_inc(q_2, 1)

                for n in range(4):
                    act.wait_ge(q_T, 4 * b + n + 1)
                    if 4 * b + n >= 2:
                        act.wait_ge(q_r, 4 * b + n - 1)
                    a = n % 2
                    nc.scalar.activation(qkf[:, n % 2, :], (psN, psM)[n % 2][:, :], ACT.Identity,
                                         bias=lncol[:, 2 * a + 1:2 * a + 2],
                                         scale=lncol[:, 2 * a:2 * a + 1]).then_inc(q_f, 1)
                    if n >= 1:
                        if b and n == 1:
                            act.wait_ge(st_d[b - 1], 16 * (4 * TERMS + 6))
                        second(n - 1)
                second(3)

            def exps(b):
                for n in range(b * NP * NU, (b + 1) * NP * NU):
                    act.wait_ge(s_mm, n + 1)
                    if n >= NPB:
                        act.wait_ge(s_pv, n - NPB + 1)
                    nc.scalar.activation(pbuf[n % NPB][:, :, :], psS[n % 2][:, :, :], ACT.Exp).then_inc(s_exp, 1)

            for b in range(B):
                modulate(b)
                squares(b)
                stds(b)
                affine(b)
            for b in range(B):
                exps(b)
                act.wait_ge(t_v[b], 7)
                nc.scalar.activation(rt[:, 1, :, :], rt[:, 0, :, :], ACT.Exp).then_inc(t_e, 1)
            for e in range(E + 1):
                if e < E:
                    act.wait_ge(h_mm, 2 * e + 1)
                    if e >= 2:
                        act.wait_ge(y_mm, e - 1)
                    for f in range(2):
                        ins = nc.scalar.activation(hid[:, e % 2, f, :],
                                                   psS[e % 2][:, 0, CAP * f:CAP * f + CAP], ACT.Relu,
                                                   bias=b1c[:, f, e:e + 1])
                    ins.then_inc(h_a, 1)
                if e >= 1:
                    d = e - 1
                    act.wait_ge(y_mm, d + 1)
                    if d >= 2:
                        act.wait_ge(y_d[d % 2], 16 * SPE * (d // 2))
                    nc.scalar.activation(ye[:, d % 2, :, :].rearrange("p t d -> p (t d)"),
                                         (psN, psM)[d % 2][:, 0:SPE * D], ACT.Copy).then_inc(y_cp, 1)

        @block.vector
        def _(dve):
            chain = [0]
            V = nc.vector

            def link(ins):
                chain[0] += 1
                ins.then_inc(v_ch, 1)
                dve.wait_ge(v_ch, chain[0])

            def rsqrt(v, n):
                a, y, t, r = (nw[:, i, 0:n] for i in range(4))
                link(V.tensor_scalar(a, v, EPS, None, ALU.add))
                link(V.tensor_scalar(t.bitcast(I32), a.bitcast(I32), 1, None, ALU.arith_shift_right))
                link(V.tensor_scalar(y.bitcast(I32), t.bitcast(I32), -1.0, float(0x5f3759df), ALU.mult, ALU.add))
                for i in range(4):
                    link(V.tensor_tensor(t, y, y, ALU.mult))
                    link(V.scalar_tensor_tensor(out=t, in0=a, scalar=-0.5, in1=t, op0=ALU.mult, op1=ALU.mult))
                    link(V.scalar_tensor_tensor(out=(r if i == 3 else y), in0=t, scalar=1.5, in1=y,
                                                op0=ALU.add, op1=ALU.mult))

            def tile_norm(src, n):
                for t in range(NT):
                    ins = V.bn_stats(bst[:, t, :], src(t))
                link(ins)
                for t in range(NT):
                    ins = V.bn_aggr(mv[:, t, :], bst[:, t, :])
                link(ins)
                rsqrt(mv[:, :, 1], NT)
                for t in range(NT):
                    ins = V.tensor_scalar(xn[:, t, :], src(t), mv[:, t, 0:1], nw[:, 3, t:t + 1],
                                          ALU.subtract, ALU.mult)
                ins.then_inc(n_xn, 1)

            V.memset(epsc[:, :], EPS)
            for b in range(2):
                V.memset(psO[b][:, :], 0.0)
            dve.wait_ge(c_T, 1)
            V.tensor_copy(cT[:, :], psM[:, 0:B]).then_inc(c_cp, 1)
            V.tensor_copy(lnT[:, :], psM[0:HD, 4:8])
            V.tensor_copy(b1c[:, :, :].rearrange("p c e -> p (c e)"), psM[:, 32:32 + FC * E]).then_inc(c_cp, 1)
            dve.wait_ge(c_exp, 1)
            link(V.tensor_scalar(silu[:, 1, :], silu[:, 0, :], 1.0, None, ALU.add))
            link(V.reciprocal(silu[:, 2, :], silu[:, 1, :]))
            link(V.tensor_tensor(sT[:, :], cT[:, :], silu[:, 2, :], ALU.mult))
            for b in range(B):
                ins = V.tensor_copy(silub[:, b, :], sT[:, b:b + 1].to_broadcast([P, P]))
            ins.then_inc(c_silu, 1)
            dve.wait_ge(l_qkv, 48)
            link(V.tensor_reduce(wmean[:, :], wst[:, :, :].rearrange("p a (h s) -> p (a h) s", s=HD), AX.X, ALU.add))
            link(V.scalar_tensor_tensor(
                out=wcen[:, :, :].rearrange("p a (h s) -> p (a h) s", s=HD),
                in0=wmean[:, :].rearrange("p (h o) -> p h o", o=1).to_broadcast([P, 2 * H, HD]),
                scalar=-1.0 / HD, in1=wst[:, :, :].rearrange("p a (h s) -> p (a h) s", s=HD),
                op0=ALU.mult, op1=ALU.add))
            for a in range(2):
                ins = V.tensor_copy(wqk[:, a, :].rearrange("k (g s p) -> k g s p", g=2, s=HD),
                                    wcen[:, a, :].rearrange("k (p g s) -> k g s p", g=2, s=HD))
            ins.then_inc(w_qk, 1)
            dve.wait_ge(c_mod, 1)
            V.tensor_copy(modc[:, 0, :], psM[:, 64:64 + B])
            V.tensor_scalar(modc[:, 1, :], psM[:, 64 + B:64 + 2 * B], 1.0, None, ALU.add)
            V.tensor_scalar(lncol[:, 0:2], psM[:, 72:74], SCALE, None, ALU.mult)
            V.tensor_copy(lncol[:, 2:4], psM[:, 74:76]).then_inc(c_modc, 1)

            def mod_rows():
                for b in range(B):
                    ins = V.tensor_copy(modr[:, b, :, :].rearrange("p a d -> p (a d)"), psO[b][:, :])
                ins.then_inc(c_modc, 1)
                dve.wait_ge(c_modc, 2)
                for b in range(B):
                    V.tensor_scalar(modr[:, b, 2, :], modr[:, b, 2, :], 1.0, None, ALU.add)
                    for i, a in enumerate((0, 3)):
                        ins = V.tensor_scalar(gsign[:, b, i, :], modr[:, b, a, :], 0.0, 2.0, ALU.is_ge, ALU.mult)
                link(ins)
                for b in range(B):
                    for i, a in enumerate((0, 3)):
                        ins = V.scalar_tensor_tensor(out=modr[:, b, a, :], in0=modr[:, b, a, :], scalar=-1.0,
                                                     in1=modr[:, b, a, :], op0=ALU.mult, op1=ALU.max)
                link(ins)
                for b in range(B):
                    for i, a in enumerate((0, 3)):
                        ins = V.tensor_scalar(modr[:, b, a, :], modr[:, b, a, :], 0.25, None, ALU.max)
                link(ins)
                for b in range(B):
                    for i, a in enumerate((0, 3)):
                        ins = V.scalar_tensor_tensor(out=modr[:, b, a, :], in0=gsign[:, b, i, :], scalar=-1.0,
                                                     in1=modr[:, b, a, :], op0=ALU.add, op1=ALU.mult)
                link(ins)
                dve.wait_ge(l_late, 48)
                for b in range(B):
                    V.tensor_tensor(wog[:, b, :], wo[:, :], modr[:, b, 0, :], ALU.mult)
                    ins = V.tensor_tensor(bog[:, b, :], bor[:, :], modr[0:1, b, 0, :], ALU.mult)
                ins.then_inc(c_modc, 1)

            def sums(b):
                for n in range(4):
                    dve.wait_ge(q_sq, 4 * b + n + 1)
                    V.tensor_reduce(var[:, n, :].rearrange("p (c h) -> p c h", h=NP),
                                    sq[:, n % 2, :].rearrange("p (c s h) -> p c h s", s=HD, h=NP),
                                    AX.X, ALU.add).then_inc(q_var, 1)
                dve.wait_ge(q_std, b + 1)
                link(V.reciprocal(rstd[:, :], std[:, :]))
                if b:
                    dve.wait_ge(q_T, 4 * b)
                for n in range(4):
                    V.tensor_tensor(
                        qkn[:, 2 * n:2 * n + 2, :, :].rearrange("p t a (g s h) -> p (t a g) s h", g=2, s=HD),
                        psS[n // 2][:, n % 2, :].rearrange("p (c s h) -> p c s h", s=HD, h=NP),
                        rstd[:, 64 * n:64 * n + 64].rearrange("p (c o h) -> p c o h", o=1, h=NP).to_broadcast(
                            [P, 8, HD, NP]), ALU.mult).then_inc(q_n, 1)

            def rests(b):
                for n in range(4):
                    half, a = divmod(n, 2)
                    dve.wait_ge(q_f, 4 * b + n + 1)
                    if b and n == 0:
                        dve.wait_ge(st_d[b - 1], 16 * (4 * TERMS + 6))
                    first = parts[:, a, 0, 512 * half:512 * half + 512]
                    link(V.tensor_copy(first, qkf[:, n % 2, :]))
                    if 4 * b + n >= 2:
                        dve.wait_ge(q_3, 4 * b + n - 1)
                    V.tensor_tensor(res[:, n % 2, :], qkf[:, n % 2, :], first, ALU.subtract).then_inc(q_r, 1)

            def maxima(b):
                for i in range(NT):
                    for h in range(H):
                        m = (b * NT + i) * H + h
                        p, g = divmod(h, 2)
                        w = (i + 1) * P
                        dve.wait_ge(m_mm, m + 1)
                        if m >= 1:
                            dve.wait_ge(m_rd, m)
                        V.tensor_tensor_reduce(out=mtmp[:, 0:w],
                                               in0=psS[m % 2][:, :, :].rearrange("p a c -> p (a c)")[:, 0:w],
                                               in1=mask[:, T - w:T], scale=1.0, scalar=-3e38,
                                               op0=ALU.add, op1=ALU.max,
                                               accum_out=mx[:, i, g * NP + p:g * NP + p + 1]).then_inc(m_rd, 1)
                for half in range(2):
                    dve.wait_ge(m_T, 2 * b + half + 1)
                    V.tensor_scalar(negm[:, 512 * half:512 * half + 512],
                                    (psN, psM)[half][0:H, :], -1.0, None, ALU.mult).then_inc(m_cp, 1)
                dve.wait_ge(m_cp, 2 * b + 2)
                if b:
                    dve.wait_ge(m_d[b - 1], 16 * 6)
                V.tensor_copy(mparts[:, 0, :], negm[:, :]).then_inc(m_p, 1)
                dve.wait_ge(m_p, 3 * b + 1)
                link(V.tensor_tensor(mres[:, :], negm[:, :], mparts[:, 0, :], ALU.subtract))
                V.tensor_copy(mparts[:, 1, :], mres[:, :]).then_inc(m_p, 1)
                dve.wait_ge(m_p, 3 * b + 2)
                V.tensor_tensor(mparts[:, 2, :], mres[:, :], mparts[:, 1, :], ALU.subtract).then_inc(m_p, 1)

            def copy_sums(n):
                dve.wait_ge(s_pv, NU * (n + 1))
                if n >= 2:
                    dve.wait_ge(o_mm, n - 1)
                V.tensor_copy(ots[:, n % 2, :], psO[n % 2][:, :]).then_inc(o_cp, 1)

            def divide(n):
                p = n % NP
                dve.wait_ge(o_mm, n + 1)
                if n == NP:
                    dve.wait_ge(t_pe[0], 2)
                v = psN[:, 0:NT * 32].rearrange("p (t g r) -> p t g r", t=NT, g=2)
                link(V.reciprocal(rl[:, n % 2, :, :], v[:, :, :, HD]))
                V.tensor_tensor(attn[:, :, 2 * HD * p:2 * HD * (p + 1)].rearrange("p t (g s) -> p t g s", g=2),
                                v[:, :, :, 0:HD],
                                rl[:, n % 2, :, :].rearrange("p t (g o) -> p t g o", o=1).to_broadcast(
                                    [P, NT, 2, HD]), ALU.mult).then_inc(o_n, 1)

            def router(b, step):
                tv = t_v[b]
                t0 = b * NT
                if step in (0, 1, 4, 5):
                    half = step % 2
                    dve.wait_ge(t_pe[b], step + 1)
                    V.tensor_copy(attnT[:, 512 * half:512 * half + 512], psM[:, :]).then_inc(tv, 1)
                if step in (2, 3):
                    half = step % 2
                    dve.wait_ge(t_pe[b], step + 1)
                    xs = xt[:, t0 + 4 * half:t0 + 4 * half + 4, :].rearrange("p t d -> p (t d)")
                    ins = V.tensor_tensor(xs, xs, psM[:, :], ALU.add)
                    if step == 2:
                        ins.then_inc(tv, 1)
                        return
                    link(ins)
                    tile_norm(lambda t: xt[:, t0 + t, :], n=B + b)
                    dve.wait_ge(n_xn, B + b + 1)
                    if b:
                        dve.wait_ge(d_d[b - 1], 16 * NT)
                    for hf in range(2):
                        ins = V.tensor_tensor(
                            h2[:, 4 * hf:4 * hf + 4, 0:D], xn[:, 4 * hf:4 * hf + 4, :],
                            modr[:, b, 2, :].rearrange("p (o d) -> p o d", o=1).to_broadcast([P, 4, D]), ALU.mult)
                    link(ins)
                    for hf in range(2):
                        V.tensor_tensor(
                            h2[:, 4 * hf:4 * hf + 4, 0:D], h2[:, 4 * hf:4 * hf + 4, 0:D],
                            modr[:, b, 1, :].rearrange("p (o d) -> p o d", o=1).to_broadcast([P, 4, D]), ALU.add)
                    V.memset(h2[:, :, D:XW], FAR)
                    link(V.tensor_copy(ro[:, 7, :], tokid[:, t0:t0 + NT]))
                    V.tensor_scalar(h2[:, :, D], ro[:, 7, :], 1.0, None, ALU.add).then_inc(tv, 1)
                if step == 6:
                    dve.wait_ge(t_pe[b], 7)
                    lg = psM[:, 0:NT * E].rearrange("p (t e) -> p t e", e=E)
                    link(V.tensor_reduce(ro[:, 0, :], lg, AX.X, ALU.max))
                    V.tensor_tensor(rt[:, 0, :, :], lg,
                                    ro[:, 0, :].rearrange("p (t o) -> p t o", o=1).to_broadcast([P, NT, E]),
                                    ALU.subtract).then_inc(tv, 1)
                    dve.wait_ge(tv, 7)
                    link(V.scalar_tensor_tensor(out=rt[:, 2, :, :], in0=rt[:, 0, :, :], scalar=0.0,
                                                in1=desc8[:, :, :], op0=ALU.is_ge, op1=ALU.mult))
                    link(V.tensor_reduce(ro[:, 1, :], rt[:, 2, :, :], AX.X, ALU.max))
                    V.tensor_tensor(oh[:, b, :, :], desc8[:, :, :],
                                    ro[:, 1, :].rearrange("p (t o) -> p t o", o=1).to_broadcast([P, NT, E]),
                                    ALU.is_equal).then_inc(tv, 1)
                if step == 7:
                    dve.wait_ge(t_pe[b], 8)
                    dve.wait_ge(t_e, b + 1)
                    cnt = psM[:, 64:64 + NT * E].rearrange("p (t e) -> p t e", e=E)
                    link(V.tensor_reduce(ro[:, 2, :], rt[:, 1, :, :], AX.X, ALU.add))
                    V.reciprocal(ro[:, 3, :], ro[:, 2, :])
                    link(V.tensor_tensor(rt[:, 3, :, :], cnt, oh[:, b, :, :], ALU.mult))
                    link(V.tensor_reduce(ro[:, 4, :], rt[:, 3, :, :], AX.X, ALU.add))
                    link(V.tensor_scalar(ro[:, 5, :], ro[:, 4, :], float(CAP), None, ALU.is_le))
                    V.tensor_tensor(gate[:, t0:t0 + NT], ro[:, 3, :], ro[:, 5, :], ALU.mult)
                    link(V.scalar_tensor_tensor(out=ro[:, 6, :], in0=ro[:, 1, :], scalar=-float(CAP),
                                                in1=ro[:, 4, :], op0=ALU.mult, op1=ALU.add))
                    link(V.scalar_tensor_tensor(out=ro[:, 4, :], in0=ro[:, 5, :], scalar=-FAR, in1=ro[:, 6, :],
                                                op0=ALU.mult, op1=ALU.add))
                    V.tensor_scalar(slot[:, t0:t0 + NT], ro[:, 4, :], FAR + E * CAP - 1, None,
                                    ALU.add).then_inc(tv, 1)

            dve.wait_ge(l_x[0], 16)
            for b in range(B):
                if b:
                    dve.wait_ge(l_x[b], 16)
                    dve.wait_ge(n_T, 2 * b)
                tile_norm(lambda t: xt[:, b * NT + t, :], b)
                if b == 0:
                    mod_rows()
                sums(b)
                rests(b)
            dve.wait_ge(v_set, 5)
            for b in range(B):
                maxima(b)
            for b in range(B):
                for p in range(NP):
                    copy_sums(b * NP + p)
                    divide(b * NP + p)
                for step in range(8):
                    router(b, step)

            def take(e):
                dve.wait_ge(x_d[e], 16)
                link(V.tensor_scalar(none[:, e, :], xe[:, e, :, D], 0.0, FAR, ALU.is_le, ALU.mult))
                V.scalar_tensor_tensor(out=back[:, e, :], in0=xe[:, e, :, D], scalar=-1.0, in1=none[:, e, :],
                                       op0=ALU.add, op1=ALU.max).then_inc(x_i, 1)
                dve.wait_ge(x_T, e + 1)
                if e >= 2:
                    dve.wait_ge(h_mm, 2 * (e - 1))
                V.tensor_copy(xeT[:, e % 2, :], psO[e % 2][:, 0:CAP]).then_inc(x_cp, 1)

            take(0)
            for e in range(E):
                if e + 1 < E:
                    take(e + 1)
                dve.wait_ge(h_mm, 2 * e + 2)
                if e >= 2:
                    dve.wait_ge(y_mm, e - 1)
                for f in range(2, 4):
                    ins = V.tensor_scalar(hid[:, e % 2, f, :], psS[e % 2][:, 1, CAP * (f - 2):CAP * (f - 1)],
                                          b1c[:, f, e:e + 1], 0.0, ALU.add, ALU.max)
                ins.then_inc(h_v, 1)
            for b in range(B):
                dve.wait_ge(f_l[b], 16)
                for t in range(b * NT, (b + 1) * NT):
                    ins = V.scalar_tensor_tensor(out=yt[:, t, :], in0=yt[:, t, :], scalar=gate[:, t:t + 1],
                                                 in1=modr[:, b, 3, :], op0=ALU.mult, op1=ALU.mult)
                link(ins)
                V.tensor_tensor(yo[:, b * NT:(b + 1) * NT, :], xt[:, b * NT:(b + 1) * NT, :],
                                yt[:, b * NT:(b + 1) * NT, :], ALU.add).then_inc(f_v, 1)

        @block.tensor
        def _(pe):
            T_ = nc.tensor
            pe.wait_ge(k_pool, K_POOL)
            pe.wait_ge(l_small, 96)
            T_.transpose(psM[:, 0:B], crow[:, :], ident[0:B, 0:B])
            T_.transpose(psM[0:HD, 4:8], lnr[:, :], ident[0:4, 0:4])
            for f in range(FC):
                ins = T_.transpose(psM[:, 32 + E * f:32 + E * f + E],
                                   b1r[:, :].rearrange("e (p c) -> e c p", c=FC)[:, f, :], ident[0:E, 0:E])
            ins.then_inc(c_T, 1)
            pe.wait_ge(c_silu, 1)
            pe.wait_ge(c_cp, 2)
            pe.wait_ge(l_wm, 16)
            for b in range(B):
                T_.matmul(psO[b][:, :], silub[:, b, :], wm[:, 2 * D:6 * D], start=True, stop=True)
            for a in range(2):
                T_.matmul(psM[:, 64 + B * a:64 + B * a + B], wm[:, D * a:D * a + D], sT[:, :], start=True, stop=True)
            T_.matmul(psM[:, 72:76], e8[:, :], lnT[:, :], start=True, stop=True).then_inc(c_mod, 1)

            def project(b):
                for half in range(2):
                    dst = (psN, psM)[half]
                    if half == 0:
                        pe.wait_ge(n_xn, b + 1)
                        if b:
                            pe.wait_ge(q_f, 4 * b)
                    if b == 0 and half == 1:
                        pe.wait_ge(c_modc, 1)
                    for t in range(4):
                        ins = T_.transpose(dst[:, P * t:P * t + P], xn[:, 4 * half + t, :], ident[:, :])
                    ins.then_inc(n_T, 1)
                pe.wait_ge(w_qk, 1)
                if b == 0:
                    pe.wait_ge(c_modc, 2)
                else:
                    pe.wait_ge(q_n, 4 * b)
                    pe.wait_ge(v_cp, 2 * b)
                for half in range(2):
                    pe.wait_ge(n_h, 2 * b + half + 1)
                    for n in range(2 * half, 2 * half + 2):
                        for t in range(2):
                            at = (2 * n + t) * P
                            ins = T_.matmul(psS[n // 2][:, n % 2, 256 * t:256 * t + 256], hT[:, at:at + P],
                                            wqk[:, :, :].rearrange("p a d -> p (a d)"), start=True, stop=True)
                        ins.then_inc(q_mm, 1)
                    for t in range(4):
                        at = (4 * half + t) * P
                        ins = T_.matmul(psO[half][:, P * t:P * t + P], hT[:, at:at + P], wv[:, :],
                                        start=True, stop=True)
                    ins.then_inc(v_mm, 1)

            def transpose_qk(b):
                for n in range(4):
                    half, a = divmod(n, 2)
                    pe.wait_ge(q_n, 4 * b + 2 * half + 2)
                    if n < 2:
                        pe.wait_ge(n_h, 2 * b + n + 1)
                    else:
                        pe.wait_ge(q_f, 4 * b + n - 1)
                    for t in range(4):
                        ins = T_.transpose((psN, psM)[n % 2][:, P * t:P * t + P], qkn[:, 4 * half + t, a, :],
                                           ident[:, :])
                    ins.then_inc(q_T, 1)

            def maxima(b):
                pe.wait_ge(st_d[b], 16 * (4 * TERMS + 6))
                if b == 0:
                    pe.wait_ge(q_n, 4 * B)
                for i in range(NT):
                    for h in range(H):
                        m = (b * NT + i) * H + h
                        p, g = divmod(h, 2)
                        if m >= 2:
                            pe.wait_ge(m_rd, m - 1)
                        w = (i + 1) * P
                        for hf in range((w + 511) // 512):
                            n = min(512, w - 512 * hf)
                            ins = T_.matmul(psS[m % 2][:, hf, 0:n],
                                            stack[b][64 * g:64 * g + KM, 0, p, i * P:i * P + P],
                                            stack[b][64 * g:64 * g + KM, 1, p, 512 * hf:512 * hf + n],
                                            start=True, stop=True)
                        ins.then_inc(m_mm, 1)
                for half in range(2):
                    pe.wait_ge(m_rd, (b * NT + 4 * half + 4) * H)
                    if b == 0:
                        pe.wait_ge(q_f, 4 * B)
                    else:
                        pe.wait_ge(m_cp, 2 * b)
                    for t in range(4):
                        ins = T_.transpose((psN, psM)[half][0:H, P * t:P * t + P], mx[:, 4 * half + t, :],
                                           ident[:, :])
                    ins.then_inc(m_T, 1)

            def scores(n):
                b, p, u = unit_of(n)
                if n < 2:
                    pe.wait_ge(m_rd, 2 * (B * NT * H // 2))
                else:
                    pe.wait_ge(s_exp, n - 1)
                if p == 0 and u == 0:
                    pe.wait_ge(st_d[b], 16 * (4 * TERMS + 6))
                    pe.wait_ge(m_d[b], 16 * 6)
                at = 0
                for j, i0, cnt in UNITS[u]:
                    w = cnt * P
                    for g in range(2):
                        ins = T_.matmul(psS[n % 2][:, g, at:at + w],
                                        stack[b][64 * g:64 * g + KS, 1, p, j * P:j * P + P],
                                        stack[b][64 * g:64 * g + KS, 0, p, i0 * P:i0 * P + w],
                                        start=True, stop=True)
                    at += w
                ins.then_inc(s_mm, 1)

            def values(n):
                b, p, u = unit_of(n)
                pair = n // NU
                pe.wait_ge(s_exp, n + 1)
                if DIAG[u] is not None:
                    pe.wait_ge(s_mask, masked_before(n) + 1)
                if u == 0:
                    pe.wait_ge(v_cp, 2 * B)
                    if pair >= 2:
                        pe.wait_ge(o_cp, pair - 1)
                at = 0
                for j, i0, cnt in UNITS[u]:
                    for par in range(2):
                        tiles = [i for i in range(i0, i0 + cnt) if i % 2 == par]
                        if not tiles:
                            continue
                        k = len(tiles)
                        for g in range(2):
                            r0 = 64 * par + 32 * g
                            src = pbuf[n % NPB][:, g, :].rearrange("p (t c) -> p t c", c=P)
                            a0 = at // P + tiles[0] - i0
                            dst = psO[pair % 2][r0:r0 + HD + 1, tiles[0] // 2 * P:(tiles[0] // 2 + k) * P]
                            ins = T_.matmul(dst, v9[:, b * NT + j, 2 * p + g, :],
                                            src[:, a0:a0 + 2 * k - 1:2, :],
                                            start=(u == 0), stop=(u == NU - 1), skip_group_check=True,
                                            tile_position=(0, r0))
                    at += cnt * P
                ins.then_inc(s_pv, 1)

            def to_tokens(n):
                pe.wait_ge(o_cp, n + 1)
                pe.wait_ge(v_set, 5)
                if n >= 1:
                    pe.wait_ge(o_n, n)
                for i in range(NT):
                    ins = T_.matmul(psN[:, 32 * i:32 * i + 32], ots[:, n % 2, P * (i // 2):P * (i // 2) + P],
                                    sel[:, i % 2, :], start=True, stop=True)
                ins.then_inc(o_mm, 1)

            def router(b, step):
                tv, tp = t_v[b], t_pe[b]
                half = step % 2
                if step == 0:
                    pe.wait_ge(o_n, NP * (b + 1))
                    if b:
                        pe.wait_ge(t_v[b - 1], 9)
                    else:
                        pe.wait_ge(m_cp, 2 * B)
                elif step in (6,):
                    pe.wait_ge(tv, 6)
                elif step == 7:
                    pe.wait_ge(tv, 8)
                else:
                    pe.wait_ge(tv, step)
                if step in (0, 1, 4, 5):
                    src = attn if step < 2 else h2
                    for t in range(4):
                        ins = T_.transpose(psM[:, P * t:P * t + P], src[:, 4 * half + t, 0:D], ident[:, :])
                if step in (2, 3):
                    pe.wait_ge(c_modc, 3)
                    for t in range(4):
                        at = (4 * half + t) * P
                        T_.matmul(psM[:, P * t:P * t + P], attnT[:, at:at + P], wog[:, b, :],
                                  start=True, stop=False)
                        ins = T_.matmul(psM[:, P * t:P * t + P], ones1[:, :], bog[:, b, :],
                                        start=False, stop=True)
                if step == 6:
                    for t in range(NT):
                        ins = T_.matmul(psM[:, E * t:E * t + E], h2T[:, P * t:P * t + P], rw[:, :],
                                        start=True, stop=True)
                if step == 7:
                    ohs = oh[:, :, :, :].rearrange("p b t e -> p (b t) e")
                    ins = T_.matmul(psM[:, 64:64 + NT * E], upper[:, :],
                                    oh[:, b, :, :].rearrange("p t e -> p (t e)"), start=True, stop=False,
                                    skip_group_check=True)
                    for t in range(b * NT + NT - 1):
                        first = max(t + 1 - b * NT, 0)
                        n = NT - first
                        last = t == b * NT + NT - 2
                        ins = T_.matmul(psM[:, 64 + E * first:64 + NT * E], onesb[:, 0:P],
                                        ohs[:, t:t + 1, :].to_broadcast([P, n, E]), start=False,
                                        stop=last, skip_group_check=True)
                ins.then_inc(tp, 1)

            project(0)
            transpose_qk(0)
            project(1)
            transpose_qk(1)
            for b in range(B):
                maxima(b)
            total = B * NP * NU
            per_batch = NP * NU
            for b in range(B):
                n0 = b * per_batch
                scores(n0)
                for n in range(n0, n0 + per_batch):
                    if n + 1 < n0 + per_batch:
                        scores(n + 1)
                    values(n)
                    if n % NU == NU - 1 and n // NU % NP == NP - 1:
                        to_tokens(n // NU)
                    elif n % NU == 1 and n // NU % NP > 0:
                        to_tokens(n // NU - 1)
                for step in range(8):
                    router(b, step)

            def rows_T(e):
                pe.wait_ge(x_d[e], 16)
                if e < 2:
                    pe.wait_ge(o_cp, B * NP)
                else:
                    pe.wait_ge(x_cp, e - 1)
                for t in range(SPE):
                    ins = T_.transpose(psO[e % 2][:, P * t:P * t + P], xe[:, e, t, 0:D], ident[:, :])
                ins.then_inc(x_T, 1)

            def hidden(e):
                pe.wait_ge(x_cp, e + 1)
                if e < 2:
                    pe.wait_ge(s_exp, total)
                else:
                    pe.wait_ge(h_a, e - 1)
                    pe.wait_ge(h_v, e - 1)
                w1v = w1s[:, e, :].rearrange("d (p c) -> d c p", c=FC)
                for f in range(FC):
                    ins = T_.matmul(psS[e % 2][:, f // 2, CAP * (f % 2):CAP * (f % 2) + CAP], w1v[:, f, :],
                                    xeT[:, e % 2, :], start=True, stop=True)
                    if f % 2:
                        ins.then_inc(h_mm, 1)

            def outputs(e):
                pe.wait_ge(h_a, e + 1)
                pe.wait_ge(h_v, e + 1)
                if e < 2:
                    pe.wait_ge(t_v[B - 1], 9)
                else:
                    pe.wait_ge(y_cp, e - 1)
                dst = (psN, psM)[e % 2]
                for t in range(SPE):
                    for f in range(FC):
                        T_.matmul(dst[:, D * t:D * t + D], hid[:, e % 2, f, P * t:P * t + P],
                                  w2s[:, e, D * f:D * f + D], start=(f == 0), stop=False)
                    ins = T_.matmul(dst[:, D * t:D * t + D], ones1[:, :], b2r[:, D * e:D * e + D],
                                    start=False, stop=True)
                ins.then_inc(y_mm, 1)

            rows_T(0)
            pe.wait_ge(l_ffn, 48)
            for e in range(E):
                if e + 1 < E:
                    rows_T(e + 1)
                hidden(e)
                if e >= 1:
                    outputs(e - 1)
            outputs(E - 1)


_INS = ["L0_attn_x", "L0_attn_Wk", "L0_attn_Wq", "L0_attn_Wv", "L0_attn_Wo", "L0_attn_bo", "L0_attn_kln_w",
        "L0_attn_kln_b", "L0_attn_qln_w", "L0_attn_qln_b", "L0_ffn_router_w", "L0_ffn_w1", "L0_ffn_b1",
        "L0_ffn_w2", "L0_ffn_b2", "L0_c", "L0_wmod"]


def kernel(**inputs):
    import numpy as _np
    import concourse.bacc as _bacc
    from concourse import mybir as _mybir
    from concourse.bass_utils import run_bass_kernel_spmd as _run

    nc = _bacc.Bacc("TRN2", target_bir_lowering=False, num_devices=1)
    arrays, args = {}, []
    for name in _INS:
        a = _np.ascontiguousarray(inputs[name])
        arrays[f"in_{name}"] = a
        args.append(nc.dram_tensor(f"in_{name}", a.shape, _mybir.dt.from_np(a.dtype), kind="ExternalInput").ap())
    shape = inputs["L0_attn_x"].shape
    args.append(nc.dram_tensor("out_0", shape, _mybir.dt.float32, kind="ExternalOutput").ap())
    adaln_block(nc, *args)
    r = _run(nc, [arrays], core_ids=[0])
    return r.results[0]["out_0"]
```

```python
from contextlib import ExitStack

import concourse.bass as bass
from concourse import mybir

F32 = mybir.dt.float32
BF16 = mybir.dt.bfloat16
I32 = mybir.dt.int32
U32 = mybir.dt.uint32
ALU = mybir.AluOpType
ACT = mybir.ActivationFunctionType
AX = mybir.AxisListType

P = 128
EPS = 1e-5
NEG = -1e30
FAR = 1e6
Q_PART = [0, 0, 1, 0, 2, 1]
K_PART = [0, 1, 0, 2, 0, 1]
TERMS = len(Q_PART)
SAFE = 64.0
BF16_ONES = 1.0 + 0x3F80 / 2.0 ** 23


def adaln_block(nc, x, Wk, Wq, Wv, Wo, bo, kln_w, kln_b, qln_w, qln_b,
                router_w, w1, b1, w2, b2, c, wmod, out):
    B, T, D = x.shape
    HD = kln_w.shape[0]
    H = D // HD
    E = router_w.shape[1]
    F = w1.shape[2]
    FC = F // P
    NT = T // P
    TT = B * NT
    CAP = B * T // E
    NS = E * CAP
    SPE = CAP // P
    NP = H // 2
    SCALE = 1.0 / float(HD) ** 0.5
    XW = D + 4
    assert D == P and HD == 8 and E == 8 and NT == 8 and T * 4 == 8 * 512
    KM = TERMS * HD
    STACK_DMAS = 2 * 2 * TERMS

    UNITS = [[(0, 0, 4)], [(0, 4, 4)], [(1, 1, 3), (3, 3, 1)], [(1, 4, 4)],
             [(2, 2, 2), (6, 6, 2)], [(2, 4, 4)], [(3, 4, 4)], [(4, 4, 4)], [(5, 5, 3), (7, 7, 1)]]
    NU = len(UNITS)
    DIAG = [[u for u in UNITS if u[0][0] == u[0][1]].index(u) if u[0][0] == u[0][1] else None for u in UNITS]
    ND = sum(d is not None for d in DIAG)

    def diag_columns(unit):
        at, cols = 0, []
        for j, i0, n in unit:
            if j == i0:
                cols.append(at)
            at += n * P
        return cols

    SIDE = {(k // 2, (2, 6)[k % 2]): ("prepare", k) for k in range(14)}
    for k, at in enumerate(((8, 6), (9, 2), (9, 6), (10, 6), (11, 6), (12, 2), (12, 6), (13, 2))):
        SIDE[at] = ("router", k)
    SCATTERS = {13: 2, 14: 3, 15: 3}
    assert B == 2 and NP == 8 and sum(SCATTERS.values()) == NT

    def unit_of(n):
        pair, u = divmod(n, NU)
        return pair // NP, pair % NP, u

    def masked_before(n):
        return (n // NU) * ND + sum(DIAG[u] is not None for u in range(n % NU))

    xs_dram = nc.dram_tensor("dispatched", [NS, XW], F32, kind="Internal").ap()
    yt_dram = nc.dram_tensor("expert_out", [B * T, D], F32, kind="Internal").ap()

    with ExitStack() as ctx:
        def sb(name, shape, dt=F32):
            return ctx.enter_context(nc.sbuf_tensor(name, shape, dt))

        def ps(name, shape):
            return ctx.enter_context(nc.psum_tensor(name, shape, F32))

        def sem(name):
            return ctx.enter_context(nc.semaphore(name))

        psS = [ps("psS0", [P, 2, 512]), ps("psS1", [P, 2, 512])]
        psO = [ps("psO0", [P, 512]), ps("psO1", [P, 512])]
        psN = ps("psN", [P, 512])
        psM = ps("psM", [P, 512])

        ident = sb("ident", [P, P])
        onesb = sb("onesb", [P, P], BF16)
        upper = sb("upper", [P, P], BF16)
        e8 = sb("e8", [HD, P])
        mask = sb("mask", [P, T])
        desc8 = sb("desc8", [P, NT, E])
        tokid = sb("tokid", [P, TT])
        zeros = sb("zeros", [P, XW * SPE])
        epsc = sb("epsc", [P, 1])
        xt = sb("xt", [P, TT, D])
        wst = sb("wst", [P, 2, D])
        wmean = sb("wmean", [P, 2 * H])
        wcen = sb("wcen", [P, 2, D])
        wqk = sb("wqk", [P, 2, D])
        wv = sb("wv", [P, D])
        wo = sb("wo", [P, D])
        bob = sb("bob", [P, D])
        lnr = sb("lnr", [4, HD])
        lnb = sb("lnb", [1, 4, HD])
        crow = sb("crow", [B, D])
        wm = sb("wm", [P, 6 * D])
        rw = sb("rw", [P, E])
        b1r = sb("b1r", [E, F])
        cT = sb("cT", [P, B])
        silu = sb("silu", [P, 3, B])
        silub = sb("silub", [P, B, P])
        sT = sb("sT", [P, B])
        lnT = sb("lnT", [HD, 4])
        lncol = sb("lncol", [P, 4])
        b1c = sb("b1c", [P, FC, E])
        modc = sb("modc", [P, 2, B])
        modr = sb("modr", [P, B, 4, D])
        gsign = sb("gsign", [P, B, 2, D])
        wog = sb("wog", [P, B, D])
        bog = sb("bog", [P, B, D])
        bprod = sb("bprod", [1, 6, HD])
        bsum = sb("bsum", [1, 8])
        flag = sb("flag", [1, 1], I32)
        bst = sb("bst", [P, NT, 6])
        mv = sb("mv", [P, NT, 2])
        nw = sb("nw", [P, 4, NT])
        xn = sb("xn", [P, NT, D])
        hT = sb("hT", [P, T])
        sq = sb("sq", [P, 2, 512])
        var = sb("var", [P, 4, 64])
        std = sb("std", [P, 256])
        rstd = sb("rstd", [P, 256])
        qkn = sb("qkn", [P, NT, 2, D])
        qkf = sb("qkf", [P, 2, 512])
        res = sb("res", [P, 2, 512])
        parts = sb("parts", [P, 2, 3, T], BF16)
        stack = [sb(f"stack{b}", [P, 2, NP, T], BF16) for b in range(B)]
        qz = sb("qz", [P, 2, 2, T], BF16)
        mtmp = hT
        negm = qkf[:, :, :].rearrange("p n t -> p (n t)")[0:H, :]
        mres = res[:, :, :].rearrange("p n t -> p (n t)")[0:H, :]
        mparts = parts[:, :, :, :].rearrange("p a n t -> p (a n t)")[0:H, 0:3 * T].rearrange("p (n t) -> p n t", n=3)
        v9 = sb("v9", [P, TT, H, HD + 1])
        mx = sb("mx", [P, NT, H])
        NPB = 3
        pbuf = [sb(f"pbuf{i}", [P, 2, 512]) for i in range(NPB)]
        ots = sb("ots", [P, 2, 512])
        rl = sb("rl", [P, 2, NT, 2])
        attn = sb("attn", [P, NT, D])
        attnT = sb("attnT", [P, T])
        h2 = sb("h2", [P, NT, XW])
        h2T = attnT
        rt = sb("rt", [P, 4, NT, E])
        ro = sb("ro", [P, 8, NT])
        oh = sb("oh", [P, B, NT, E], BF16)
        ohs32 = sb("ohs32", [P, E])
        ohsum = sb("ohsum", [P, E], BF16)
        gate = sb("gate", [P, TT])
        slot = sb("slot", [P, TT], U32)
        w12 = stack[0][:, :, :, :].rearrange("p a h t -> p (a h t)").bitcast(F32)
        w1s = w12[:, 0:E * F].rearrange("p (e f) -> p e f", e=E)
        w2s = w12[:, E * F:2 * E * F].rearrange("p (e f) -> p e f", e=E)
        xe = sb("xe", [P, E, SPE, XW])
        back = sb("back", [P, E, SPE], U32)
        none = sb("none", [P, E, SPE])
        xeT = sb("xeT", [P, 2, CAP])
        hid = qkn[:, :, :, :].rearrange("p t a d -> p (t a d)").rearrange("p (b f c) -> p b f c", b=2, f=FC)
        ye = sb("ye", [P, 2, SPE, D])
        yall = stack[1][:, :, :, :].rearrange("p a h t -> p (a h t)").bitcast(F32)
        yt = yall[:, 0:TT * D].rearrange(
            "p (t d) -> p t d", t=TT)
        yo = yall[:, TT * D:2 * TT * D].rearrange(
            "p (t d) -> p t d", t=TT)
        gg = yall[:, 2 * TT * D:3 * TT * D].rearrange(
            "p (t d) -> p t d", t=TT)
        b2b = xn

        l_small = sem("l_small")
        l_wm = sem("l_wm")
        l_x = [sem(f"l_x{b}") for b in range(B)]
        l_qkv = sem("l_qkv")
        l_late = sem("l_late")
        l_ffn = sem("l_ffn")
        l_b2 = sem("l_b2")
        k_pool = sem("k_pool")
        c_T = sem("c_T")
        c_cp = sem("c_cp")
        c_exp = sem("c_exp")
        c_silu = sem("c_silu")
        c_mod = sem("c_mod")
        c_modc = sem("c_modc")
        w_qk = sem("w_qk")
        v_ch = sem("v_ch")
        a_ch = sem("a_ch")
        g_ch = sem("g_ch")
        n_xn = sem("n_xn")
        n_T = sem("n_T")
        n_h = sem("n_h")
        q_mm = sem("q_mm")
        v_mm = sem("v_mm")
        v_cp = sem("v_cp")
        q_sq = sem("q_sq")
        q_var = sem("q_var")
        q_std = sem("q_std")
        q_n = sem("q_n")
        q_T = sem("q_T")
        q_f = sem("q_f")
        q_r = sem("q_r")
        q_2 = sem("q_2")
        q_3 = sem("q_3")
        k_st = [sem(f"k_st{b}") for b in range(B)]
        c_ep = sem("c_ep")
        k_qz = sem("k_qz")
        b_pe = sem("b_pe")
        b_v = sem("b_v")
        b_3 = sem("b_3")
        c_bs = sem("c_bs")
        c_bq = sem("c_bq")
        c_fl = sem("c_fl")
        m_ch = sem("m_ch")
        q_z = sem("q_z")
        st_d = [sem(f"st_d{b}") for b in range(B)]
        v_set = sem("v_set")
        m_mm = sem("m_mm")
        m_rd = sem("m_rd")
        m_T = sem("m_T")
        m_cp = sem("m_cp")
        m_p = sem("m_p")
        m_d = [sem(f"m_d{b}") for b in range(B)]
        s_mm = sem("s_mm")
        s_exp = sem("s_exp")
        s_mask = sem("s_mask")
        s_pv = sem("s_pv")
        o_cp = sem("o_cp")
        o_mm = sem("o_mm")
        o_n = sem("o_n")
        t_pe = [sem(f"t_pe{b}") for b in range(B)]
        t_v = [sem(f"t_v{b}") for b in range(B)]
        t_e = sem("t_e")
        z_d = sem("z_d")
        d_d = [sem(f"d_d{b}") for b in range(B)]
        x_d = [sem(f"x_d{i}") for i in range(E)]
        x_i = sem("x_i")
        x_T = sem("x_T")
        x_cp = sem("x_cp")
        h_mm = sem("h_mm")
        h_a = sem("h_a")
        h_v = sem("h_v")
        y_mm = sem("y_mm")
        y_cp = sem("y_cp")
        y_d = [sem(f"y_d{i}") for i in range(2)]
        f_l = [sem(f"f_l{b}") for b in range(4)]
        w_gg = sem("w_gg")
        f_v = sem("f_v")
        f_o = sem("f_o")

        K_POOL = 4
        QT = TT // 4
        block = ctx.enter_context(nc.Block())

        def bank(b, half):
            return psN if b == B - 1 and half else psM

        def read_flag(engine):
            register = engine.alloc_register("general")
            engine.reg_load(register, flag[0:1, 0:1])
            return engine.snap(register)

        def stack_side(engine, b, a, order):
            for g in range(2):
                for n, part in enumerate(order):
                    at = 64 * g + HD * n
                    engine.dma_start(stack[b][at:at + HD, a, :, :],
                                     parts[64 * g:64 * g + 64, a, part, :]).then_inc(st_d[b], 16)

        @block.sync
        def _(sp):
            sp.dma_start(crow[:, :], c).then_inc(l_small, 16)
            sp.dma_start(xt[:, 0:NT, :], x[0].rearrange("(t p) d -> p t d", p=P)).then_inc(l_x[0], 16)
            for n, v in enumerate((qln_w, qln_b, kln_w, kln_b)):
                sp.dma_start(lnr[n:n + 1, :], v.rearrange("(a s) -> a s", a=1)).then_inc(l_small, 16)
            sp.dma_start(b1r[:, :], b1).then_inc(l_small, 16)
            sp.dma_start(wm[:, :], wmod).then_inc(l_wm, 16)
            for n, w in enumerate((Wq, Wk)):
                sp.dma_start(wst[:, n, :], w).then_inc(l_qkv, 16)
            sp.dma_start(wv[:, :], Wv).then_inc(l_qkv, 16)
            for n, v in enumerate((qln_w, qln_b, kln_w, kln_b)):
                sp.dma_start(lnb[:, n, :], v.rearrange("(a s) -> a s", a=1)).then_inc(l_late, 16)
            for b in range(1, B):
                sp.dma_start(xt[:, b * NT:(b + 1) * NT, :],
                             x[b].rearrange("(t p) d -> p t d", p=P)).then_inc(l_x[b], 16)
            sp.dma_start(wo[:, :], Wo).then_inc(l_late, 16)
            sp.dma_start(bob[:, :], bo.partition_broadcast(P)).then_inc(l_late, 16)
            sp.dma_start(rw[:, :], router_w).then_inc(l_late, 16)

            def stack_parts(b):
                if b == 0:
                    sp.wait_ge(q_r, 4)
                    sp.wait_ge(q_2, 4)
                    sp.wait_ge(q_3, 4)
                else:
                    sp.wait_ge(b_3, 4)
                sp.wait_ge(k_st[b], 1)
                for a, order in enumerate((Q_PART, K_PART)):
                    if b == 0 and a == 1:
                        continue
                    stack_side(sp, b, a, order)

            def stack_shift(b):
                sp.wait_ge(m_p, 3 * (b + 1))
                for g in range(2):
                    for n in range(3):
                        at = 64 * g + KM + n
                        sp.dma_start(stack[b][at:at + 1, 0, :, :],
                                     mparts[NP * g:NP * g + NP, n, :]).then_inc(m_d[b], 16)

            stack_parts(0)
            sp.wait_ge(k_pool, K_POOL)
            for e in range(E):
                sp.dma_start(xs_dram[e * CAP:(e + 1) * CAP, :].rearrange("(p t) w -> p (t w)", p=P),
                             zeros[:, :]).then_inc(z_d, 16)
                sp.dma_start(yt_dram[e * CAP:(e + 1) * CAP, :].rearrange("(p t) w -> p (t w)", p=P),
                             zeros[:, 0:SPE * D]).then_inc(z_d, 16)
            sp.wait_ge(c_fl, 1)
            general = read_flag(sp)
            with sp.If(general != 0):
                stack_shift(0)
            sp.wait_ge(b_pe, 2)
            sp.dma_start(b2b[:, :, :].rearrange("p e d -> p (e d)"),
                         b2.rearrange("e d -> (e d)").partition_broadcast(P)).then_inc(l_b2, 16)
            stack_parts(1)
            with sp.If(general != 0):
                stack_shift(1)
            sp.wait_ge(s_mm, NP * NU)
            sp.dma_start(w1s[:, :, :], w1.rearrange("e d f -> d e f")).then_inc(l_ffn, 16)
            sp.dma_start(w2s[:, :, :], w2.rearrange("e (p c) d -> p e (c d)", c=FC)).then_inc(l_ffn, 16)
            for b in range(B):
                sp.wait_ge(d_d[b], 16 * NT)
            for e in range(E):
                sp.dma_start(xe[:, e, :, :], xs_dram[e * CAP:(e + 1) * CAP, :].rearrange(
                    "(t p) w -> p t w", p=P)).then_inc(x_d[e], 16)
            for i in range(2):
                sp.wait_ge(y_d[i], 16 * SPE * E // 2)
            for q in range(4):
                sp.dma_start(yt[:, q * QT:(q + 1) * QT, :], yt_dram[q * QT * P:(q + 1) * QT * P, :].rearrange(
                    "(t p) d -> p t d", p=P)).then_inc(f_l[q], 16)
            for q in range(4):
                sp.wait_ge(f_v, q + 1)
                b, t0 = divmod(q * QT, NT)
                sp.dma_start(out[b].rearrange("(t p) d -> p t d", p=P)[:, t0:t0 + QT, :],
                             yo[:, q * QT:(q + 1) * QT, :]).then_inc(f_o, 16)
            sp.wait_ge(f_o, 16 * 4)

        @block.gpsimd
        def _(pool):
            chain = [0]

            def link(ins):
                chain[0] += 1
                ins.then_inc(g_ch, 1)
                pool.wait_ge(g_ch, chain[0])

            def fill_stack(b):
                for a, value in enumerate((0.0, BF16_ONES)):
                    ins = nc.gpsimd.memset(stack[b][:, a, :, :].rearrange("p h t -> p (h t)").bitcast(F32), value)
                ins.then_inc(k_st[b], 1)

            link(nc.gpsimd.memset(ident[:, :], 0.0))
            nc.gpsimd.affine_select(out=ident[:, :], in_=ident[:, :], compare_op=ALU.not_equal, fill=1.0, base=0,
                                    pattern=[[-1, P]], channel_multiplier=1).then_inc(k_pool, 1)
            link(nc.gpsimd.memset(e8[:, :], 0.0))
            nc.gpsimd.affine_select(out=e8[:, :].rearrange("k (g s p) -> k g s p", g=2, s=HD),
                                    in_=e8[:, :].rearrange("k (g s p) -> k g s p", g=2, s=HD),
                                    compare_op=ALU.not_equal, fill=1.0, base=0,
                                    pattern=[[0, 2], [-1, HD], [0, NP]],
                                    channel_multiplier=1).then_inc(k_pool, 1)
            nc.gpsimd.memset(zeros[:, :], 0.0).then_inc(k_pool, 1)
            nc.gpsimd.memset(onesb[:, :], 1.0).then_inc(k_pool, 1)
            fill_stack(0)
            nc.gpsimd.memset(qz[:, :, :, :].rearrange("p n g t -> p (n g t)").bitcast(F32), 0.0).then_inc(k_qz, 1)
            nc.gpsimd.memset(v9[:, :, :, HD:HD + 1], 1.0).then_inc(v_set, 1)
            pool.wait_ge(k_pool, K_POOL)
            nc.gpsimd.affine_select(out=upper[:, :], in_=onesb[:, 0:P], compare_op=ALU.is_ge, fill=0.0, base=0,
                                    pattern=[[1, P]], channel_multiplier=-1).then_inc(v_set, 1)
            link(nc.gpsimd.memset(mask[:, :], 0.0))
            nc.gpsimd.affine_select(out=mask[:, T - P:T], in_=mask[:, T - P:T], compare_op=ALU.is_ge, fill=NEG,
                                    base=0, pattern=[[-1, P]], channel_multiplier=1).then_inc(v_set, 1)
            nc.gpsimd.iota(desc8[:, :, :], pattern=[[0, NT], [-1, E]], base=E, channel_multiplier=0,
                           allow_small_or_imprecise_dtypes=True).then_inc(v_set, 1)
            nc.gpsimd.iota(tokid[:, :], pattern=[[P, TT]], base=0, channel_multiplier=1,
                           allow_small_or_imprecise_dtypes=True).then_inc(v_set, 1)

            def third_parts():
                for n in range(4):
                    half, a = divmod(n, 2)
                    pool.wait_ge(q_2, n + 1)
                    nc.gpsimd.tensor_tensor(parts[:, a, 2, 512 * half:512 * half + 512], res[:, n % 2, :],
                                            parts[:, a, 1, 512 * half:512 * half + 512],
                                            ALU.subtract).then_inc(q_3, 1)

            def scatter(b, t):
                nc.gpsimd.indirect_dma_start(
                    out=xs_dram[:, :], out_offset=bass.IndirectOffsetOnAxis(
                        ap=slot[:, b * NT + t:b * NT + t + 1], axis=0),
                    in_=h2[:, t, :], in_offset=None, bounds_check=NS - 1,
                    oob_is_err=False).then_inc(d_d[b], 16)

            def mask_units():
                sent = 0
                for n in range(B * NP * NU):
                    pair, u = divmod(n, NU)
                    if DIAG[u] is None:
                        continue
                    pool.wait_ge(s_exp, n + 1)
                    cols = diag_columns(UNITS[u])
                    for at in cols:
                        v = pbuf[n % NPB][:, :, at:at + P]
                        ins = nc.gpsimd.affine_select(out=v, in_=v, compare_op=ALU.is_ge, fill=0.0, base=0,
                                                      pattern=[[0, 2], [1, P]], channel_multiplier=-1)
                        if at == cols[-1]:
                            ins.then_inc(s_mask, 1)
                    if u == 4 and pair in SCATTERS:
                        if sent == 0:
                            pool.wait_ge(t_v[0], 10)
                            pool.wait_ge(z_d, 16 * 2 * E)
                        for t in range(sent, sent + SCATTERS[pair]):
                            scatter(0, t)
                        sent += SCATTERS[pair]

            third_parts()
            fill_stack(1)
            mask_units()
            pool.wait_ge(t_v[B - 1], 10)
            for t in range(NT):
                scatter(B - 1, t)
            for e in range(E):
                pool.wait_ge(x_i, e + 1)
                pool.wait_ge(y_cp, e + 1)
                for t in range(SPE):
                    nc.gpsimd.indirect_dma_start(
                        out=yt_dram[:, :], out_offset=bass.IndirectOffsetOnAxis(
                            ap=back[:, e, t:t + 1], axis=0),
                        in_=ye[:, e % 2, t, :], in_offset=None, bounds_check=B * T - 1,
                        oob_is_err=False).then_inc(y_d[e % 2], 16)

        @block.scalar
        def _(act):
            act.wait_ge(c_cp, 1)
            nc.scalar.activation(silu[:, 0, :], cT[:, :], ACT.Exp, scale=-1.0).then_inc(c_exp, 1)
            act.wait_ge(c_modc, 1)

            def router_exp(b):
                act.wait_ge(t_v[b], 8)
                if b:
                    act.wait_ge(t_v[b - 1], 10)
                nc.scalar.activation(rt[:, 1, :, :], rt[:, 0, :, :], ACT.Exp).then_inc(t_e, 1)

            for half in range(2):
                act.wait_ge(n_T, half + 1)
                src = psN if half == 0 else psM
                nc.scalar.activation(hT[:, 512 * half:512 * half + 512], src[:, :], ACT.Identity,
                                     bias=modc[:, 0, 0:1], scale=modc[:, 1, 0:1]).then_inc(n_h, 1)
            for n in range(4):
                act.wait_ge(q_mm, n + 1)
                if n >= 2:
                    act.wait_ge(q_var, n - 1)
                nc.scalar.activation(sq[:, n % 2, :], psS[n // 2][:, n % 2, :],
                                     ACT.Square).then_inc(q_sq, 1)
            act.wait_ge(q_var, 4)
            act.wait_ge(c_ep, 1)
            nc.scalar.activation(std[:, :], var[:, :, :].rearrange("p a c -> p (a c)"), ACT.Sqrt,
                                 bias=epsc[:, :], scale=1.0 / HD).then_inc(q_std, 1)
            act.wait_ge(c_bs, 1)
            nc.scalar.activation(bsum[:, 4:6], bsum[:, 2:4], ACT.Sqrt).then_inc(c_bq, 1)
            for n in range(2):
                act.wait_ge(v_mm, n + 1)
                nc.scalar.activation(v9[:, 4 * n:4 * n + 4, :, 0:HD],
                                     psO[n][:, :].rearrange("p (t h s) -> p t h s", t=4, h=H),
                                     ACT.Copy).then_inc(v_cp, 1)

            def second(n):
                half, a = divmod(n, 2)
                act.wait_ge(q_r, n + 1)
                nc.scalar.activation(parts[:, a, 1, 512 * half:512 * half + 512], res[:, n % 2, :],
                                     ACT.Copy).then_inc(q_2, 1)

            for n in range(4):
                act.wait_ge(q_T, n + 1)
                if n >= 2:
                    act.wait_ge(q_r, n - 1)
                a = n % 2
                nc.scalar.activation(qkf[:, n % 2, :], (psN, psM)[n % 2][:, :], ACT.Identity,
                                     bias=lncol[:, 2 * a + 1:2 * a + 2],
                                     scale=lncol[:, 2 * a:2 * a + 1]).then_inc(q_f, 1)
                if n >= 1:
                    second(n - 1)
            second(3)
            act.wait_ge(k_st[0], 1)
            act.wait_ge(q_r, 4)
            act.wait_ge(q_2, 4)
            act.wait_ge(q_3, 4)
            stack_side(act, 0, 1, K_PART)

            for n in range(B * NP * NU):
                act.wait_ge(s_mm, n + 1)
                if n >= NPB:
                    act.wait_ge(s_pv, n - NPB + 1)
                nc.scalar.activation(pbuf[n % NPB][:, :, :], psS[n % 2][:, :, :], ACT.Exp).then_inc(s_exp, 1)
                if n == 13 * NU:
                    router_exp(0)
            router_exp(B - 1)
            for e in range(E):
                act.wait_ge(h_mm, 2 * e + 1)
                if e >= 2:
                    act.wait_ge(y_mm, e - 1)
                for f in range(2):
                    ins = nc.scalar.activation(hid[:, e % 2, f, :],
                                               psS[e % 2][:, 0, CAP * f:CAP * f + CAP], ACT.Relu,
                                               bias=b1c[:, f, e:e + 1])
                ins.then_inc(h_a, 1)

        @block.vector
        def _(dve):
            chain = [0]
            V = nc.vector

            def link(ins):
                chain[0] += 1
                ins.then_inc(v_ch, 1)
                dve.wait_ge(v_ch, chain[0])

            def rsqrt(v, scale, a, y, t, r):
                link(V.tensor_scalar(a, v, scale, EPS, ALU.mult, ALU.add))
                link(V.tensor_scalar(t.bitcast(I32), a.bitcast(I32), 1, None, ALU.arith_shift_right))
                link(V.tensor_scalar(y.bitcast(I32), t.bitcast(I32), -1.0, float(0x5f3759df), ALU.mult, ALU.add))
                for i in range(3):
                    link(V.tensor_tensor(t, y, y, ALU.mult))
                    link(V.scalar_tensor_tensor(out=t, in0=a, scalar=-0.5, in1=t, op0=ALU.mult, op1=ALU.mult))
                    link(V.scalar_tensor_tensor(out=(r if i == 2 else y), in0=t, scalar=1.5, in1=y,
                                                op0=ALU.add, op1=ALU.mult))

            def tile_stats(src, tiles):
                for t in tiles:
                    ins = V.bn_stats(bst[:, t, :], src(t))
                link(ins)

            def tile_rstd():
                for t in range(NT):
                    ins = V.bn_aggr(mv[:, t, :], bst[:, t, :])
                link(ins)
                rsqrt(mv[:, :, 1], 1.0, *(nw[:, i, :] for i in range(4)))

            def normalise(b):
                tile_stats(lambda t: xt[:, b * NT + t, :], range(NT))
                tile_rstd()
                for t in range(NT):
                    ins = V.tensor_scalar(xn[:, t, :], xt[:, b * NT + t, :], mv[:, t, 0:1], nw[:, 3, t:t + 1],
                                          ALU.subtract, ALU.mult)
                    if t % 4 == 3:
                        ins.then_inc(n_xn, 1)

            V.memset(epsc[:, :], EPS).then_inc(c_ep, 1)
            for b in range(2):
                V.memset(psO[b][:, :], 0.0)
            dve.wait_ge(c_T, 1)
            V.tensor_copy(cT[:, :], psM[:, 0:B]).then_inc(c_cp, 1)
            V.tensor_copy(lnT[:, :], psM[0:HD, 4:8])
            V.tensor_copy(b1c[:, :, :].rearrange("p c e -> p (c e)"), psM[:, 32:32 + FC * E]).then_inc(c_cp, 1)
            dve.wait_ge(l_x[0], 16)
            normalise(0)
            dve.wait_ge(c_exp, 1)
            link(V.tensor_scalar(silu[:, 1, :], silu[:, 0, :], 1.0, None, ALU.add))
            link(V.reciprocal(silu[:, 2, :], silu[:, 1, :]))
            link(V.tensor_tensor(sT[:, :], cT[:, :], silu[:, 2, :], ALU.mult))
            for b in range(B):
                ins = V.tensor_copy(silub[:, b, :], sT[:, b:b + 1].to_broadcast([P, P]))
            ins.then_inc(c_silu, 1)
            dve.wait_ge(c_mod, 1)
            V.tensor_copy(modc[:, 0, :], psM[:, 64:64 + B])
            V.tensor_scalar(modc[:, 1, :], psM[:, 64 + B:64 + 2 * B], 1.0, None, ALU.add)
            V.tensor_scalar(lncol[:, 0:2], psM[:, 72:74], SCALE, None, ALU.mult)
            V.tensor_copy(lncol[:, 2:4], psM[:, 74:76]).then_inc(c_modc, 1)
            dve.wait_ge(l_qkv, 48)
            link(V.tensor_reduce(wmean[:, :], wst[:, :, :].rearrange("p a (h s) -> p (a h) s", s=HD), AX.X, ALU.add))
            link(V.scalar_tensor_tensor(
                out=wcen[:, :, :].rearrange("p a (h s) -> p (a h) s", s=HD),
                in0=wmean[:, :].rearrange("p (h o) -> p h o", o=1).to_broadcast([P, 2 * H, HD]),
                scalar=-1.0 / HD, in1=wst[:, :, :].rearrange("p a (h s) -> p (a h) s", s=HD),
                op0=ALU.mult, op1=ALU.add))
            for a in range(2):
                ins = V.tensor_copy(wqk[:, a, :].rearrange("k (g s p) -> k g s p", g=2, s=HD),
                                    wcen[:, a, :].rearrange("k (p g s) -> k g s p", g=2, s=HD))
            ins.then_inc(w_qk, 1)

            dve.wait_ge(l_late, 16 * 7)
            w_, b_ = lnb[:, 0:4:2, :], lnb[:, 1:4:2, :]
            V.tensor_tensor(bprod[:, 0, :], lnb[:, 0, :], lnb[:, 2, :], ALU.mult)
            V.tensor_tensor(bprod[:, 1, :], lnb[:, 1, :], lnb[:, 3, :], ALU.mult)
            V.tensor_tensor(bprod[:, 2, :], lnb[:, 1, :], lnb[:, 2, :], ALU.mult)
            link(V.tensor_tensor(bprod[:, 3, :], lnb[:, 0, :], lnb[:, 3, :], ALU.mult))
            V.tensor_tensor(bprod[:, 4, :], bprod[:, 2, :], bprod[:, 2, :], ALU.mult)
            V.tensor_tensor(bprod[:, 5, :], bprod[:, 3, :], bprod[:, 3, :], ALU.mult)
            link(V.scalar_tensor_tensor(out=bprod[:, 0, :], in0=bprod[:, 0, :], scalar=-1.0,
                                        in1=bprod[:, 0, :], op0=ALU.mult, op1=ALU.max))
            V.tensor_reduce(bsum[:, 0:1], bprod[:, 0, :], AX.X, ALU.max)
            link(V.tensor_reduce(bsum[:, 1:2], bprod[:, 1, :], AX.X, ALU.add))
            V.tensor_reduce(bsum[:, 2:4], bprod[:, 4:6, :], AX.X, ALU.add).then_inc(c_bs, 1)
            link(V.scalar_tensor_tensor(out=bsum[:, 1:2], in0=bsum[:, 1:2], scalar=-1.0, in1=bsum[:, 1:2],
                                        op0=ALU.mult, op1=ALU.max))
            link(V.tensor_scalar(bsum[:, 1:2], bsum[:, 1:2], SCALE, None, ALU.mult))
            link(V.scalar_tensor_tensor(out=bsum[:, 0:1], in0=bsum[:, 0:1], scalar=1.0 / SCALE, in1=bsum[:, 1:2],
                                        op0=ALU.mult, op1=ALU.add))

            for n in range(4):
                dve.wait_ge(q_sq, n + 1)
                V.tensor_reduce(var[:, n, :].rearrange("p (c h) -> p c h", h=NP),
                                sq[:, n % 2, :].rearrange("p (c s h) -> p c h s", s=HD, h=NP),
                                AX.X, ALU.add).then_inc(q_var, 1)
            dve.wait_ge(q_std, 1)
            link(V.reciprocal(rstd[:, :], std[:, :]))

            def scaled(n, src):
                V.tensor_tensor(
                    qkn[:, 2 * n:2 * n + 2, :, :].rearrange("p t a (g s h) -> p (t a g) s h", g=2, s=HD),
                    src.rearrange("p (c s h) -> p c s h", s=HD, h=NP),
                    rstd[:, 64 * n:64 * n + 64].rearrange("p (c o h) -> p c o h", o=1, h=NP).to_broadcast(
                        [P, 8, HD, NP]), ALU.mult).then_inc(q_n, 1)

            for n in range(4):
                scaled(n, psS[n // 2][:, n % 2, :])
            for n in range(4):
                half, a = divmod(n, 2)
                dve.wait_ge(q_f, n + 1)
                first = parts[:, a, 0, 512 * half:512 * half + 512]
                link(V.tensor_copy(first, qkf[:, n % 2, :]))
                if n >= 2:
                    dve.wait_ge(q_3, n - 1)
                V.tensor_tensor(res[:, n % 2, :], qkf[:, n % 2, :], first, ALU.subtract).then_inc(q_r, 1)
            dve.wait_ge(c_bq, 1)
            link(V.tensor_reduce(bsum[:, 6:7], bsum[:, 4:6], AX.X, ALU.add))
            link(V.tensor_tensor(bsum[:, 7:8], bsum[:, 6:7], bsum[:, 0:1], ALU.add))
            link(V.tensor_scalar(bsum[:, 6:7], bsum[:, 7:8], SAFE, -1.0, ALU.is_le, ALU.mult))
            V.tensor_scalar(flag[:, :], bsum[:, 6:7], 1.0, None, ALU.add).then_inc(c_fl, 1)

            def prepare(k):
                dve.wait_ge(b_pe, k + 1)
                if k < 2:
                    if k == 0:
                        dve.wait_ge(q_mm, 4)
                        dve.wait_ge(v_mm, 2)
                    V.tensor_scalar(hT[:, 512 * k:512 * k + 512], psM[:, :], modc[:, 1, 1:2], modc[:, 0, 1:2],
                                    ALU.mult, ALU.add).then_inc(b_v, 1)
                elif k < 6:
                    n = k - 2
                    if n == 0:
                        dve.wait_ge(q_T, 4)
                    raw = qkn[:, 2 * n:2 * n + 2, :, :].rearrange("p t a d -> p (t a d)")
                    V.tensor_copy(raw, psM[:, :]).then_inc(b_v, 1)
                    dve.wait_ge(b_v, k + 1)
                    link(V.tensor_tensor(sq[:, n % 2, :], raw, raw, ALU.mult))
                    link(V.tensor_reduce(var[:, n, :].rearrange("p (c h) -> p c h", h=NP),
                                         sq[:, n % 2, :].rearrange("p (c s h) -> p c h s", s=HD, h=NP),
                                         AX.X, ALU.add))
                elif k < 8:
                    t0 = NT + 4 * (k - 6)
                    V.tensor_copy(v9[:, t0:t0 + 4, :, 0:HD],
                                  psM[:, :].rearrange("p (t h s) -> p t h s", t=4, h=H)).then_inc(b_v, 1)
                    if k == 7:
                        rsqrt(var[:, :, :].rearrange("p a c -> p (a c)"), 1.0 / HD, std[:, :], sq[:, 0, 0:256],
                              sq[:, 1, 0:256], rstd[:, :])
                        for n in range(4):
                            scaled(n, qkn[:, 2 * n:2 * n + 2, :, :].rearrange("p t a d -> p (t a d)"))
                elif k < 12:
                    n = k - 8
                    half, a = divmod(n, 2)
                    if n == 0:
                        dve.wait_ge(st_d[0], 16 * STACK_DMAS)
                    V.tensor_scalar(qkf[:, n % 2, :], psM[:, :], lncol[:, 2 * a:2 * a + 1],
                                    lncol[:, 2 * a + 1:2 * a + 2], ALU.mult, ALU.add).then_inc(b_v, 1)
                    dve.wait_ge(b_v, k + 1)
                    first, second, third = (parts[:, a, i, 512 * half:512 * half + 512] for i in range(3))
                    link(V.tensor_copy(first, qkf[:, n % 2, :]))
                    link(V.tensor_tensor(res[:, n % 2, :], qkf[:, n % 2, :], first, ALU.subtract))
                    link(V.tensor_copy(second, res[:, n % 2, :]))
                    V.tensor_tensor(third, res[:, n % 2, :], second, ALU.subtract).then_inc(b_3, 1)
                else:
                    b = k - 12
                    V.tensor_copy(modr[:, b, :, :].rearrange("p a d -> p (a d)"), psM[:, :]).then_inc(b_v, 1)
                    if b == B - 1:
                        dve.wait_ge(b_v, k + 1)
                        mod_rows()

            def mod_rows():
                for b in range(B):
                    V.tensor_scalar(modr[:, b, 2, :], modr[:, b, 2, :], 1.0, None, ALU.add)
                    for i, a in enumerate((0, 3)):
                        ins = V.tensor_scalar(gsign[:, b, i, :], modr[:, b, a, :], 0.0, 2.0, ALU.is_ge, ALU.mult)
                link(ins)
                for b in range(B):
                    for a in (0, 3):
                        ins = V.scalar_tensor_tensor(out=modr[:, b, a, :], in0=modr[:, b, a, :], scalar=-1.0,
                                                     in1=modr[:, b, a, :], op0=ALU.mult, op1=ALU.max)
                link(ins)
                for b in range(B):
                    for a in (0, 3):
                        ins = V.tensor_scalar(modr[:, b, a, :], modr[:, b, a, :], 0.25, None, ALU.max)
                link(ins)
                for b in range(B):
                    for i, a in enumerate((0, 3)):
                        ins = V.scalar_tensor_tensor(out=modr[:, b, a, :], in0=gsign[:, b, i, :], scalar=-1.0,
                                                     in1=modr[:, b, a, :], op0=ALU.add, op1=ALU.mult)
                link(ins)
                for b in range(B):
                    V.tensor_tensor(wog[:, b, :], wo[:, :], modr[:, b, 0, :], ALU.mult)
                    ins = V.tensor_tensor(bog[:, b, :], bob[:, :], modr[:, b, 0, :], ALU.mult)
                ins.then_inc(c_modc, 1)
                dve.wait_ge(c_modc, 2)
                for b in range(B):
                    xs = xt[:, b * NT:(b + 1) * NT, :]
                    ins = V.tensor_tensor(xs, xs, bog[:, b:b + 1, :].to_broadcast([P, NT, D]), ALU.add)
                link(ins)

            def lay_q(pair):
                b, p = divmod(pair, NP)
                if pair == 0:
                    dve.wait_ge(k_qz, 1)
                if p == 0:
                    dve.wait_ge(st_d[b], 16 * STACK_DMAS)
                if pair >= 2:
                    dve.wait_ge(s_mm, NU * (pair - 1))
                V.tensor_copy(qz[0:64, pair % 2, 0, :], stack[b][0:64, 0, p, :])
                V.tensor_copy(qz[64:128, pair % 2, 1, :], stack[b][64:128, 0, p, :]).then_inc(q_z, 1)

            m_chain = [0]

            def m_link(ins):
                m_chain[0] += 1
                ins.then_inc(m_ch, 1)
                dve.wait_ge(m_ch, m_chain[0])

            def maxima(b):
                dve.wait_ge(v_set, 4)
                if b == 0:
                    dve.wait_ge(q_mm, 4)
                    dve.wait_ge(v_mm, 2)
                for i in range(NT):
                    for h in range(H):
                        m = (b * NT + i) * H + h
                        p, g = divmod(h, 2)
                        w = (i + 1) * P
                        dve.wait_ge(m_mm, m + 1)
                        if m >= 1:
                            dve.wait_ge(m_rd, m)
                        V.tensor_tensor_reduce(out=mtmp[:, 0:w],
                                               in0=psS[m % 2][:, :, :].rearrange("p a c -> p (a c)")[:, 0:w],
                                               in1=mask[:, T - w:T], scale=1.0, scalar=-3e38,
                                               op0=ALU.add, op1=ALU.max,
                                               accum_out=mx[:, i, g * NP + p:g * NP + p + 1]).then_inc(m_rd, 1)
                for half in range(2):
                    dve.wait_ge(m_T, 2 * b + half + 1)
                    if b == 0:
                        dve.wait_ge(q_r, 4)
                        dve.wait_ge(q_2, 4)
                        dve.wait_ge(q_3, 4)
                    else:
                        dve.wait_ge(b_3, 4)
                    V.tensor_scalar(negm[:, 512 * half:512 * half + 512],
                                    (psN, psM)[half][0:H, :], -1.0, None, ALU.mult).then_inc(m_cp, 1)
                dve.wait_ge(m_cp, 2 * b + 2)
                dve.wait_ge(st_d[b], 16 * STACK_DMAS)
                V.tensor_copy(mparts[:, 0, :], negm[:, :]).then_inc(m_p, 1)
                dve.wait_ge(m_p, 3 * b + 1)
                m_link(V.tensor_tensor(mres[:, :], negm[:, :], mparts[:, 0, :], ALU.subtract))
                V.tensor_copy(mparts[:, 1, :], mres[:, :]).then_inc(m_p, 1)
                dve.wait_ge(m_p, 3 * b + 2)
                V.tensor_tensor(mparts[:, 2, :], mres[:, :], mparts[:, 1, :], ALU.subtract).then_inc(m_p, 1)
                dve.wait_ge(m_d[b], 16 * 6)

            def copy_sums(n):
                dve.wait_ge(s_pv, NU * (n + 1))
                if n >= 2:
                    dve.wait_ge(o_mm, n - 1)
                V.tensor_copy(ots[:, n % 2, :], psO[n % 2][:, :]).then_inc(o_cp, 1)

            def divide(n):
                p = n % NP
                dve.wait_ge(o_mm, n + 1)
                if n == NP:
                    dve.wait_ge(t_pe[0], 2)
                v = psN[:, :].rearrange("p (t g r) -> p t g r", t=NT, g=2)
                link(V.reciprocal(rl[:, n % 2, :, :], v[:, :, :, HD]))
                V.tensor_tensor(attn[:, :, 2 * HD * p:2 * HD * (p + 1)].rearrange("p t (g s) -> p t g s", g=2),
                                v[:, :, :, 0:HD],
                                rl[:, n % 2, :, :].rearrange("p t (g o) -> p t g o", o=1).to_broadcast(
                                    [P, NT, 2, HD]), ALU.mult).then_inc(o_n, 1)

            def router(b, step):
                tv = t_v[b]
                t0 = b * NT
                if step in (0, 1, 4, 5):
                    half = step % 2
                    dve.wait_ge(t_pe[b], step + 1)
                    V.tensor_copy(attnT[:, 512 * half:512 * half + 512], bank(b, half)[:, :]).then_inc(tv, 1)
                if step in (2, 3):
                    half = step % 2
                    dve.wait_ge(t_pe[b], step + 1)
                    xs = xt[:, t0 + 4 * half:t0 + 4 * half + 4, :].rearrange("p t d -> p (t d)")
                    V.tensor_tensor(xs, xs, bank(b, half)[:, :], ALU.add).then_inc(tv, 1)
                    dve.wait_ge(tv, step + 1)
                    tile_stats(lambda t: xt[:, t0 + t, :], range(4 * half, 4 * half + 4))
                    if step == 2:
                        return
                    tile_rstd()
                    if b:
                        dve.wait_ge(d_d[b - 1], 16 * NT)
                    for t in range(NT):
                        ins = V.scalar_tensor_tensor(out=h2[:, t, 0:D], in0=xt[:, t0 + t, :], scalar=mv[:, t, 0:1],
                                                     in1=modr[:, b, 2, :], op0=ALU.subtract, op1=ALU.mult)
                    link(ins)
                    for t in range(NT):
                        V.scalar_tensor_tensor(out=h2[:, t, 0:D], in0=h2[:, t, 0:D], scalar=nw[:, 3, t:t + 1],
                                               in1=modr[:, b, 1, :], op0=ALU.mult, op1=ALU.add)
                    V.memset(h2[:, :, D:XW], FAR)
                    link(V.tensor_copy(ro[:, 7, :], tokid[:, t0:t0 + NT]))
                    V.tensor_scalar(h2[:, :, D], ro[:, 7, :], 1.0, None, ALU.add).then_inc(tv, 1)
                if step == 6:
                    dve.wait_ge(t_pe[b], 7)
                    lg = psM[:, 0:NT * E].rearrange("p (t e) -> p t e", e=E)
                    link(V.tensor_reduce(ro[:, 0, :], lg, AX.X, ALU.max))
                    V.tensor_tensor(rt[:, 0, :, :], lg,
                                    ro[:, 0, :].rearrange("p (t o) -> p t o", o=1).to_broadcast([P, NT, E]),
                                    ALU.subtract).then_inc(tv, 1)
                    dve.wait_ge(tv, 8)
                    link(V.scalar_tensor_tensor(out=rt[:, 2, :, :], in0=rt[:, 0, :, :], scalar=0.0,
                                                in1=desc8[:, :, :], op0=ALU.is_ge, op1=ALU.mult))
                    link(V.tensor_reduce(ro[:, 1, :], rt[:, 2, :, :], AX.X, ALU.max))
                    V.tensor_tensor(oh[:, b, :, :], desc8[:, :, :],
                                    ro[:, 1, :].rearrange("p (t o) -> p t o", o=1).to_broadcast([P, NT, E]),
                                    ALU.is_equal).then_inc(tv, 1)
                    if b + 1 < B:
                        dve.wait_ge(tv, 9)
                        link(V.tensor_reduce(ohs32[:, :], oh[:, b, :, :].rearrange("p t e -> p e t"), AX.X, ALU.add))
                        link(V.tensor_copy(ohsum[:, :], ohs32[:, :]))
                if step == 7:
                    dve.wait_ge(t_pe[b], 8)
                    dve.wait_ge(t_e, b + 1)
                    cnt = psM[:, 64:64 + NT * E].rearrange("p (t e) -> p t e", e=E)
                    link(V.tensor_reduce(ro[:, 2, :], rt[:, 1, :, :], AX.X, ALU.add))
                    V.reciprocal(ro[:, 3, :], ro[:, 2, :])
                    link(V.tensor_tensor(rt[:, 3, :, :], cnt, oh[:, b, :, :], ALU.mult))
                    link(V.tensor_reduce(ro[:, 4, :], rt[:, 3, :, :], AX.X, ALU.add))
                    link(V.tensor_scalar(ro[:, 5, :], ro[:, 4, :], float(CAP), None, ALU.is_le))
                    V.tensor_tensor(gate[:, t0:t0 + NT], ro[:, 3, :], ro[:, 5, :], ALU.mult)
                    link(V.scalar_tensor_tensor(out=ro[:, 6, :], in0=ro[:, 1, :], scalar=-float(CAP),
                                                in1=ro[:, 4, :], op0=ALU.mult, op1=ALU.add))
                    link(V.scalar_tensor_tensor(out=ro[:, 4, :], in0=ro[:, 5, :], scalar=-FAR, in1=ro[:, 6, :],
                                                op0=ALU.mult, op1=ALU.add))
                    V.tensor_scalar(slot[:, t0:t0 + NT], ro[:, 4, :], FAR + E * CAP - 1, None,
                                    ALU.add).then_inc(tv, 1)

            dve.wait_ge(l_x[1], 16)
            dve.wait_ge(n_T, 2)
            normalise(1)
            dve.wait_ge(c_fl, 1)
            general = read_flag(dve)
            with dve.If(general != 0):
                maxima(0)
            lay_q(0)
            lay_q(1)

            def side(pair, u):
                kind, k = SIDE.get((pair, u), (None, 0))
                if kind == "prepare":
                    prepare(k)
                if kind == "router":
                    router(0, k)

            for pair in range(B * NP):
                side(pair, 2)
                if pair:
                    divide(pair - 1)
                side(pair, 6)
                if pair == NP - 1:
                    with dve.If(general != 0):
                        maxima(1)
                    lay_q(NP)
                copy_sums(pair)
                if pair != NP - 2 and pair + 2 < B * NP:
                    lay_q(pair + 2)
            divide(B * NP - 1)
            for step in range(8):
                router(B - 1, step)

            def take(e):
                dve.wait_ge(x_d[e], 16)
                link(V.tensor_scalar(none[:, e, :], xe[:, e, :, D], 0.0, FAR, ALU.is_le, ALU.mult))
                V.scalar_tensor_tensor(out=back[:, e, :], in0=xe[:, e, :, D], scalar=-1.0, in1=none[:, e, :],
                                       op0=ALU.add, op1=ALU.max).then_inc(x_i, 1)
                dve.wait_ge(x_T, e + 1)
                if e >= 2:
                    dve.wait_ge(h_mm, 2 * (e - 1))
                V.tensor_copy(xeT[:, e % 2, :], psO[e % 2][:, 0:CAP]).then_inc(x_cp, 1)

            def finish(e):
                dve.wait_ge(y_mm, e + 1)
                if e == 0:
                    dve.wait_ge(l_b2, 16)
                if e >= 2:
                    dve.wait_ge(y_d[e % 2], 16 * SPE * (e // 2))
                V.tensor_tensor(ye[:, e % 2, :, :],
                                (psN, psM)[e % 2][:, 0:SPE * D].rearrange("p (t d) -> p t d", t=SPE),
                                b2b[:, e:e + 1, :].to_broadcast([P, SPE, D]), ALU.add).then_inc(y_cp, 1)

            dve.wait_ge(s_mm, B * NP * NU)
            for t in range(TT):
                ins = V.tensor_scalar(gg[:, t, :], modr[:, t // NT, 3, :], gate[:, t:t + 1], None, ALU.mult)
            link(ins)
            take(0)
            for e in range(E):
                if e + 1 < E:
                    take(e + 1)
                dve.wait_ge(h_mm, 2 * e + 2)
                if e >= 2:
                    dve.wait_ge(y_mm, e - 1)
                for f in range(2, 4):
                    ins = V.tensor_scalar(hid[:, e % 2, f, :], psS[e % 2][:, 1, CAP * (f - 2):CAP * (f - 1)],
                                          b1c[:, f, e:e + 1], 0.0, ALU.add, ALU.max)
                ins.then_inc(h_v, 1)
                if e >= 1:
                    finish(e - 1)
            finish(E - 1)
            for q in range(4):
                dve.wait_ge(f_l[q], 16)
                tiles = slice(q * QT, (q + 1) * QT)
                link(V.tensor_tensor(yt[:, tiles, :], yt[:, tiles, :], gg[:, tiles, :], ALU.mult))
                V.tensor_tensor(yo[:, tiles, :], xt[:, tiles, :], yt[:, tiles, :], ALU.add).then_inc(f_v, 1)

        @block.tensor
        def _(pe):
            T_ = nc.tensor
            pe.wait_ge(k_pool, K_POOL)
            pe.wait_ge(l_small, 96)
            T_.transpose(psM[:, 0:B], crow[:, :], ident[0:B, 0:B])
            T_.transpose(psM[0:HD, 4:8], lnr[:, :], ident[0:4, 0:4])
            for f in range(FC):
                ins = T_.transpose(psM[:, 32 + E * f:32 + E * f + E],
                                   b1r[:, :].rearrange("e (p c) -> e c p", c=FC)[:, f, :], ident[0:E, 0:E])
            ins.then_inc(c_T, 1)
            pe.wait_ge(n_xn, 1)
            for t in range(4):
                ins = T_.transpose(psN[:, P * t:P * t + P], xn[:, t, :], ident[:, :])
            ins.then_inc(n_T, 1)
            pe.wait_ge(c_silu, 1)
            pe.wait_ge(c_cp, 2)
            pe.wait_ge(l_wm, 16)
            for a in range(2):
                T_.matmul(psM[:, 64 + B * a:64 + B * a + B], wm[:, D * a:D * a + D], sT[:, :], start=True, stop=True)
            T_.matmul(psM[:, 72:76], e8[:, :], lnT[:, :], start=True, stop=True).then_inc(c_mod, 1)
            pe.wait_ge(c_modc, 1)
            pe.wait_ge(n_xn, 2)
            for t in range(4):
                ins = T_.transpose(psM[:, P * t:P * t + P], xn[:, 4 + t, :], ident[:, :])
            ins.then_inc(n_T, 1)

            def project_qk(dst, t0):
                for t in range(2):
                    at = (t0 + t) * P
                    ins = T_.matmul(dst[:, 256 * t:256 * t + 256], hT[:, at:at + P],
                                    wqk[:, :, :].rearrange("p a d -> p (a d)"), start=True, stop=True)
                return ins

            def project_v(dst, t0):
                for t in range(4):
                    at = (t0 + t) * P
                    ins = T_.matmul(dst[:, P * t:P * t + P], hT[:, at:at + P], wv[:, :], start=True, stop=True)
                return ins

            def transpose_qk(dst, half, a):
                for t in range(4):
                    ins = T_.transpose(dst[:, P * t:P * t + P], qkn[:, 4 * half + t, a, :], ident[:, :])
                return ins

            pe.wait_ge(w_qk, 1)
            for half in range(2):
                pe.wait_ge(n_h, half + 1)
                for n in range(2 * half, 2 * half + 2):
                    project_qk(psS[n // 2][:, n % 2, :], 2 * n).then_inc(q_mm, 1)
            for half in range(2):
                project_v(psO[half], 4 * half).then_inc(v_mm, 1)
            for n in range(4):
                half, a = divmod(n, 2)
                pe.wait_ge(q_n, 2 * half + 2)
                if n < 2:
                    pe.wait_ge(n_h, n + 1)
                else:
                    pe.wait_ge(q_f, n - 1)
                transpose_qk((psN, psM)[n % 2], half, a).then_inc(q_T, 1)

            def prepare(k):
                if k == 0:
                    pe.wait_ge(n_xn, 4)
                    pe.wait_ge(q_f, 4)
                else:
                    pe.wait_ge(b_v, k)
                if k < 2:
                    for t in range(4):
                        ins = T_.transpose(psM[:, P * t:P * t + P], xn[:, 4 * k + t, :], ident[:, :])
                elif k < 6:
                    ins = project_qk(psM, 2 * (k - 2))
                elif k < 8:
                    ins = project_v(psM, 4 * (k - 6))
                elif k < 12:
                    half, a = divmod(k - 8, 2)
                    pe.wait_ge(q_n, 4 + 2 * half + 2)
                    ins = transpose_qk(psM, half, a)
                else:
                    b = k - 12
                    ins = T_.matmul(psM[:, :], silub[:, b, :], wm[:, 2 * D:6 * D], start=True, stop=True)
                ins.then_inc(b_pe, 1)

            def maxima(b):
                pe.wait_ge(st_d[b], 16 * STACK_DMAS)
                if b == 0:
                    pe.wait_ge(q_n, 4)
                else:
                    pe.wait_ge(s_exp, NP * NU)
                for i in range(NT):
                    for h in range(H):
                        m = (b * NT + i) * H + h
                        p, g = divmod(h, 2)
                        if m >= 2:
                            pe.wait_ge(m_rd, m - 1)
                        w = (i + 1) * P
                        for hf in range((w + 511) // 512):
                            n = min(512, w - 512 * hf)
                            ins = T_.matmul(psS[m % 2][:, hf, 0:n],
                                            stack[b][64 * g:64 * g + KM, 0, p, i * P:i * P + P],
                                            stack[b][64 * g:64 * g + KM, 1, p, 512 * hf:512 * hf + n],
                                            start=True, stop=True)
                        ins.then_inc(m_mm, 1)
                for half in range(2):
                    pe.wait_ge(m_rd, (b * NT + 4 * half + 4) * H)
                    if b == 0:
                        pe.wait_ge(q_f, 4)
                    else:
                        pe.wait_ge(o_n, NP - 1)
                        pe.wait_ge(b_v, 14)
                    for t in range(4):
                        ins = T_.transpose((psN, psM)[half][0:H, P * t:P * t + P], mx[:, 4 * half + t, :],
                                           ident[:, :])
                    ins.then_inc(m_T, 1)
                pe.wait_ge(m_cp, 2 * b + 2)
                pe.wait_ge(m_d[b], 16 * 6)

            def scores(n):
                b, p, u = unit_of(n)
                pair = n // NU
                if n < 2:
                    pe.wait_ge(q_n, 4)
                else:
                    pe.wait_ge(s_exp, n - 1)
                if u == 0:
                    pe.wait_ge(q_z, pair + 1)
                at = 0
                for j, i0, cnt in UNITS[u]:
                    w = cnt * P
                    for g in range(2):
                        ins = T_.matmul(psS[n % 2][:, g, at:at + w], stack[b][:, 1, p, j * P:j * P + P],
                                        qz[:, pair % 2, g, i0 * P:i0 * P + w], start=True, stop=True)
                    at += w
                ins.then_inc(s_mm, 1)

            def values(n):
                b, p, u = unit_of(n)
                pair = n // NU
                pe.wait_ge(s_exp, n + 1)
                if DIAG[u] is not None:
                    pe.wait_ge(s_mask, masked_before(n) + 1)
                if u == 0:
                    pe.wait_ge(v_cp, 2)
                    if b:
                        pe.wait_ge(b_v, 8)
                    pe.wait_ge(v_set, 1)
                    if pair >= 2:
                        pe.wait_ge(o_cp, pair - 1)
                at = 0
                for j, i0, cnt in UNITS[u]:
                    for par in range(2):
                        tiles = [i for i in range(i0, i0 + cnt) if i % 2 == par]
                        if not tiles:
                            continue
                        k = len(tiles)
                        for g in range(2):
                            r0 = 64 * par + 32 * g
                            src = pbuf[n % NPB][:, g, :].rearrange("p (t c) -> p t c", c=P)
                            a0 = at // P + tiles[0] - i0
                            dst = psO[pair % 2][r0:r0 + HD + 1, tiles[0] // 2 * P:(tiles[0] // 2 + k) * P]
                            ins = T_.matmul(dst, v9[:, b * NT + j, 2 * p + g, :],
                                            src[:, a0:a0 + 2 * k - 1:2, :],
                                            start=(u == 0), stop=(u == NU - 1), skip_group_check=True,
                                            tile_position=(0, r0))
                    at += cnt * P
                ins.then_inc(s_pv, 1)

            def to_tokens(n):
                pe.wait_ge(o_cp, n + 1)
                if n == 0:
                    pe.wait_ge(q_f, 4)
                else:
                    pe.wait_ge(o_n, n)
                for i in range(4):
                    ins = T_.transpose(psN[:, P * i:P * i + P], ots[:, n % 2, P * i:P * i + P], ident[:, :])
                ins.then_inc(o_mm, 1)

            def router(b, step):
                tv, tp = t_v[b], t_pe[b]
                half = step % 2
                two = b == B - 1
                if step == 0:
                    pe.wait_ge(o_n, NP * (b + 1))
                    if b:
                        pe.wait_ge(t_v[b - 1], 10)
                    else:
                        pe.wait_ge(b_v, 14)
                elif step < 4:
                    if two and step > 1:
                        pe.wait_ge(tv, step - 1)
                    elif not two:
                        pe.wait_ge(tv, step)
                elif step < 6:
                    pe.wait_ge(tv, 5 if two or step == 4 else 6)
                else:
                    pe.wait_ge(tv, 7 if step == 6 else 9)
                if step in (0, 1, 4, 5):
                    src = attn if step < 2 else h2
                    for t in range(4):
                        ins = T_.transpose(bank(b, half)[:, P * t:P * t + P], src[:, 4 * half + t, 0:D], ident[:, :])
                if step in (2, 3):
                    pe.wait_ge(c_modc, 2)
                    for t in range(4):
                        at = (4 * half + t) * P
                        ins = T_.matmul(bank(b, half)[:, P * t:P * t + P], attnT[:, at:at + P], wog[:, b, :],
                                        start=True, stop=True)
                if step == 6:
                    for t in range(NT):
                        ins = T_.matmul(psM[:, E * t:E * t + E], h2T[:, P * t:P * t + P], rw[:, :],
                                        start=True, stop=True)
                if step == 7:
                    pe.wait_ge(v_set, 2)
                    counts = psM[:, 64:64 + NT * E]
                    T_.matmul(counts, upper[:, :], oh[:, b, :, :].rearrange("p t e -> p (t e)"),
                              start=True, stop=False, skip_group_check=True)
                    if b:
                        T_.matmul(counts, onesb[:, :],
                                  ohsum[:, :].rearrange("p (o e) -> p o e", o=1).to_broadcast([P, NT, E]),
                                  start=False, stop=False, skip_group_check=True)
                    for t in range(NT - 1):
                        n = NT - t - 1
                        ins = T_.matmul(psM[:, 64 + E * (t + 1):64 + NT * E], onesb[:, :],
                                        oh[:, b, t:t + 1, :].to_broadcast([P, n, E]), start=False,
                                        stop=t == NT - 2, skip_group_check=True)
                ins.then_inc(tp, 1)

            pe.wait_ge(c_fl, 1)
            general = read_flag(pe)
            with pe.If(general != 0):
                maxima(0)
            total = B * NP * NU
            scores(0)
            for n in range(total):
                pair, u = divmod(n, NU)
                if n + 1 == NP * NU:
                    with pe.If(general != 0):
                        maxima(1)
                if n + 1 < total:
                    scores(n + 1)
                values(n)
                kind, k = SIDE.get((pair, u), (None, 0))
                if kind == "prepare":
                    prepare(k)
                if kind == "router":
                    router(0, k)
                if u == 4 and pair:
                    to_tokens(pair - 1)
            to_tokens(B * NP - 1)
            for step in range(8):
                router(B - 1, step)

            def rows_T(e):
                pe.wait_ge(x_d[e], 16)
                if e < 2:
                    pe.wait_ge(o_cp, B * NP)
                else:
                    pe.wait_ge(x_cp, e - 1)
                for t in range(SPE):
                    ins = T_.transpose(psO[e % 2][:, P * t:P * t + P], xe[:, e, t, 0:D], ident[:, :])
                ins.then_inc(x_T, 1)

            def hidden(e):
                pe.wait_ge(x_cp, e + 1)
                if e < 2:
                    pe.wait_ge(s_exp, total)
                else:
                    pe.wait_ge(h_a, e - 1)
                    pe.wait_ge(h_v, e - 1)
                w1v = w1s[:, e, :].rearrange("d (p c) -> d c p", c=FC)
                for f in range(FC):
                    ins = T_.matmul(psS[e % 2][:, f // 2, CAP * (f % 2):CAP * (f % 2) + CAP], w1v[:, f, :],
                                    xeT[:, e % 2, :], start=True, stop=True)
                    if f % 2:
                        ins.then_inc(h_mm, 1)

            def outputs(e):
                pe.wait_ge(h_a, e + 1)
                pe.wait_ge(h_v, e + 1)
                if e < 2:
                    pe.wait_ge(t_v[B - 1], 10)
                else:
                    pe.wait_ge(y_cp, e - 1)
                dst = (psN, psM)[e % 2]
                for t in range(SPE):
                    for f in range(FC):
                        ins = T_.matmul(dst[:, D * t:D * t + D], hid[:, e % 2, f, P * t:P * t + P],
                                        w2s[:, e, D * f:D * f + D], start=(f == 0), stop=(f == FC - 1))
                ins.then_inc(y_mm, 1)

            rows_T(0)
            pe.wait_ge(l_ffn, 32)
            for e in range(E):
                if e + 1 < E:
                    rows_T(e + 1)
                hidden(e)
                if e >= 1:
                    outputs(e - 1)
            outputs(E - 1)


_INS = ["L0_attn_x", "L0_attn_Wk", "L0_attn_Wq", "L0_attn_Wv", "L0_attn_Wo", "L0_attn_bo", "L0_attn_kln_w",
        "L0_attn_kln_b", "L0_attn_qln_w", "L0_attn_qln_b", "L0_ffn_router_w", "L0_ffn_w1", "L0_ffn_b1",
        "L0_ffn_w2", "L0_ffn_b2", "L0_c", "L0_wmod"]


def kernel(**inputs):
    import numpy as _np
    import concourse.bacc as _bacc
    from concourse import mybir as _mybir
    from concourse.bass_utils import run_bass_kernel_spmd as _run

    nc = _bacc.Bacc("TRN2", target_bir_lowering=False, num_devices=1)
    arrays, args = {}, []
    for name in _INS:
        a = _np.ascontiguousarray(inputs[name])
        arrays[f"in_{name}"] = a
        args.append(nc.dram_tensor(f"in_{name}", a.shape, _mybir.dt.from_np(a.dtype), kind="ExternalInput").ap())
    shape = inputs["L0_attn_x"].shape
    args.append(nc.dram_tensor("out_0", shape, _mybir.dt.float32, kind="ExternalOutput").ap())
    adaln_block(nc, *args)
    r = _run(nc, [arrays], core_ids=[0])
    return r.results[0]["out_0"]
```

```python
from contextlib import ExitStack

import concourse.bass as bass
from concourse import mybir

F32 = mybir.dt.float32
BF16 = mybir.dt.bfloat16
I32 = mybir.dt.int32
U32 = mybir.dt.uint32
ALU = mybir.AluOpType
ACT = mybir.ActivationFunctionType
AX = mybir.AxisListType

P = 128
EPS = 1e-5
NEG = -1e30
FAR = 1e6
Q_PART = [0, 0, 1, 0, 2, 1]
K_PART = [0, 1, 0, 2, 0, 1]
TERMS = len(Q_PART)
SAFE = 64.0
BF16_ONES = 1.0 + 0x3F80 / 2.0 ** 23


def adaln_block(nc, x, Wk, Wq, Wv, Wo, bo, kln_w, kln_b, qln_w, qln_b,
                router_w, w1, b1, w2, b2, c, wmod, out):
    B, T, D = x.shape
    HD = kln_w.shape[0]
    H = D // HD
    E = router_w.shape[1]
    F = w1.shape[2]
    FC = F // P
    NT = T // P
    TT = B * NT
    CAP = B * T // E
    NS = E * CAP
    SPE = CAP // P
    NP = H // 2
    SCALE = 1.0 / float(HD) ** 0.5
    XW = D + 4
    assert D == P and HD == 8 and E == 8 and NT == 8 and T * 4 == 8 * 512
    KM = 2 * TERMS * HD
    ON_POOL = (Q_PART.count(2) + K_PART.count(2))
    STACK_DMAS = [2 * TERMS - ON_POOL, 2 * TERMS]

    ALL_QUERIES = [[(0, 0, 4)], [(0, 4, 4)], [(1, 1, 3), (3, 3, 1)], [(1, 4, 4)],
                   [(2, 2, 2), (6, 6, 2)], [(2, 4, 4)], [(3, 4, 4)], [(4, 4, 4)], [(5, 5, 3), (7, 7, 1)]]
    FIRST_HALF = [[(0, 0, 4)], [(1, 1, 3), (3, 3, 1)], [(2, 2, 2)]]
    SECOND_HALF = [[(0, 4, 4)], [(1, 4, 4)], [(2, 4, 4)], [(3, 4, 4)], [(4, 4, 4)], [(5, 5, 3), (7, 7, 1)],
                   [(6, 6, 2)]]
    ROUNDS = ([(0, p, ALL_QUERIES, 0, NT) for p in range(NP)]
              + [(1, p, FIRST_HALF, 0, NT // 2) for p in range(NP)]
              + [(1, p, SECOND_HALF, NT // 2, NT // 2) for p in range(NP)])
    NR = len(ROUNDS)
    NU = [len(r[2]) for r in ROUNDS]
    FIRST = [sum(NU[:r]) for r in range(NR + 1)]
    WHERE = [(r, u) for r in range(NR) for u in range(NU[r])]
    TOTAL = len(WHERE)
    TOKEN_UNIT = {9: 4, 3: 1, 7: 5}

    def masked(n):
        r, u = WHERE[n]
        return any(j == i0 for j, i0, _ in ROUNDS[r][2][u])

    def width(n):
        r, u = WHERE[n]
        return sum(count for _, _, count in ROUNDS[r][2][u]) * P

    STAGES = TT // 4
    STEPS = ["turn", "project", "modulate", "turn_h", "logits", "counts"]
    ORDER = [(0, "turn"), (1, "turn"), (0, "project"), (0, "modulate"), (0, "turn_h"), (0, "logits"),
             (0, "counts"), (1, "project"), (1, "modulate"), (1, "turn_h"), (1, "logits"), (1, "counts"),
             (2, "turn"), (2, "project"), (2, "modulate"), (2, "turn_h"), (2, "logits"), (2, "counts")]
    ORDER += [(3, step) for step in STEPS]
    ON_PE = [step for step in ORDER if step[1] != "modulate"]
    SIDE = {(0, 2): ("parts", 0), (0, 6): ("parts", 1), (1, 2): ("parts", 2), (1, 6): ("parts", 3),
            (2, 2): ("rows", 0), (3, 2): ("bias", 0), (3, 6): ("bias", 1)}
    for item, at in zip(ORDER, ((9, 0), (15, 0), (15, 2), (16, 0), (17, 0), (17, 2), (17, 4), (18, 0), (18, 1),
                                (19, 1), (19, 3), (19, 6), (20, 2), (20, 4), (21, 0), (21, 6), (22, 1), (22, 4))):
        SIDE[at] = item
    assert B == 2 and NT == 8 and STAGES == 4 and len(set(SIDE)) == len(SIDE)
    ROUTER_EXP = {(17, 5): 0, (20, 0): 1, (22, 5): 2}
    SCATTERS = {18: 3, 19: 1, 20: 3, 21: 1, 22: 2, 23: 2}

    UNITS = [(half, e) for half in range(SPE) for e in range(E)]
    GROUP = E // 2
    NY = 4
    assert SPE == 2
    xs_dram = nc.dram_tensor("dispatched", [NS, XW], F32, kind="Internal").ap()
    xl_dram = nc.dram_tensor("dispatched_last", [NS, XW], F32, kind="Internal").ap()
    out_rows = out.rearrange("b t d -> (b t) d")

    with ExitStack() as ctx:
        def sb(name, shape, dt=F32):
            return ctx.enter_context(nc.sbuf_tensor(name, shape, dt))

        def ps(name, shape):
            return ctx.enter_context(nc.psum_tensor(name, shape, F32))

        def sem(name):
            return ctx.enter_context(nc.semaphore(name))

        psS = [ps("psS0", [P, 2, 512]), ps("psS1", [P, 2, 512])]
        psO = [ps("psO0", [P, 512]), ps("psO1", [P, 512])]
        psN = ps("psN", [P, 512])
        psM = ps("psM", [P, 512])

        ident = sb("ident", [P, P])
        onesb = sb("onesb", [P, P], BF16)
        upper = sb("upper", [P, P], BF16)
        e8 = sb("e8", [HD, P])
        mask = sb("mask", [P, T])
        desc8 = sb("desc8", [P, NT, E])
        tokid = sb("tokid", [P, TT])
        zeros = sb("zeros", [P, XW * SPE])
        epsc = sb("epsc", [P, 1])
        warm = sb("warm", [P, 1])
        xt = sb("xt", [P, TT, D])
        wst = sb("wst", [P, 2, D])
        wmean = sb("wmean", [P, 2 * H])
        wcen = sb("wcen", [P, 2, D])
        wqk = sb("wqk", [P, 2, D])
        wv = sb("wv", [P, D])
        wo = sb("wo", [P, D])
        bob = sb("bob", [P, D])
        lnr = sb("lnr", [4, HD])
        lnb = sb("lnb", [1, 4, HD])
        crow = sb("crow", [B, D])
        wm = sb("wm", [P, 6 * D])
        rw = sb("rw", [P, E])
        b1r = sb("b1r", [E, F])
        ownr = sb("ownr", [1, 2, P])
        own = sb("own", [P, 2])
        cT = sb("cT", [P, B])
        silu = sb("silu", [P, 3, B])
        silub = sb("silub", [P, B, P])
        sT = sb("sT", [P, B])
        lnT = sb("lnT", [HD, 4])
        lncol = sb("lncol", [P, 4])
        b1c = sb("b1c", [P, FC, E])
        modc = sb("modc", [P, 2, B])
        modr = sb("modr", [P, B, 4, D])
        gsign = sb("gsign", [P, B, 2, D])
        wog = sb("wog", [P, B, D])
        bog = sb("bog", [P, B, D])
        bprod = sb("bprod", [1, 6, HD])
        bsum = sb("bsum", [1, 8])
        flag = sb("flag", [1, 1], I32)
        bst = sb("bst", [P, NT, 6])
        mv = sb("mv", [P, NT, 2])
        nw = sb("nw", [P, 4, NT])
        xn = sb("xn", [P, NT, D])
        hT = sb("hT", [P, T])
        sq = sb("sq", [P, 2, 512])
        var = sb("var", [P, 4, 64])
        std = sb("std", [P, 256])
        rstd = sb("rstd", [P, 256])
        qkn = sb("qkn", [P, NT, 2, D])
        qkf = sb("qkf", [P, 2, 512])
        res = sb("res", [P, 2, 512])
        parts = sb("parts", [P, 2, 3, T], BF16)
        stack = [sb(f"stack{b}", [P, 2, NP, T], BF16) for b in range(B)]
        qz = sb("qz", [P, 2, 2, T], BF16)
        mtmp = hT
        negm = qkf[:, :, :].rearrange("p n t -> p (n t)")[0:H, :]
        mres = res[:, :, :].rearrange("p n t -> p (n t)")[0:H, :]
        mparts = parts[:, :, :, :].rearrange("p a n t -> p (a n t)")[0:H, 0:3 * T].rearrange(
            "p (n t) -> p n t", n=3)
        v9 = sb("v9", [P, TT, H, HD + 1])
        mx = sb("mx", [P, NT, H])
        NPB = 4
        pbuf = [sb(f"pbuf{i}", [P, 2, 512]) for i in range(NPB)]
        ots = sb("ots", [P, 2, 512])
        rl = sb("rl", [P, 2, NT, 2])
        attn = sb("attn", [P, NT, D])
        attnT = sb("attnT", [P, T])
        h2 = sb("h2", [P, NT, XW])
        h2T = attnT
        rt = sb("rt", [P, 4, NT, E])
        ro = sb("ro", [P, 8, NT])
        oh = sb("oh", [P, STAGES, 4, E], BF16)
        ohs32 = sb("ohs32", [P, 3, E])
        ohsum = sb("ohsum", [P, 3, E], BF16)
        slot = sb("slot", [P, TT], U32)
        w12 = stack[0][:, :, :, :].rearrange("p a h t -> p (a h t)").bitcast(F32)
        w1s = w12[:, 0:E * F].rearrange("p (e f) -> p e f", e=E)
        w2s = w12[:, E * F:2 * E * F].rearrange("p (e f) -> p e f", e=E)
        xe = sb("xe", [P, SPE, E, XW])
        xl = stack[1][:, :, :, :].rearrange("p a h t -> p (a h t)").bitcast(F32)[:, 0:SPE * E * XW].rearrange(
            "p (s e w) -> p s e w", s=SPE, e=E)
        back = sb("back", [P, SPE, E], U32)
        none = sb("none", [P, SPE, E])
        few = sb("few", [1, 2, E])
        late = sb("late", [1, 1], I32)
        xeT = sb("xeT", [P, 2, P])
        hid = qkn[:, :, :, :].rearrange("p t a d -> p (t a d)")[:, 0:2 * FC * P].rearrange(
            "p (b f c) -> p b f c", b=2, f=FC)
        ye = sb("ye", [P, NY, D])
        yw = gsign[:, :, :, :].rearrange("p b i d -> p (b i) d")
        b2b = xn

        l_small = sem("l_small")
        l_wm = sem("l_wm")
        l_x = [sem(f"l_x{b}") for b in range(B)]
        l_qkv = sem("l_qkv")
        l_late = sem("l_late")
        l_ffn = sem("l_ffn")
        l_b2 = sem("l_b2")
        k_pool = sem("k_pool")
        c_T = sem("c_T")
        c_cp = sem("c_cp")
        c_exp = sem("c_exp")
        c_silu = sem("c_silu")
        c_mod = sem("c_mod")
        c_own = sem("c_own")
        c_modc = sem("c_modc")
        w_qk = sem("w_qk")
        v_ch = sem("v_ch")
        a_ch = sem("a_ch")
        g_ch = sem("g_ch")
        n_mv = sem("n_mv")
        n_std = sem("n_std")
        n_f = sem("n_f")
        n_a = sem("n_a")
        n_xn = sem("n_xn")
        n_T = sem("n_T")
        n_h = sem("n_h")
        q_mm = sem("q_mm")
        v_mm = sem("v_mm")
        v_cp = sem("v_cp")
        q_sq = sem("q_sq")
        q_var = sem("q_var")
        q_std = sem("q_std")
        q_n = sem("q_n")
        q_T = sem("q_T")
        q_f = sem("q_f")
        q_r = sem("q_r")
        q_2 = sem("q_2")
        q_3 = sem("q_3")
        k_st = [sem(f"k_st{b}") for b in range(B)]
        c_ep = sem("c_ep")
        c_mc = sem("c_mc")
        c_sb = sem("c_sb")
        c_mr = sem("c_mr")
        b_pe = sem("b_pe")
        b_v = sem("b_v")
        b_3 = sem("b_3")
        c_bs = sem("c_bs")
        c_bq = sem("c_bq")
        c_fl = sem("c_fl")
        m_ch = sem("m_ch")
        q_z0 = sem("q_z0")
        q_z = sem("q_z")
        st_d = [sem(f"st_d{b}") for b in range(B)]
        st_g = sem("st_g")
        v_set = sem("v_set")
        m_z = sem("m_z")
        m_mm = sem("m_mm")
        m_rd = sem("m_rd")
        m_T = sem("m_T")
        m_cp = sem("m_cp")
        m_p = sem("m_p")
        m_d = [sem(f"m_d{b}") for b in range(B)]
        s_mm = sem("s_mm")
        s_exp = sem("s_exp")
        s_mask = sem("s_mask")
        s_pv = sem("s_pv")
        o_cp = sem("o_cp")
        o_mm = sem("o_mm")
        o_n = sem("o_n")
        t_pe = sem("t_pe")
        t_v = sem("t_v")
        t_s = sem("t_s")
        t_l = sem("t_l")
        t_e = sem("t_e")
        z_d = sem("z_d")
        d_d = [sem(f"d_d{r}") for r in range(STAGES)]
        x_d = [sem(f"x_d{i}") for i in range(2 * SPE)]
        x_l = [sem(f"x_l{i}") for i in range(2 * SPE)]
        x_s = [sem(f"x_s{i}") for i in range(SPE)]
        x_n = sem("x_n")
        c_f2 = sem("c_f2")
        x_i = sem("x_i")
        x_T = sem("x_T")
        x_cp = sem("x_cp")
        h_mm = sem("h_mm")
        h_a = sem("h_a")
        h_v = sem("h_v")
        y_mm = sem("y_mm")
        y_cp = sem("y_cp")
        y_d = [sem(f"y_d{i}") for i in range(NY)]
        w_a = sem("w_a")
        f_o = sem("f_o")

        K_POOL = 5
        block = ctx.enter_context(nc.Block())

        def read_flag(engine, word, name):
            register = engine.alloc_register(name)
            engine.reg_load(register, word[0:1, 0:1])
            return engine.snap(register)

        def stack_part(engine, b, part, placed, sides=(0, 1)):
            for a in sides:
                order = (Q_PART, K_PART)[a]
                for n in range(TERMS):
                    if order[n] == part:
                        engine.dma_start(stack[b][2 * HD * n:2 * HD * (n + 1), a, :, :],
                                         parts[:, a, part, :]).then_inc(placed, 16)

        @block.sync
        def _(sp):
            sp.dma_start(crow[:, :], c).then_inc(l_small, 16)
            sp.dma_start(xt[:, 0:NT, :], x[0].rearrange("(t p) d -> p t d", p=P)).then_inc(l_x[0], 16)
            for n, v in enumerate((qln_w, qln_b, kln_w, kln_b)):
                sp.dma_start(lnr[n:n + 1, :], v.rearrange("(a s) -> a s", a=1)).then_inc(l_small, 16)
            sp.dma_start(b1r[:, :], b1).then_inc(l_small, 16)
            sp.dma_start(wm[:, :], wmod).then_inc(l_wm, 16)
            for n, w in enumerate((Wq, Wk)):
                sp.dma_start(wst[:, n, :], w).then_inc(l_qkv, 16)
            sp.dma_start(wv[:, :], Wv).then_inc(l_qkv, 16)
            for n, v in enumerate((qln_w, qln_b, kln_w, kln_b)):
                sp.dma_start(lnb[:, n, :], v.rearrange("(a s) -> a s", a=1)).then_inc(l_late, 16)
            for b in range(1, B):
                sp.dma_start(xt[:, b * NT:(b + 1) * NT, :],
                             x[b].rearrange("(t p) d -> p t d", p=P)).then_inc(l_x[b], 16)
            sp.dma_start(wo[:, :], Wo).then_inc(l_late, 16)
            sp.dma_start(bob[:, :], bo.partition_broadcast(P)).then_inc(l_late, 16)
            sp.dma_start(rw[:, :], router_w).then_inc(l_late, 16)

            def stack_shift(b):
                sp.wait_ge(m_p, 3 * (b + 1))
                for n in range(3):
                    at = KM + 2 * n
                    sp.dma_start(stack[b][at:at + 2, 0, :, :], mparts[:, n, :]).then_inc(m_d[b], 16)

            sp.wait_ge(k_st[0], 1)
            sp.wait_ge(q_r, 3)
            stack_part(sp, 0, 0, st_d[0], sides=(0,))
            sp.wait_ge(q_r, 4)
            stack_part(sp, 0, 0, st_d[0], sides=(1,))
            sp.wait_ge(q_2, 4)
            stack_part(sp, 0, 1, st_d[0])
            sp.wait_ge(k_pool, K_POOL)
            for e in range(E):
                for rows in (xs_dram, xl_dram):
                    sp.dma_start(rows[e * CAP:(e + 1) * CAP, :].rearrange("(p t) w -> p (t w)", p=P),
                                 zeros[:, :]).then_inc(z_d, 16)
            sp.wait_ge(c_fl, 1)
            general = read_flag(sp, flag, "general")
            with sp.If(general != 0):
                stack_shift(0)
            sp.wait_ge(n_T, 4)
            sp.dma_start(b2b[:, :, :].rearrange("p e d -> p (e d)"),
                         b2.rearrange("e d -> (e d)").partition_broadcast(P)).then_inc(l_b2, 16)
            sp.wait_ge(k_st[1], 1)
            sp.wait_ge(b_3, 4)
            for part in range(3):
                stack_part(sp, 1, part, st_d[1])
            with sp.If(general != 0):
                stack_shift(1)
            sp.wait_ge(s_mm, FIRST[NP])
            sp.dma_start(w1s[:, :, :], w1.rearrange("e d f -> d e f")).then_inc(l_ffn, 16)
            sp.dma_start(w2s[:, :, :], w2.rearrange("e (p c) d -> p e (c d)", c=FC)).then_inc(l_ffn, 16)

            def write_result(r):
                sp.wait_ge(t_v, ORDER.index((r, "project")) + 1)
                b, t0 = divmod(4 * r, NT)
                sp.dma_start(out[b].rearrange("(t p) d -> p t d", p=P)[:, t0:t0 + 4, :],
                             xt[:, 4 * r:4 * r + 4, :]).then_inc(f_o, 16)

            def read_rows(rows, into, half, done):
                for g in range(2):
                    experts = slice(GROUP * g, GROUP * (g + 1))
                    sp.dma_start(into[:, half, experts, :], rows.rearrange(
                        "(e s p) w -> p s e w", s=SPE, p=P)[:, half, experts, :]).then_inc(done[2 * half + g], 16)

            for r in range(STAGES - 1):
                write_result(r)
            for r in range(STAGES - 1):
                sp.wait_ge(d_d[r], 16 * 4)
            for half in range(SPE):
                read_rows(xs_dram, xe, half, x_d)
            sp.wait_ge(s_mm, TOTAL)
            sp.wait_ge(q_z, NR)
            sp.wait_ge(c_f2, 1)
            wait_for_last = read_flag(sp, late, "late")
            write_result(STAGES - 1)
            with sp.If(wait_for_last != 0):
                sp.wait_ge(d_d[STAGES - 1], 16 * 4)
                read_rows(xl_dram, xl, 0, x_l)
            sp.wait_ge(d_d[STAGES - 1], 16 * 4)
            read_rows(xl_dram, xl, 1, x_l)
            for i in range(NY):
                sp.wait_ge(y_d[i], 16 * len(UNITS) // NY)

        @block.gpsimd
        def _(pool):
            chain = [0]

            def link(ins):
                chain[0] += 1
                ins.then_inc(g_ch, 1)
                pool.wait_ge(g_ch, chain[0])

            def fill_stack(b):
                for a, value in enumerate((0.0, BF16_ONES)):
                    ins = nc.gpsimd.memset(stack[b][:, a, :, :].rearrange("p h t -> p (h t)").bitcast(F32), value)
                ins.then_inc(k_st[b], 1)

            link(nc.gpsimd.memset(ident[:, :], 0.0))
            nc.gpsimd.affine_select(out=ident[:, :], in_=ident[:, :], compare_op=ALU.not_equal, fill=1.0, base=0,
                                    pattern=[[-1, P]], channel_multiplier=1).then_inc(k_pool, 1)
            link(nc.gpsimd.memset(e8[:, :], 0.0))
            nc.gpsimd.affine_select(out=e8[:, :].rearrange("k (g s p) -> k g s p", g=2, s=HD),
                                    in_=e8[:, :].rearrange("k (g s p) -> k g s p", g=2, s=HD),
                                    compare_op=ALU.not_equal, fill=1.0, base=0,
                                    pattern=[[0, 2], [-1, HD], [0, NP]],
                                    channel_multiplier=1).then_inc(k_pool, 1)
            link(nc.gpsimd.memset(ownr[:, :, :], 0.0))
            for g in range(2):
                nc.gpsimd.memset(ownr[:, g, 0:KM].rearrange("o (n a s) -> o n a s", a=2, s=HD)[:, :, g, :], 1.0)
                ins = nc.gpsimd.memset(ownr[:, g, KM:P].rearrange("o (n a) -> o n a", a=2)[:, :, g:g + 1], 1.0)
            ins.then_inc(k_pool, 1)
            nc.gpsimd.memset(zeros[:, :], 0.0).then_inc(k_pool, 1)
            nc.gpsimd.memset(onesb[:, :], 1.0).then_inc(k_pool, 1)
            fill_stack(0)
            nc.gpsimd.memset(v9[:, :, :, HD:HD + 1], 1.0).then_inc(v_set, 1)
            pool.wait_ge(k_pool, K_POOL)
            nc.gpsimd.affine_select(out=upper[:, :], in_=onesb[:, 0:P], compare_op=ALU.is_ge, fill=0.0, base=0,
                                    pattern=[[1, P]], channel_multiplier=-1).then_inc(v_set, 1)
            link(nc.gpsimd.memset(mask[:, :], 0.0))
            nc.gpsimd.affine_select(out=mask[:, T - P:T], in_=mask[:, T - P:T], compare_op=ALU.is_ge, fill=NEG,
                                    base=0, pattern=[[-1, P]], channel_multiplier=1).then_inc(v_set, 1)
            nc.gpsimd.iota(desc8[:, :, :], pattern=[[0, NT], [-1, E]], base=E, channel_multiplier=0,
                           allow_small_or_imprecise_dtypes=True).then_inc(v_set, 1)
            nc.gpsimd.iota(tokid[:, :], pattern=[[P, TT]], base=0, channel_multiplier=1,
                           allow_small_or_imprecise_dtypes=True).then_inc(v_set, 1)

            def third_parts():
                for n in range(4):
                    half, a = divmod(n, 2)
                    pool.wait_ge(q_2, n + 1)
                    nc.gpsimd.tensor_tensor(parts[:, a, 2, 512 * half:512 * half + 512], res[:, n % 2, :],
                                            parts[:, a, 1, 512 * half:512 * half + 512],
                                            ALU.subtract).then_inc(q_3, 1)

            def scatter(t):
                stage = t // 4
                if t % 4 == 0:
                    pool.wait_ge(t_v, ORDER.index((stage, "counts")) + 1)
                nc.gpsimd.indirect_dma_start(
                    out=(xl_dram if stage == STAGES - 1 else xs_dram)[:, :],
                    out_offset=bass.IndirectOffsetOnAxis(ap=slot[:, t:t + 1], axis=0),
                    in_=h2[:, t % NT, :], in_offset=None, bounds_check=NS - 1,
                    oob_is_err=False).then_inc(d_d[stage], 16)

            def mask_units():
                sent = 0
                for n in range(TOTAL):
                    r, u = WHERE[n]
                    if masked(n):
                        pool.wait_ge(s_exp, n + 1)
                        at = 0
                        for j, i0, count in ROUNDS[r][2][u]:
                            if j == i0:
                                v = pbuf[n % NPB][:, :, at:at + P]
                                ins = nc.gpsimd.affine_select(
                                    out=v, in_=v, compare_op=ALU.is_ge, fill=0.0, base=0,
                                    pattern=[[0, 2], [1, P]], channel_multiplier=-1)
                            at += count * P
                        ins.then_inc(s_mask, 1)
                    if u == NU[r] - 1 and r in SCATTERS:
                        if sent == 0:
                            pool.wait_ge(z_d, 16 * 2 * E)
                        for t in range(sent, sent + SCATTERS[r]):
                            scatter(t)
                        sent += SCATTERS[r]
                return sent

            fill_stack(1)
            third_parts()
            pool.wait_ge(q_3, 4)
            stack_part(pool, 0, 2, st_g)
            for t in range(mask_units(), TT):
                scatter(t)
            pool.wait_ge(f_o, 16 * STAGES)
            for n, (half, e) in enumerate(UNITS):
                pool.wait_ge(x_i, n // GROUP + 1)
                pool.wait_ge(y_cp, n + 1)
                nc.gpsimd.indirect_dma_start(
                    out=out_rows, out_offset=bass.IndirectOffsetOnAxis(
                        ap=back[:, half, e:e + 1], axis=0),
                    in_=ye[:, n % NY, :], in_offset=None, bounds_check=B * T - 1,
                    oob_is_err=False, compute_op=ALU.add).then_inc(y_d[n % NY], 16)

        @block.scalar
        def _(act):
            act.wait_ge(c_cp, 1)
            nc.scalar.activation(silu[:, 0, :], cT[:, :], ACT.Exp, scale=-1.0).then_inc(c_exp, 1)

            def token_std(count, tiles):
                act.wait_ge(n_mv, count)
                nc.scalar.activation(nw[:, 0, tiles], mv[:, tiles, 1], ACT.Sqrt, bias=epsc[:, :]).then_inc(n_std, 1)

            act.wait_ge(c_ep, 1)
            nc.scalar.activation(warm[:, :], epsc[:, :], ACT.Sqrt).then_inc(a_ch, 1)

            def normalise(b, half):
                act.wait_ge(n_f, b + 1)
                for t in range(4 * half, 4 * half + 4):
                    ins = nc.scalar.activation(xn[:, t, :], xt[:, b * NT + t, :], ACT.Identity,
                                               bias=nw[:, 1, t:t + 1], scale=nw[:, 3, t:t + 1])
                ins.then_inc(n_a, 1)

            token_std(1, slice(0, NT))
            normalise(0, 1)
            act.wait_ge(c_modc, 1)

            def router_exp(stage):
                act.wait_ge(t_l, stage + 1)
                tiles = slice(4 * (stage % 2), 4 * (stage % 2) + 4)
                nc.scalar.activation(rt[:, 1, tiles, :], rt[:, 0, tiles, :], ACT.Exp).then_inc(t_e, 1)

            def modulate(b, half, src):
                act.wait_ge(n_T, 2 * b + half + 1)
                if b:
                    act.wait_ge(q_mm, 4)
                    act.wait_ge(v_mm, 2)
                nc.scalar.activation(hT[:, 512 * half:512 * half + 512], src[:, :], ACT.Identity,
                                     bias=modc[:, 0, b:b + 1], scale=modc[:, 1, b:b + 1]).then_inc(n_h, 1)

            def squares(b):
                for n in range(4):
                    act.wait_ge(q_mm, 4 * b + n + 1)
                    if 4 * b + n >= 2:
                        act.wait_ge(q_var, 4 * b + n - 1)
                    nc.scalar.activation(sq[:, n % 2, :], psS[n // 2][:, n % 2, :],
                                         ACT.Square).then_inc(q_sq, 1)
                for half in range(2):
                    act.wait_ge(q_var, 4 * b + 2 * half + 2)
                    if half == 0:
                        act.wait_ge(c_ep, 1)
                        if b:
                            act.wait_ge(q_n, 4)
                    nc.scalar.activation(std[:, 128 * half:128 * half + 128],
                                         var[:, 2 * half:2 * half + 2, :].rearrange("p a c -> p (a c)"), ACT.Sqrt,
                                         bias=epsc[:, :], scale=1.0 / HD).then_inc(q_std, 1)

            def copy_v(b, src):
                for n in range(2):
                    act.wait_ge(v_mm, 2 * b + n + 1)
                    t0 = b * NT + 4 * n
                    nc.scalar.activation(v9[:, t0:t0 + 4, :, 0:HD],
                                         src[n][:, :].rearrange("p (t h s) -> p t h s", t=4, h=H),
                                         ACT.Copy).then_inc(v_cp, 1)

            def second(n):
                half, a = divmod(n, 2)
                act.wait_ge(q_r, n + 1)
                nc.scalar.activation(parts[:, a, 1, 512 * half:512 * half + 512], res[:, n % 2, :],
                                     ACT.Copy).then_inc(q_2, 1)

            for half in range(2):
                modulate(0, half, (psN, psM)[half])
            token_std(2, slice(0, NT))
            squares(0)
            copy_v(0, psO)
            act.wait_ge(n_T, 2)
            normalise(1, 0)
            normalise(1, 1)
            for n in range(4):
                act.wait_ge(q_T, n + 1)
                if n >= 2:
                    act.wait_ge(q_r, n - 1)
                a = n % 2
                nc.scalar.activation(qkf[:, n % 2, :], (psN, psM)[n % 2][:, :], ACT.Identity,
                                     bias=lncol[:, 2 * a + 1:2 * a + 2],
                                     scale=lncol[:, 2 * a:2 * a + 1]).then_inc(q_f, 1)
                if n >= 1:
                    second(n - 1)
                if n == 3:
                    modulate(1, 0, psO[0])
            second(3)
            modulate(1, 1, psO[1])
            act.wait_ge(c_bs, 1)
            nc.scalar.activation(bsum[:, 4:6], bsum[:, 2:4], ACT.Sqrt).then_inc(c_bq, 1)
            squares(1)
            copy_v(1, (psN, psM))
            act.wait_ge(a_ch, 1)
            nc.scalar.activation(warm[:, :], epsc[:, :], ACT.Exp).then_inc(a_ch, 1)

            for n in range(TOTAL):
                w = width(n)
                if n < B:
                    act.wait_ge(c_mr, n + 1)
                    nc.scalar.activation(modr[:, n, :, :].rearrange("p a d -> p (a d)"), psO[n][:, :],
                                         ACT.Copy).then_inc(c_mc, 1)
                act.wait_ge(s_mm, n + 1)
                if n >= NPB:
                    act.wait_ge(s_pv, n - NPB + 1)
                nc.scalar.activation(pbuf[n % NPB][:, :, 0:w], psS[n % 2][:, :, 0:w], ACT.Exp).then_inc(s_exp, 1)
                if WHERE[n] in ROUTER_EXP:
                    router_exp(ROUTER_EXP[WHERE[n]])
            act.wait_ge(a_ch, 2)
            nc.scalar.activation(warm[:, :], epsc[:, :], ACT.Sqrt).then_inc(a_ch, 1)
            token_std(3, slice(4, NT))
            act.wait_ge(a_ch, 3)
            nc.scalar.activation(warm[:, :], epsc[:, :], ACT.Exp).then_inc(a_ch, 1)
            router_exp(STAGES - 1)
            for n, (half, e) in enumerate(UNITS):
                act.wait_ge(x_i, n // GROUP + 1)
                if n >= NY:
                    act.wait_ge(y_cp, n - NY + 1)
                nc.scalar.activation(yw[:, n % NY, :], modr[:, 0, 3, :], ACT.Copy,
                                     scale=xe[:, half, e, D + 1:D + 2]).then_inc(w_a, 1)
                act.wait_ge(h_mm, 2 * n + 1)
                if n >= 2:
                    act.wait_ge(y_mm, n - 1)
                for f in range(2):
                    ins = nc.scalar.activation(hid[:, n % 2, f, :], psS[n % 2][:, 0, P * f:P * f + P], ACT.Relu,
                                               bias=b1c[:, f, e:e + 1])
                ins.then_inc(h_a, 1)

        @block.vector
        def _(dve):
            chain = [0]
            V = nc.vector

            def link(ins):
                chain[0] += 1
                ins.then_inc(v_ch, 1)
                dve.wait_ge(v_ch, chain[0])

            def rsqrt(v, scale, a, y, t, r):
                link(V.tensor_scalar(a, v, scale, EPS, ALU.mult, ALU.add))
                link(V.tensor_scalar(t.bitcast(I32), a.bitcast(I32), 1, None, ALU.arith_shift_right))
                link(V.tensor_scalar(y.bitcast(I32), t.bitcast(I32), -1.0, float(0x5f3759df), ALU.mult, ALU.add))
                for i in range(3):
                    link(V.tensor_tensor(t, y, y, ALU.mult))
                    link(V.scalar_tensor_tensor(out=t, in0=a, scalar=-0.5, in1=t, op0=ALU.mult, op1=ALU.mult))
                    link(V.scalar_tensor_tensor(out=(r if i == 2 else y), in0=t, scalar=1.5, in1=y,
                                                op0=ALU.add, op1=ALU.mult))

            def tile_stats(src, tiles):
                for t in tiles:
                    ins = V.bn_stats(bst[:, t, :], src(t))
                link(ins)

            def tile_moments(tiles):
                for t in tiles:
                    ins = V.bn_aggr(mv[:, t, :], bst[:, t, :])
                return ins

            def tile_rstd(tiles, count):
                tile_moments(tiles).then_inc(n_mv, 1)
                dve.wait_ge(n_std, count)
                link(V.reciprocal(nw[:, 3, tiles.start:tiles.stop], nw[:, 0, tiles.start:tiles.stop]))

            def tile_rsqrt(t0, t1):
                link(tile_moments(range(t0, t1)))
                rsqrt(mv[:, t0:t1, 1], 1.0, *(nw[:, i, t0:t1] for i in range(4)))

            def offsets():
                V.scalar_tensor_tensor(out=nw[:, 1, :], in0=mv[:, :, 0], scalar=-1.0, in1=nw[:, 3, :],
                                       op0=ALU.mult, op1=ALU.mult).then_inc(n_f, 1)

            V.memset(epsc[:, :], EPS).then_inc(c_ep, 1)
            for b in range(2):
                V.memset(psO[b][:, :], 0.0)
            dve.wait_ge(c_T, 1)
            V.tensor_copy(cT[:, :], psM[:, 0:B]).then_inc(c_cp, 1)
            V.tensor_copy(lnT[:, :], psM[0:HD, 4:8])
            V.tensor_copy(b1c[:, :, :].rearrange("p c e -> p (c e)"), psM[:, 32:32 + FC * E]).then_inc(c_cp, 1)
            dve.wait_ge(l_x[0], 16)
            tile_stats(lambda t: xt[:, t, :], range(NT))
            dve.wait_ge(c_exp, 1)
            link(V.tensor_scalar(silu[:, 1, :], silu[:, 0, :], 1.0, None, ALU.add))
            link(V.reciprocal(silu[:, 2, :], silu[:, 1, :]))
            V.tensor_tensor(sT[:, :], cT[:, :], silu[:, 2, :], ALU.mult).then_inc(c_silu, 1)
            tile_rstd(range(NT), 1)
            offsets()
            for t in range(4):
                ins = V.tensor_scalar(xn[:, t, :], xt[:, t, :], mv[:, t, 0:1], nw[:, 3, t:t + 1],
                                      ALU.subtract, ALU.mult)
            ins.then_inc(n_xn, 1)
            dve.wait_ge(c_mod, 1)
            V.tensor_copy(modc[:, 0, :], psM[:, 64:64 + B])
            V.tensor_scalar(modc[:, 1, :], psM[:, 64 + B:64 + 2 * B], 1.0, None, ALU.add)
            V.tensor_scalar(lncol[:, 0:2], psM[:, 72:74], SCALE, None, ALU.mult)
            V.tensor_copy(lncol[:, 2:4], psM[:, 74:76]).then_inc(c_modc, 1)
            V.tensor_copy(own[:, :], psM[:, 76:78]).then_inc(c_own, 1)
            dve.wait_ge(l_qkv, 48)
            link(V.tensor_reduce(wmean[:, :], wst[:, :, :].rearrange("p a (h s) -> p (a h) s", s=HD), AX.X, ALU.add))
            link(V.scalar_tensor_tensor(
                out=wcen[:, :, :].rearrange("p a (h s) -> p (a h) s", s=HD),
                in0=wmean[:, :].rearrange("p (h o) -> p h o", o=1).to_broadcast([P, 2 * H, HD]),
                scalar=-1.0 / HD, in1=wst[:, :, :].rearrange("p a (h s) -> p (a h) s", s=HD),
                op0=ALU.mult, op1=ALU.add))
            for a in range(2):
                ins = V.tensor_copy(wqk[:, a, :].rearrange("k (g s p) -> k g s p", g=2, s=HD),
                                    wcen[:, a, :].rearrange("k (p g s) -> k g s p", g=2, s=HD))
            ins.then_inc(w_qk, 1)
            dve.wait_ge(l_x[1], 16)
            dve.wait_ge(n_xn, 1)
            dve.wait_ge(n_a, 1)
            tile_stats(lambda t: xt[:, NT + t, :], range(NT))
            tile_moments(range(NT)).then_inc(n_mv, 1)
            dve.wait_ge(n_std, 2)
            link(V.reciprocal(nw[:, 3, :], nw[:, 0, :]))
            offsets()

            def sums(b):
                for n in range(4):
                    dve.wait_ge(q_sq, 4 * b + n + 1)
                    V.tensor_reduce(var[:, n, :].rearrange("p (c h) -> p c h", h=NP),
                                    sq[:, n % 2, :].rearrange("p (c s h) -> p c h s", s=HD, h=NP),
                                    AX.X, ALU.add).then_inc(q_var, 1)

            def rstds(b, half):
                dve.wait_ge(q_std, 2 * b + half + 1)
                cols = slice(128 * half, 128 * half + 128)
                link(V.reciprocal(rstd[:, cols], std[:, cols]))

            def scaled(n, src):
                V.tensor_tensor(
                    qkn[:, 2 * n:2 * n + 2, :, :].rearrange("p t a (g s h) -> p (t a g) s h", g=2, s=HD),
                    src.rearrange("p (c s h) -> p c s h", s=HD, h=NP),
                    rstd[:, 64 * n:64 * n + 64].rearrange("p (c o h) -> p c o h", o=1, h=NP).to_broadcast(
                        [P, 8, HD, NP]), ALU.mult).then_inc(q_n, 1)

            sums(0)
            for half in range(2):
                rstds(0, half)
                for n in range(2 * half, 2 * half + 2):
                    scaled(n, psS[n // 2][:, n % 2, :])
            for n in range(4):
                half, a = divmod(n, 2)
                dve.wait_ge(q_f, n + 1)
                first = parts[:, a, 0, 512 * half:512 * half + 512]
                link(V.tensor_copy(first, qkf[:, n % 2, :]))
                if n >= 2:
                    dve.wait_ge(q_3, n - 1)
                V.tensor_tensor(res[:, n % 2, :], qkf[:, n % 2, :], first, ALU.subtract).then_inc(q_r, 1)
            dve.wait_ge(l_late, 16 * 7)
            V.tensor_tensor(bprod[:, 0, :], lnb[:, 0, :], lnb[:, 2, :], ALU.mult)
            V.tensor_tensor(bprod[:, 1, :], lnb[:, 1, :], lnb[:, 3, :], ALU.mult)
            V.tensor_tensor(bprod[:, 2, :], lnb[:, 1, :], lnb[:, 2, :], ALU.mult)
            link(V.tensor_tensor(bprod[:, 3, :], lnb[:, 0, :], lnb[:, 3, :], ALU.mult))
            V.tensor_tensor(bprod[:, 4, :], bprod[:, 2, :], bprod[:, 2, :], ALU.mult)
            V.tensor_tensor(bprod[:, 5, :], bprod[:, 3, :], bprod[:, 3, :], ALU.mult)
            link(V.scalar_tensor_tensor(out=bprod[:, 0, :], in0=bprod[:, 0, :], scalar=-1.0,
                                        in1=bprod[:, 0, :], op0=ALU.mult, op1=ALU.max))
            V.tensor_reduce(bsum[:, 0:1], bprod[:, 0, :], AX.X, ALU.max)
            link(V.tensor_reduce(bsum[:, 1:2], bprod[:, 1, :], AX.X, ALU.add))
            V.tensor_reduce(bsum[:, 2:4], bprod[:, 4:6, :], AX.X, ALU.add).then_inc(c_bs, 1)
            link(V.scalar_tensor_tensor(out=bsum[:, 1:2], in0=bsum[:, 1:2], scalar=-1.0, in1=bsum[:, 1:2],
                                        op0=ALU.mult, op1=ALU.max))
            link(V.tensor_scalar(bsum[:, 1:2], bsum[:, 1:2], SCALE, None, ALU.mult))
            link(V.scalar_tensor_tensor(out=bsum[:, 0:1], in0=bsum[:, 0:1], scalar=1.0 / SCALE, in1=bsum[:, 1:2],
                                        op0=ALU.mult, op1=ALU.add))

            dve.wait_ge(c_bq, 1)
            link(V.tensor_reduce(bsum[:, 6:7], bsum[:, 4:6], AX.X, ALU.add))
            link(V.tensor_tensor(bsum[:, 7:8], bsum[:, 6:7], bsum[:, 0:1], ALU.add))
            link(V.tensor_scalar(bsum[:, 6:7], bsum[:, 7:8], SAFE, -1.0, ALU.is_le, ALU.mult))
            V.tensor_scalar(flag[:, :], bsum[:, 6:7], 1.0, None, ALU.add).then_inc(c_fl, 1)

            dve.wait_ge(c_silu, 1)
            for b in range(B):
                ins = V.tensor_copy(silub[:, b, :], sT[:, b:b + 1].to_broadcast([P, P]))
            ins.then_inc(c_sb, 1)
            def split(n):
                half, a = divmod(n, 2)
                dve.wait_ge(b_pe, n + 1)
                if n == 0:
                    dve.wait_ge(q_2, 4)
                    dve.wait_ge(q_3, 4)
                    dve.wait_ge(st_d[0], 16 * STACK_DMAS[0])
                    dve.wait_ge(st_g, 16 * ON_POOL)
                V.tensor_scalar(qkf[:, n % 2, :], psM[:, :], lncol[:, 2 * a:2 * a + 1],
                                lncol[:, 2 * a + 1:2 * a + 2], ALU.mult, ALU.add).then_inc(b_v, 1)
                dve.wait_ge(b_v, n + 1)
                first, second, third = (parts[:, a, i, 512 * half:512 * half + 512] for i in range(3))
                link(V.tensor_copy(first, qkf[:, n % 2, :]))
                link(V.tensor_tensor(res[:, n % 2, :], qkf[:, n % 2, :], first, ALU.subtract))
                link(V.tensor_copy(second, res[:, n % 2, :]))
                V.tensor_tensor(third, res[:, n % 2, :], second, ALU.subtract).then_inc(b_3, 1)

            def mod_rows():
                dve.wait_ge(c_mc, B)
                for b in range(B):
                    V.tensor_scalar(modr[:, b, 2, :], modr[:, b, 2, :], 1.0, None, ALU.add)
                    for i, a in enumerate((0, 3)):
                        ins = V.tensor_scalar(gsign[:, b, i, :], modr[:, b, a, :], 0.0, 2.0, ALU.is_ge, ALU.mult)
                link(ins)
                for b in range(B):
                    for a in (0, 3):
                        ins = V.scalar_tensor_tensor(out=modr[:, b, a, :], in0=modr[:, b, a, :], scalar=-1.0,
                                                     in1=modr[:, b, a, :], op0=ALU.mult, op1=ALU.max)
                link(ins)
                for b in range(B):
                    for a in (0, 3):
                        ins = V.tensor_scalar(modr[:, b, a, :], modr[:, b, a, :], 0.25, None, ALU.max)
                link(ins)
                for b in range(B):
                    for i, a in enumerate((0, 3)):
                        ins = V.scalar_tensor_tensor(out=modr[:, b, a, :], in0=gsign[:, b, i, :], scalar=-1.0,
                                                     in1=modr[:, b, a, :], op0=ALU.add, op1=ALU.mult)
                link(ins)
                for b in range(B):
                    V.tensor_tensor(wog[:, b, :], wo[:, :], modr[:, b, 0, :], ALU.mult)
                    ins = V.tensor_tensor(bog[:, b, :], bob[:, :], modr[:, b, 0, :], ALU.mult)
                ins.then_inc(c_modc, 1)

            def add_bias(b):
                dve.wait_ge(c_modc, 2)
                xs = xt[:, b * NT:(b + 1) * NT, :]
                link(V.tensor_tensor(xs, xs, bog[:, b:b + 1, :].to_broadcast([P, NT, D]), ALU.add))

            def own_rows(b, p, buffer, cols):
                for g in range(2):
                    ins = V.tensor_scalar(qz[:, buffer, g, cols], stack[b][:, 0, p, cols], own[:, g:g + 1], None,
                                          ALU.mult)
                return ins

            def lay_q(r):
                b, p, _, t0, count = ROUNDS[r]
                if p == 0 and t0 == 0:
                    dve.wait_ge(st_d[b], 16 * STACK_DMAS[b])
                    dve.wait_ge(st_g, 16 * ON_POOL)
                if r >= 2:
                    dve.wait_ge(s_mm, FIRST[r - 1])
                own_rows(b, p, r % 2, slice(t0 * P, (t0 + count) * P)).then_inc(q_z, 1)

            def lay_first():
                dve.wait_ge(c_own, 1)
                dve.wait_ge(st_d[0], 16 * STACK_DMAS[0])
                dve.wait_ge(st_g, 16 * ON_POOL)
                own_rows(0, 0, 0, slice(0, T // 2)).then_inc(q_z0, 1)

            m_chain = [0]

            def m_link(ins):
                m_chain[0] += 1
                ins.then_inc(m_ch, 1)
                dve.wait_ge(m_ch, m_chain[0])

            def lay_pair(b, p):
                if p == 0:
                    dve.wait_ge(st_d[b], 16 * STACK_DMAS[b])
                    dve.wait_ge(st_g, 16 * ON_POOL)
                own_rows(b, p, p % 2, slice(0, T)).then_inc(m_z, 1)

            def maxima(b):
                dve.wait_ge(v_set, 4)
                if b == 0:
                    dve.wait_ge(q_mm, 8)
                    dve.wait_ge(v_mm, 4)
                else:
                    dve.wait_ge(s_mm, FIRST[NP])
                lay_pair(b, 0)
                for h in range(H):
                    p, g = divmod(h, 2)
                    if g == 0 and p + 1 < NP:
                        lay_pair(b, p + 1)
                    for i in range(NT):
                        m = (b * H + h) * NT + i
                        w = (i + 1) * P
                        dve.wait_ge(m_mm, m + 1)
                        if m >= 1:
                            dve.wait_ge(m_rd, m)
                        V.tensor_tensor_reduce(out=mtmp[:, 0:w],
                                               in0=psS[m % 2][:, :, :].rearrange("p a c -> p (a c)")[:, 0:w],
                                               in1=mask[:, T - w:T], scale=1.0, scalar=-3e38,
                                               op0=ALU.add, op1=ALU.max,
                                               accum_out=mx[:, i, g * NP + p:g * NP + p + 1]).then_inc(m_rd, 1)
                for half in range(2):
                    dve.wait_ge(m_T, 2 * b + half + 1)
                    if b == 0:
                        dve.wait_ge(q_r, 4)
                        dve.wait_ge(q_2, 4)
                        dve.wait_ge(q_3, 4)
                    else:
                        dve.wait_ge(b_3, 4)
                    V.tensor_scalar(negm[:, 512 * half:512 * half + 512],
                                    (psN, psM)[half][0:H, :], -1.0, None, ALU.mult).then_inc(m_cp, 1)
                dve.wait_ge(m_cp, 2 * b + 2)
                dve.wait_ge(st_d[b], 16 * STACK_DMAS[b])
                dve.wait_ge(st_g, 16 * ON_POOL)
                V.tensor_copy(mparts[:, 0, :], negm[:, :]).then_inc(m_p, 1)
                dve.wait_ge(m_p, 3 * b + 1)
                m_link(V.tensor_tensor(mres[:, :], negm[:, :], mparts[:, 0, :], ALU.subtract))
                V.tensor_copy(mparts[:, 1, :], mres[:, :]).then_inc(m_p, 1)
                dve.wait_ge(m_p, 3 * b + 2)
                V.tensor_tensor(mparts[:, 2, :], mres[:, :], mparts[:, 1, :], ALU.subtract).then_inc(m_p, 1)
                dve.wait_ge(m_d[b], 16 * 3)

            def copy_sums(r):
                t0, count = ROUNDS[r][3:]
                cols = slice(t0 // 2 * P, (t0 + count) // 2 * P)
                dve.wait_ge(s_pv, FIRST[r + 1])
                if r >= 2:
                    dve.wait_ge(o_mm, r - 1)
                V.tensor_copy(ots[:, r % 2, cols], psO[r % 2][:, cols]).then_inc(o_cp, 1)

            def divide(r):
                b, p, _, t0, count = ROUNDS[r]
                dve.wait_ge(o_mm, r + 1)
                if r == NP:
                    dve.wait_ge(t_pe, 1)
                if r == 2 * NP:
                    dve.wait_ge(t_pe, 2)
                tiles = slice(t0, t0 + count)
                v = psN[:, :].rearrange("p (t g r) -> p t g r", t=NT, g=2)[:, tiles]
                link(V.reciprocal(rl[:, r % 2, tiles, :], v[:, :, :, HD]))
                V.tensor_tensor(attn[:, tiles, 2 * HD * p:2 * HD * (p + 1)].rearrange("p t (g s) -> p t g s", g=2),
                                v[:, :, :, 0:HD],
                                rl[:, r % 2, tiles, :].rearrange("p t (g o) -> p t g o", o=1).to_broadcast(
                                    [P, count, 2, HD]), ALU.mult).then_inc(o_n, 1)

            def centre(stage):
                if stage >= 2:
                    dve.wait_ge(d_d[stage - 2], 16 * 4)
                h0, t0 = 4 * (stage % 2), 4 * stage
                tiles = slice(h0, h0 + 4)
                V.memset(h2[:, tiles, D:XW], 0.0)
                for t in range(4):
                    ins = V.scalar_tensor_tensor(out=h2[:, h0 + t, 0:D], in0=xt[:, t0 + t, :],
                                                 scalar=mv[:, h0 + t, 0:1], in1=modr[:, stage // 2, 2, :],
                                                 op0=ALU.subtract, op1=ALU.mult)
                link(ins)
                V.tensor_scalar(h2[:, tiles, D], tokid[:, t0:t0 + 4], 1.0, None, ALU.add)

            def router(stage, step):
                index = ORDER.index((stage, step))
                b = stage // 2
                h0 = 4 * (stage % 2)
                t0 = 4 * stage
                tiles = slice(h0, h0 + 4)
                if step != "modulate":
                    dve.wait_ge(t_pe, ON_PE.index((stage, step)) + 1)
                if step in ("turn", "turn_h"):
                    V.tensor_copy(attnT[:, P * h0:P * h0 + 512], psM[:, :]).then_inc(t_v, 1)
                if step == "project":
                    xs = xt[:, t0:t0 + 4, :].rearrange("p t d -> p (t d)")
                    V.tensor_tensor(xs, xs, psM[:, :], ALU.add).then_inc(t_v, 1)
                    dve.wait_ge(t_v, index + 1)
                    tile_stats(lambda t: xt[:, t0 + t - h0, :], range(h0, h0 + 4))
                    if stage == STAGES - 1:
                        tile_moments(range(h0, h0 + 4)).then_inc(n_mv, 1)
                        dve.wait_ge(n_mv, 3)
                        centre(stage)
                        dve.wait_ge(n_std, 3)
                        link(V.reciprocal(nw[:, 3, tiles], nw[:, 0, tiles]))
                    else:
                        tile_rsqrt(h0, h0 + 4)
                if step == "modulate":
                    if stage < STAGES - 1:
                        centre(stage)
                    for t in range(h0, h0 + 4):
                        ins = V.scalar_tensor_tensor(out=h2[:, t, 0:D], in0=h2[:, t, 0:D],
                                                     scalar=nw[:, 3, t:t + 1], in1=modr[:, b, 1, :],
                                                     op0=ALU.mult, op1=ALU.add)
                    ins.then_inc(t_v, 1)
                if step == "logits":
                    lg = psM[:, 0:4 * E].rearrange("p (t e) -> p t e", e=E)
                    link(V.tensor_reduce(ro[:, 0, tiles], lg, AX.X, ALU.max))
                    V.tensor_tensor(rt[:, 0, tiles, :], lg,
                                    ro[:, 0, tiles].rearrange("p (t o) -> p t o", o=1).to_broadcast([P, 4, E]),
                                    ALU.subtract).then_inc(t_l, 1)
                    dve.wait_ge(t_l, stage + 1)
                    link(V.scalar_tensor_tensor(out=rt[:, 2, tiles, :], in0=rt[:, 0, tiles, :], scalar=0.0,
                                                in1=desc8[:, tiles, :], op0=ALU.is_ge, op1=ALU.mult))
                    link(V.tensor_reduce(ro[:, 1, tiles], rt[:, 2, tiles, :], AX.X, ALU.max))
                    V.tensor_tensor(oh[:, stage, :, :], desc8[:, tiles, :],
                                    ro[:, 1, tiles].rearrange("p (t o) -> p t o", o=1).to_broadcast([P, 4, E]),
                                    ALU.is_equal).then_inc(t_v, 1)
                    if stage + 1 < STAGES:
                        dve.wait_ge(t_v, index + 1)
                        link(V.tensor_reduce(ohs32[:, stage, :], oh[:, stage, :, :].rearrange("p t e -> p e t"),
                                             AX.X, ALU.add))
                        if stage:
                            link(V.tensor_tensor(ohs32[:, stage, :], ohs32[:, stage, :], ohs32[:, stage - 1, :],
                                                 ALU.add))
                        V.tensor_copy(ohsum[:, stage, :], ohs32[:, stage, :]).then_inc(t_s, 1)
                if step == "counts" and stage == STAGES - 2:
                    link(V.tensor_scalar(few[:, 0, :], psM[0:1, 128:128 + E], -1.0, None, ALU.mult))
                    link(V.tensor_reduce(few[:, 1, 0:1], few[:, 0, :], AX.X, ALU.max))
                    link(V.tensor_scalar(few[:, 1, 1:2], few[:, 1, 0:1], -float(P), -1.0, ALU.is_le, ALU.mult))
                    V.tensor_scalar(late[:, :], few[:, 1, 1:2], 1.0, None, ALU.add).then_inc(c_f2, 1)
                if step == "counts":
                    dve.wait_ge(t_e, stage + 1)
                    cnt = psM[:, 64:64 + 4 * E].rearrange("p (t e) -> p t e", e=E)
                    link(V.tensor_reduce(ro[:, 2, tiles], rt[:, 1, tiles, :], AX.X, ALU.add))
                    V.reciprocal(ro[:, 3, tiles], ro[:, 2, tiles])
                    link(V.tensor_tensor(rt[:, 3, tiles, :], cnt, oh[:, stage, :, :], ALU.mult))
                    link(V.tensor_reduce(ro[:, 4, tiles], rt[:, 3, tiles, :], AX.X, ALU.add))
                    link(V.tensor_scalar(ro[:, 5, tiles], ro[:, 4, tiles], float(CAP), None, ALU.is_le))
                    V.tensor_copy(h2[:, tiles, D + 1 + b], ro[:, 3, tiles])
                    link(V.scalar_tensor_tensor(out=ro[:, 6, tiles], in0=ro[:, 1, tiles], scalar=-float(CAP),
                                                in1=ro[:, 4, tiles], op0=ALU.mult, op1=ALU.add))
                    link(V.scalar_tensor_tensor(out=ro[:, 7, tiles], in0=ro[:, 5, tiles], scalar=-FAR,
                                                in1=ro[:, 6, tiles], op0=ALU.mult, op1=ALU.add))
                    V.tensor_scalar(slot[:, t0:t0 + 4], ro[:, 7, tiles], FAR + E * CAP - 1, None,
                                    ALU.add).then_inc(t_v, 1)

            def add_last(group):
                half, g = divmod(group, 2)
                experts = slice(GROUP * g, GROUP * (g + 1))
                dve.wait_ge(x_l[group], 16)
                V.tensor_tensor(xe[:, half, experts, :], xe[:, half, experts, :], xl[:, half, experts, :],
                                ALU.add).then_inc(x_s[half], 1)
                dve.wait_ge(x_s[half], g + 1)

            def number(group):
                half, g = divmod(group, 2)
                experts = slice(GROUP * g, GROUP * (g + 1))
                dve.wait_ge(x_d[group], 16)
                if half == 1:
                    add_last(group)
                V.tensor_scalar(none[:, half, experts], xe[:, half, experts, D], 0.0, FAR, ALU.is_le,
                                ALU.mult).then_inc(x_n, 1)
                dve.wait_ge(x_n, group + 1)
                V.scalar_tensor_tensor(out=back[:, half, experts], in0=xe[:, half, experts, D], scalar=-1.0,
                                       in1=none[:, half, experts], op0=ALU.add, op1=ALU.max).then_inc(x_i, 1)

            def take(n):
                dve.wait_ge(x_T, n + 1)
                if n >= 2:
                    dve.wait_ge(h_mm, 2 * (n - 1))
                V.tensor_copy(xeT[:, n % 2, :], psO[n % 2][:, 0:P]).then_inc(x_cp, 1)

            dve.wait_ge(c_fl, 1)
            general = read_flag(dve, flag, "general")
            sums(1)
            dve.wait_ge(q_T, 4)
            rstds(1, 0)
            for n in range(2):
                scaled(n, psS[0][:, n % 2, :])
            rstds(1, 1)
            with dve.If(general == 0):
                lay_first()
            for n in range(2, 4):
                scaled(n, psS[1][:, n % 2, :])
            with dve.If(general != 0):
                maxima(0)
                lay_first()
            own_rows(0, 0, 0, slice(T // 2, T)).then_inc(q_z, 1)
            lay_q(1)

            def side(r, units):
                for u in units:
                    kind, k = SIDE.get((r, u), (None, 0))
                    if kind == "parts":
                        split(k)
                    elif kind == "rows":
                        mod_rows()
                    elif kind == "bias":
                        add_bias(k)
                    elif kind is not None:
                        router(kind, k)

            for r in range(NR):
                moved = TOKEN_UNIT[NU[r]]
                short = NU[r] == 3
                side(r, range(moved))
                if short:
                    lay_q(r + 2)
                if r:
                    divide(r - 1)
                side(r, range(moved, NU[r]))
                if r == NP - 1:
                    with dve.If(general != 0):
                        maxima(1)
                    lay_q(NP)
                if not short and r != NP - 2 and r + 2 < NR:
                    lay_q(r + 2)
                copy_sums(r)
            divide(NR - 1)
            wait_for_last = read_flag(dve, late, "late")
            for step in STEPS:
                router(STAGES - 1, step)
                if step == "modulate":
                    with dve.If(wait_for_last == 0):
                        number(0)
                if step == "turn_h":
                    with dve.If(wait_for_last == 0):
                        take(0)
                        take(1)
            with dve.If(wait_for_last != 0):
                for group in range(2):
                    dve.wait_ge(x_d[group], 16)
                    add_last(group)
                number(0)
                take(0)
                take(1)

            def finish(n):
                half, e = UNITS[n]
                dve.wait_ge(y_mm, n + 1)
                if n == 0:
                    dve.wait_ge(l_b2, 16)
                if n >= NY:
                    dve.wait_ge(y_d[n % NY], 16 * (n // NY))
                link(V.tensor_tensor(ye[:, n % NY, :], (psN, psM)[n % 2][:, 0:D], b2b[:, e, :], ALU.add))
                V.tensor_tensor(ye[:, n % NY, :], ye[:, n % NY, :], yw[:, n % NY, :], ALU.mult).then_inc(y_cp, 1)

            def factor(n):
                half, e = UNITS[n]
                dve.wait_ge(w_a, n + 1)
                link(V.scalar_tensor_tensor(out=yw[:, n % NY, :], in0=modr[:, 1, 3, :],
                                            scalar=xe[:, half, e, D + 2:D + 3], in1=yw[:, n % NY, :],
                                            op0=ALU.mult, op1=ALU.add))

            for n, (half, e) in enumerate(UNITS):
                if n % GROUP == 1 and n // GROUP + 1 < 2 * SPE:
                    number(n // GROUP + 1)
                if 2 <= n + 1 < len(UNITS):
                    take(n + 1)
                dve.wait_ge(h_mm, 2 * n + 2)
                if n >= 2:
                    dve.wait_ge(y_mm, n - 1)
                for f in range(2, 4):
                    ins = V.tensor_scalar(hid[:, n % 2, f, :], psS[n % 2][:, 1, P * (f - 2):P * (f - 1)],
                                          b1c[:, f, e:e + 1], 0.0, ALU.add, ALU.max)
                ins.then_inc(h_v, 1)
                factor(n)
                if n >= 1:
                    finish(n - 1)
            finish(len(UNITS) - 1)

        @block.tensor
        def _(pe):
            T_ = nc.tensor
            pe.wait_ge(k_pool, K_POOL)
            pe.wait_ge(l_small, 96)
            T_.transpose(psM[:, 0:B], crow[:, :], ident[0:B, 0:B])
            T_.transpose(psM[0:HD, 4:8], lnr[:, :], ident[0:4, 0:4])
            for f in range(FC):
                ins = T_.transpose(psM[:, 32 + E * f:32 + E * f + E],
                                   b1r[:, :].rearrange("e (p c) -> e c p", c=FC)[:, f, :], ident[0:E, 0:E])
            ins.then_inc(c_T, 1)
            pe.wait_ge(c_silu, 1)
            pe.wait_ge(c_cp, 2)
            pe.wait_ge(l_wm, 16)
            for a in range(2):
                T_.matmul(psM[:, 64 + B * a:64 + B * a + B], wm[:, D * a:D * a + D], sT[:, :], start=True, stop=True)
            for g in range(2):
                T_.transpose(psM[:, 76 + g:77 + g], ownr[:, g, :], ident[0:1, 0:1])
            T_.matmul(psM[:, 72:76], e8[:, :], lnT[:, :], start=True, stop=True).then_inc(c_mod, 1)
            pe.wait_ge(n_xn, 1)
            for t in range(4):
                ins = T_.transpose(psN[:, P * t:P * t + P], xn[:, t, :], ident[:, :])
            ins.then_inc(n_T, 1)
            pe.wait_ge(c_own, 1)
            pe.wait_ge(n_a, 1)
            for t in range(4):
                ins = T_.transpose(psM[:, P * t:P * t + P], xn[:, 4 + t, :], ident[:, :])
            ins.then_inc(n_T, 1)

            def project_qk(dst, t0):
                for t in range(2):
                    at = (t0 + t) * P
                    ins = T_.matmul(dst[:, 256 * t:256 * t + 256], hT[:, at:at + P],
                                    wqk[:, :, :].rearrange("p a d -> p (a d)"), start=True, stop=True)
                return ins

            def project_v(dst, t0):
                for t in range(4):
                    at = (t0 + t) * P
                    ins = T_.matmul(dst[:, P * t:P * t + P], hT[:, at:at + P], wv[:, :], start=True, stop=True)
                return ins

            def transpose_qk(dst, half, a):
                for t in range(4):
                    ins = T_.transpose(dst[:, P * t:P * t + P], qkn[:, 4 * half + t, a, :], ident[:, :])
                return ins

            pe.wait_ge(w_qk, 1)
            for half in range(2):
                pe.wait_ge(n_h, half + 1)
                for n in range(2 * half, 2 * half + 2):
                    project_qk(psS[n // 2][:, n % 2, :], 2 * n).then_inc(q_mm, 1)
            for half in range(2):
                project_v(psO[half], 4 * half).then_inc(v_mm, 1)
            for n in range(4):
                half, a = divmod(n, 2)
                pe.wait_ge(q_n, 2 * half + 2)
                if n < 2:
                    pe.wait_ge(n_h, n + 1)
                else:
                    pe.wait_ge(q_f, n - 1)
                transpose_qk((psN, psM)[n % 2], half, a).then_inc(q_T, 1)

            for half in range(2):
                pe.wait_ge(n_a, half + 2)
                pe.wait_ge(v_cp, half + 1)
                for t in range(4):
                    ins = T_.transpose(psO[half][:, P * t:P * t + P], xn[:, 4 * half + t, :], ident[:, :])
                ins.then_inc(n_T, 1)
            pe.wait_ge(q_n, 4)
            for half in range(2):
                pe.wait_ge(n_h, 3 + half)
                for n in range(2 * half, 2 * half + 2):
                    project_qk(psS[n // 2][:, n % 2, :], 2 * n).then_inc(q_mm, 1)
            for half in range(2):
                pe.wait_ge(q_f, 3 + half)
                project_v((psN, psM)[half], 4 * half).then_inc(v_mm, 1)

            def modulation_rows(b):
                pe.wait_ge(c_sb, 1)
                T_.matmul(psO[b][:, :], silub[:, b, :], wm[:, 2 * D:6 * D], start=True, stop=True).then_inc(c_mr, 1)

            def transpose_parts(n):
                half, a = divmod(n, 2)
                pe.wait_ge(q_n, 4 + 2 * half + 2)
                if n == 0:
                    pe.wait_ge(v_cp, 4)
                else:
                    pe.wait_ge(b_v, n)
                transpose_qk(psM, half, a).then_inc(b_pe, 1)

            def maxima(b):
                pe.wait_ge(st_d[b], 16 * STACK_DMAS[b])
                pe.wait_ge(st_g, 16 * ON_POOL)
                if b == 0:
                    pe.wait_ge(q_n, 8)
                else:
                    pe.wait_ge(s_exp, FIRST[NP])
                for h in range(H):
                    p, g = divmod(h, 2)
                    pe.wait_ge(m_z, b * NP + p + 1)
                    for i in range(NT):
                        m = (b * H + h) * NT + i
                        if m >= 2:
                            pe.wait_ge(m_rd, m - 1)
                        w = (i + 1) * P
                        for hf in range((w + 511) // 512):
                            n = min(512, w - 512 * hf)
                            ins = T_.matmul(psS[m % 2][:, hf, 0:n],
                                            qz[:, p % 2, g, i * P:i * P + P],
                                            stack[b][:, 1, p, 512 * hf:512 * hf + n],
                                            start=True, stop=True)
                        ins.then_inc(m_mm, 1)
                for half in range(2):
                    pe.wait_ge(m_rd, (b + 1) * NT * H)
                    if b == 0:
                        pe.wait_ge(v_cp, 4)
                    else:
                        pe.wait_ge(o_n, NP - 1)
                        pe.wait_ge(b_v, 4)
                    for t in range(4):
                        ins = T_.transpose((psN, psM)[half][0:H, P * t:P * t + P], mx[:, 4 * half + t, :],
                                           ident[:, :])
                    ins.then_inc(m_T, 1)
                pe.wait_ge(m_cp, 2 * b + 2)
                pe.wait_ge(m_d[b], 16 * 3)

            def scores(n):
                r, u = WHERE[n]
                b, p, units = ROUNDS[r][:3]
                if n < 2:
                    pe.wait_ge(q_n, 6 + 2 * n)
                else:
                    pe.wait_ge(s_exp, n - 1)
                if n == 0:
                    pe.wait_ge(q_z0, 1)
                elif n == 1:
                    pe.wait_ge(q_z, 1)
                elif u == 0:
                    pe.wait_ge(q_z, r + 1)
                at = 0
                for j, i0, cnt in units[u]:
                    w = cnt * P
                    for g in range(2):
                        ins = T_.matmul(psS[n % 2][:, g, at:at + w], stack[b][:, 1, p, j * P:j * P + P],
                                        qz[:, r % 2, g, i0 * P:i0 * P + w], start=True, stop=True)
                    at += w
                ins.then_inc(s_mm, 1)

            def values(n):
                r, u = WHERE[n]
                b, p, units = ROUNDS[r][:3]
                pe.wait_ge(s_exp, n + 1)
                if masked(n):
                    pe.wait_ge(s_mask, sum(masked(m) for m in range(n)) + 1)
                if u == 0:
                    pe.wait_ge(v_cp, 2 * (b + 1))
                    pe.wait_ge(c_mc, min(r + 1, B))
                    pe.wait_ge(v_set, 1)
                    if r >= 2:
                        pe.wait_ge(o_cp, r - 1)
                at = 0
                for j, i0, cnt in units[u]:
                    for par in range(2):
                        tiles = [i for i in range(i0, i0 + cnt) if i % 2 == par]
                        if not tiles:
                            continue
                        k = len(tiles)
                        for g in range(2):
                            r0 = 64 * par + 32 * g
                            src = pbuf[n % NPB][:, g, :].rearrange("p (t c) -> p t c", c=P)
                            a0 = at // P + tiles[0] - i0
                            dst = psO[r % 2][r0:r0 + HD + 1, tiles[0] // 2 * P:(tiles[0] // 2 + k) * P]
                            ins = T_.matmul(dst, v9[:, b * NT + j, 2 * p + g, :],
                                            src[:, a0:a0 + 2 * k - 1:2, :],
                                            start=(u == 0), stop=(u == len(units) - 1), skip_group_check=True,
                                            tile_position=(0, r0))
                    at += cnt * P
                ins.then_inc(s_pv, 1)

            def to_tokens(n):
                pe.wait_ge(o_cp, n + 1)
                if n == 0:
                    pe.wait_ge(v_cp, 4)
                else:
                    pe.wait_ge(o_n, n)
                t0, count = ROUNDS[n][3:]
                for i in range(t0 // 2, (t0 + count) // 2):
                    ins = T_.transpose(psN[:, P * i:P * i + P], ots[:, n % 2, P * i:P * i + P], ident[:, :])
                ins.then_inc(o_mm, 1)

            def router(stage, step):
                if step == "modulate":
                    return
                b = stage // 2
                h0 = 4 * (stage % 2)
                index = ORDER.index((stage, step))
                if index:
                    pe.wait_ge(t_v, index)
                else:
                    pe.wait_ge(b_v, 4)
                if step in ("turn", "turn_h"):
                    src = attn if step == "turn" else h2
                    if step == "turn":
                        pe.wait_ge(o_n, (NP, NP, 2 * NP, 3 * NP)[stage])
                    for t in range(4):
                        ins = T_.transpose(psM[:, P * t:P * t + P], src[:, h0 + t, 0:D], ident[:, :])
                if step == "project":
                    pe.wait_ge(c_modc, 2)
                    for t in range(4):
                        at = (h0 + t) * P
                        ins = T_.matmul(psM[:, P * t:P * t + P], attnT[:, at:at + P], wog[:, b, :],
                                        start=True, stop=True)
                if step == "logits":
                    for t in range(4):
                        at = (h0 + t) * P
                        ins = T_.matmul(psM[:, E * t:E * t + E], h2T[:, at:at + P], rw[:, :],
                                        start=True, stop=True)
                if step == "counts":
                    pe.wait_ge(v_set, 2)
                    counts = psM[:, 64:64 + 4 * E]
                    T_.matmul(counts, upper[:, :], oh[:, stage, :, :].rearrange("p t e -> p (t e)"),
                              start=True, stop=False, skip_group_check=True)
                    if stage:
                        pe.wait_ge(t_s, stage)
                        T_.matmul(counts, onesb[:, :],
                                  ohsum[:, stage - 1:stage, :].to_broadcast([P, 4, E]),
                                  start=False, stop=False, skip_group_check=True)
                    for t in range(3):
                        ins = T_.matmul(psM[:, 64 + E * (t + 1):64 + 4 * E], onesb[:, :],
                                        oh[:, stage, t:t + 1, :].to_broadcast([P, 3 - t, E]), start=False,
                                        stop=t == 2, skip_group_check=True)
                    if stage == STAGES - 2:
                        pe.wait_ge(t_s, stage + 1)
                        ins = T_.matmul(psM[:, 128:128 + E], onesb[:, :], ohsum[:, stage, :], start=True, stop=True)
                ins.then_inc(t_pe, 1)

            pe.wait_ge(c_fl, 1)
            general = read_flag(pe, flag, "general")
            with pe.If(general != 0):
                maxima(0)
            transpose_parts(0)
            def rows_T(n):
                half, e = UNITS[n]
                pe.wait_ge(x_i, n // GROUP + 1)
                if n < 2:
                    pe.wait_ge(o_cp, NR)
                else:
                    pe.wait_ge(x_cp, n - 1)
                T_.transpose(psO[n % 2][:, 0:P], xe[:, half, e, 0:D], ident[:, :]).then_inc(x_T, 1)

            def hidden(n):
                e = UNITS[n][1]
                pe.wait_ge(x_cp, n + 1)
                if n == 0:
                    pe.wait_ge(l_ffn, 32)
                if n < 2:
                    pe.wait_ge(s_exp, TOTAL)
                else:
                    pe.wait_ge(h_a, n - 1)
                    pe.wait_ge(h_v, n - 1)
                w1v = w1s[:, e, :].rearrange("d (p c) -> d c p", c=FC)
                for f in range(FC):
                    ins = T_.matmul(psS[n % 2][:, f // 2, P * (f % 2):P * (f % 2) + P], w1v[:, f, :], xeT[:, n % 2, :],
                                    start=True, stop=True)
                    if f % 2:
                        ins.then_inc(h_mm, 1)

            for b in range(B):
                modulation_rows(b)
                scores(b)
            for n in range(-1, TOTAL):
                if n + 3 == FIRST[NP]:
                    with pe.If(general != 0):
                        maxima(1)
                if 2 <= n + 3 < TOTAL:
                    scores(n + 3)
                if n < 0:
                    continue
                r, u = WHERE[n]
                values(n)
                kind, k = SIDE.get((r, u), (None, 0))
                if kind == "parts":
                    if k:
                        transpose_parts(k)
                elif kind not in (None, "rows", "bias"):
                    router(kind, k)
                if r and u == TOKEN_UNIT[NU[r]]:
                    to_tokens(r - 1)
            to_tokens(NR - 1)
            pe.wait_ge(c_f2, 1)
            wait_for_last = read_flag(pe, late, "late")
            for step in STEPS:
                router(STAGES - 1, step)
                if step == "turn_h":
                    with pe.If(wait_for_last == 0):
                        rows_T(0)
                        rows_T(1)
                if step == "logits":
                    with pe.If(wait_for_last == 0):
                        hidden(0)
            with pe.If(wait_for_last != 0):
                rows_T(0)
                rows_T(1)
                hidden(0)

            def outputs(n):
                e = UNITS[n][1]
                pe.wait_ge(h_a, n + 1)
                pe.wait_ge(h_v, n + 1)
                if n < 2:
                    pe.wait_ge(t_v, len(ORDER))
                else:
                    pe.wait_ge(y_cp, n - 1)
                for f in range(FC):
                    ins = T_.matmul((psN, psM)[n % 2][:, 0:D], hid[:, n % 2, f, :], w2s[:, e, D * f:D * f + D],
                                    start=(f == 0), stop=(f == FC - 1))
                ins.then_inc(y_mm, 1)

            for n in range(len(UNITS)):
                if 2 <= n + 1 < len(UNITS):
                    rows_T(n + 1)
                if n:
                    hidden(n)
                if n >= 1:
                    outputs(n - 1)
            outputs(len(UNITS) - 1)


_INS = ["L0_attn_x", "L0_attn_Wk", "L0_attn_Wq", "L0_attn_Wv", "L0_attn_Wo", "L0_attn_bo", "L0_attn_kln_w",
        "L0_attn_kln_b", "L0_attn_qln_w", "L0_attn_qln_b", "L0_ffn_router_w", "L0_ffn_w1", "L0_ffn_b1",
        "L0_ffn_w2", "L0_ffn_b2", "L0_c", "L0_wmod"]


def kernel(**inputs):
    import numpy as _np
    import concourse.bacc as _bacc
    from concourse import mybir as _mybir
    from concourse.bass_utils import run_bass_kernel_spmd as _run

    nc = _bacc.Bacc("TRN2", target_bir_lowering=False, num_devices=1)
    arrays, args = {}, []
    for name in _INS:
        a = _np.ascontiguousarray(inputs[name])
        arrays[f"in_{name}"] = a
        args.append(nc.dram_tensor(f"in_{name}", a.shape, _mybir.dt.from_np(a.dtype), kind="ExternalInput").ap())
    shape = inputs["L0_attn_x"].shape
    args.append(nc.dram_tensor("out_0", shape, _mybir.dt.float32, kind="ExternalOutput").ap())
    adaln_block(nc, *args)
    r = _run(nc, [arrays], core_ids=[0])
    return r.results[0]["out_0"]
```
